# Optimizing a Trainium2 kernel written in Bass

```python
import numpy as np
import jax
import jax.numpy as jnp

def _softmax(x, axis=-1):
    return jax.nn.softmax(x, axis=axis)

def _gelu(x):
    return jax.nn.gelu(x, approximate=True)

def _silu(x):
    return jax.nn.silu(x)

def _sigmoid(x):
    return jax.nn.sigmoid(x)

def _layernorm(x, axis=-1, eps=1e-05):
    m = jnp.mean(x, axis=axis, keepdims=True)
    v = jnp.var(x, axis=axis, keepdims=True)
    return (x - m) / jnp.sqrt(v + eps)

def _scatter_add(tgt, idx, src, axis=0):
    return tgt.at[idx].add(src)

def _segment_sum(src, seg, n):
    return jax.ops.segment_sum(src, seg, n)
kernel_name = 'mk_lm_tower_d2_tok_ids768_r4_7b7ae4'

def setup_inputs(seed: int=0):
    np.random.seed(seed)
    _w = jnp.asarray

    def _rec_inputs():
        import jax
        import jax.numpy as jnp
        _rk = jax.random.key(seed)
        x = jax.random.randint(jax.random.fold_in(_rk, 1), (8, 256), 0, 31993, jnp.int32)
        return x
    x = _rec_inputs()

    def _L0_tok_setup():
        import jax, jax.numpy as jnp
        import numpy as np
        NUM_HEADS = 12
        EPS = 1e-05

        def _layer_norm(x, gamma, beta):
            mean = jnp.mean(x, axis=-1, keepdims=True)
            std = jnp.sqrt(jnp.mean((x - mean) ** 2, axis=-1, keepdims=True))
            return (x - mean) / (std + EPS) * gamma + beta

        def _pos_encoding(L, D, dtype):
            pos = jnp.arange(L, dtype=dtype)[:, None]
            i = jnp.arange(D, dtype=dtype)[None, :]
            ang = pos / jnp.power(jnp.asarray(10000.0, dtype), 2.0 * i / D)
            even = jnp.arange(D) % 2 == 0
            return jnp.where(even[None, :], jnp.cos(ang), jnp.sin(ang))
        key = jax.random.key(seed)
        ks = jax.random.split(key, 12)
        B, L, D, F, V = (4, 512, 192, 768, 8000)
        s = lambda d: 1.0 / np.sqrt(d)
        return {'tokens': jax.random.randint(ks[0], (B, L), 0, V, dtype=jnp.int32), 'emb': jax.random.normal(ks[1], (V, D), jnp.float32) * 0.02, 'wq': jax.random.normal(ks[2], (D, D), jnp.float32) * s(D), 'bq': jnp.zeros((D,), jnp.float32), 'wk': jax.random.normal(ks[3], (D, D), jnp.float32) * s(D), 'bk': jnp.zeros((D,), jnp.float32), 'wv': jax.random.normal(ks[4], (D, D), jnp.float32) * s(D), 'bv': jnp.zeros((D,), jnp.float32), 'wo': jax.random.normal(ks[5], (D, D), jnp.float32) * s(D), 'bo': jnp.zeros((D,), jnp.float32), 'w1': jax.random.normal(ks[6], (D, F), jnp.float32) * s(D), 'b1': jnp.zeros((F,), jnp.float32), 'w2': jax.random.normal(ks[7], (F, D), jnp.float32) * s(F), 'b2': jnp.zeros((D,), jnp.float32), 'gamma1': jnp.ones((D,), jnp.float32), 'beta1': jnp.zeros((D,), jnp.float32), 'gamma2': jnp.ones((D,), jnp.float32), 'beta2': jnp.zeros((D,), jnp.float32)}
    _L0_tok_all = _L0_tok_setup()
    _L0_tok_in = {k: v for k, v in _L0_tok_all.items() if k in ('emb', 'wq', 'bq', 'wk', 'bk', 'wv', 'bv', 'wo', 'bo', 'w1', 'b1', 'w2', 'b2', 'gamma1', 'beta1', 'gamma2', 'beta2')}
    del _L0_tok_all

    def _L0_attn_setup():
        import jax, jax.numpy as jnp
        import numpy as np
        L = 8
        D = 192
        H = 12
        DH = D // H
        MLP_D = 4 * D
        B, S = (32, 577)
        EPS = 1e-05

        def _layernorm(x, g, b):
            m = jnp.mean(x, axis=-1, keepdims=True)
            v = jnp.mean((x - m) ** 2, axis=-1, keepdims=True)
            return (x - m) * jax.lax.rsqrt(v + EPS) * g + b

        def _msa(xn, qw, qb, kw, kb, vw, vb):
            xh = xn.reshape(xn.shape[0], xn.shape[1], H, DH)
            q = jnp.einsum('bshd,hed->bshe', xh, qw) + qb
            k = jnp.einsum('bshd,hed->bshe', xh, kw) + kb
            v = jnp.einsum('bshd,hed->bshe', xh, vw) + vb
            scores = jnp.einsum('bshe,bthe->bhst', q, k) / jnp.sqrt(jnp.float32(DH))
            attn = jax.nn.softmax(scores, axis=-1)
            out = jnp.einsum('bhst,bthd->bshd', attn, v)
            return out.reshape(xn.shape[0], xn.shape[1], D)
        key = jax.random.key(seed)
        ks = jax.random.split(key, 16)
        s = 0.02
        inp = {'x': jax.random.normal(ks[0], (B, S, D), dtype=jnp.float32), 'ln1_g': jnp.ones((L, D), jnp.float32), 'ln1_b': jnp.zeros((L, D), jnp.float32), 'qw': jax.random.normal(ks[1], (L, H, DH, DH), jnp.float32) * s, 'qb': jax.random.normal(ks[2], (L, H, DH), jnp.float32) * s, 'kw': jax.random.normal(ks[3], (L, H, DH, DH), jnp.float32) * s, 'kb': jax.random.normal(ks[4], (L, H, DH), jnp.float32) * s, 'vw': jax.random.normal(ks[5], (L, H, DH, DH), jnp.float32) * s, 'vb': jax.random.normal(ks[6], (L, H, DH), jnp.float32) * s, 'ln2_g': jnp.ones((L, D), jnp.float32), 'ln2_b': jnp.zeros((L, D), jnp.float32), 'w1': jax.random.normal(ks[7], (L, MLP_D, D), jnp.float32) * s, 'b1': jnp.zeros((L, MLP_D), jnp.float32), 'w2': jax.random.normal(ks[8], (L, D, MLP_D), jnp.float32) * s, 'b2': jnp.zeros((L, D), jnp.float32)}
        return inp
    _L0_attn_all = _L0_attn_setup()
    _L0_attn_in = {k: v for k, v in _L0_attn_all.items() if k in ('ln1_g', 'ln1_b', 'qw', 'qb', 'kw', 'kb', 'vw', 'vb', 'ln2_g', 'ln2_b', 'w1', 'b1', 'w2', 'b2')}
    del _L0_attn_all

    def _L0_ffn_setup():
        import jax, jax.numpy as jnp
        import numpy as np
        N_HEAD = 8 * 0 + 12
        TOP_K = 2
        GELU_C = 0.7978845608028654

        def _gelu(x):
            return 0.5 * x * (1.0 + jnp.tanh(GELU_C * (x + 0.044715 * x * x * x)))

        def _layernorm_global(x, w, b, eps=1e-12):
            m = jnp.mean(x)
            v = jnp.var(x, ddof=1)
            return (x - m) / jnp.sqrt(v + eps) * w + b

        def _attn(x, W1_w, W1_b, W2_w, W2_b):
            B, N, D = x.shape
            h = N_HEAD
            dh = D // h
            qkv = x @ W1_w + W1_b
            Q, K, V = jnp.split(qkv, 3, axis=-1)
            q = Q.reshape(B, N, h, dh).transpose(0, 2, 3, 1)
            k = K.reshape(B, N, h, dh).transpose(0, 2, 1, 3)
            v = V.reshape(B, N, h, dh).transpose(0, 2, 3, 1)
            w = jax.nn.softmax(q @ k / jnp.sqrt(jnp.asarray(N, x.dtype)), axis=-1)
            out = (w @ v).reshape(B, N, h * dh)
            return out @ W2_w + W2_b

        def _moe(x, r_w, r_b, fc_w, fc_b, proj_w, proj_b):
            B, N, D = x.shape
            scores = x @ r_w + r_b
            gate = jax.nn.softmax(jnp.mean(scores, axis=1), axis=-1)
            vals, idx = jax.lax.top_k(gate, TOP_K)
            hmid = _gelu(jnp.einsum('bnd,edf->benf', x, fc_w) + fc_b[None, :, None, :])
            outs = jnp.einsum('benf,efd->bend', hmid, proj_w) + proj_b[None, :, None, :]
            k_outs = jnp.take_along_axis(outs, idx[:, :, None, None], axis=1)
            return jnp.sum(vals[:, :, None, None] * k_outs, axis=1)
        key = jax.random.key(seed)
        ks = jax.random.split(key, 16)
        B, N, D, E = (2, 512, 192, 8)
        H = 4 * D
        s = 0.02
        return {'x': jax.random.normal(ks[0], (B, N, D), jnp.float32), 'W1_w': jax.random.normal(ks[1], (D, 3 * D), jnp.float32) * s, 'W1_b': jnp.zeros((3 * D,), jnp.float32), 'W2_w': jax.random.normal(ks[2], (D, D), jnp.float32) * s, 'W2_b': jnp.zeros((D,), jnp.float32), 'r_w': jax.random.normal(ks[3], (D, E), jnp.float32) * s, 'r_b': jnp.zeros((E,), jnp.float32), 'fc_w': jax.random.normal(ks[4], (E, D, H), jnp.float32) * s, 'fc_b': jnp.zeros((E, H), jnp.float32), 'proj_w': jax.random.normal(ks[5], (E, H, D), jnp.float32) * s, 'proj_b': jnp.zeros((E, D), jnp.float32), 'ln1_w': jnp.ones((D,), jnp.float32), 'ln1_b': jnp.zeros((D,), jnp.float32), 'ln2_w': jnp.ones((D,), jnp.float32), 'ln2_b': jnp.zeros((D,), jnp.float32)}
    _L0_ffn_all = _L0_ffn_setup()
    _L0_ffn_in = {k: v for k, v in _L0_ffn_all.items() if k in ('W1_w', 'W1_b', 'W2_w', 'W2_b', 'r_w', 'r_b', 'fc_w', 'fc_b', 'proj_w', 'proj_b', 'ln1_w', 'ln1_b', 'ln2_w', 'ln2_b')}
    del _L0_ffn_all

    def _L1_attn_setup():
        import jax, jax.numpy as jnp
        import numpy as np
        NUM_HEADS = 12
        HEAD_DIM = 64
        key = jax.random.key(seed)
        k1, k2, k3, k4 = jax.random.split(key, 4)
        B, N, D = (16, 256, 192)
        x = jax.random.normal(k1, (B, N, D), dtype=jnp.float32)
        W_qkv = jax.random.normal(k2, (D, 3 * D), dtype=jnp.float32) * D ** (-0.5)
        W_proj = jax.random.normal(k3, (D, D), dtype=jnp.float32) * D ** (-0.5)
        b_proj = jax.random.normal(k4, (D,), dtype=jnp.float32) * 0.01
        return {'x': x, 'W_qkv': W_qkv, 'W_proj': W_proj, 'b_proj': b_proj}
    _L1_attn_all = _L1_attn_setup()
    _L1_attn_in = {k: v for k, v in _L1_attn_all.items() if k in ('W_qkv', 'W_proj', 'b_proj')}
    del _L1_attn_all

    def _L1_ffn_setup():
        import jax, jax.numpy as jnp
        import numpy as np
        B, T, E = (2, 256, 192)
        H = 768
        N_EXP = 4
        key = jax.random.key(seed)
        ks = jax.random.split(key, 8)
        s_e = 1.0 / np.sqrt(E)
        s_h = 1.0 / np.sqrt(H)
        return {'x': jax.random.normal(ks[0], (B, T, E), dtype=jnp.float32), 'Wg': jax.random.uniform(ks[1], (E, N_EXP), minval=-s_e, maxval=s_e, dtype=jnp.float32), 'bg': jax.random.uniform(ks[2], (N_EXP,), minval=-s_e, maxval=s_e, dtype=jnp.float32), 'W1': jax.random.uniform(ks[3], (N_EXP, E, H), minval=-s_e, maxval=s_e, dtype=jnp.float32), 'b1': jax.random.uniform(ks[4], (N_EXP, H), minval=-s_e, maxval=s_e, dtype=jnp.float32), 'W2': jax.random.uniform(ks[5], (N_EXP, H, E), minval=-s_h, maxval=s_h, dtype=jnp.float32), 'b2': jax.random.uniform(ks[6], (N_EXP, E), minval=-s_h, maxval=s_h, dtype=jnp.float32)}
    _L1_ffn_all = _L1_ffn_setup()
    _L1_ffn_in = {k: v for k, v in _L1_ffn_all.items() if k in ('Wg', 'bg', 'W1', 'b1', 'W2', 'b2')}
    del _L1_ffn_all
    return {'x': x, 'L0_tok_emb': _L0_tok_in['emb'], 'L0_tok_wq': _L0_tok_in['wq'], 'L0_tok_bq': _L0_tok_in['bq'], 'L0_tok_wk': _L0_tok_in['wk'], 'L0_tok_bk': _L0_tok_in['bk'], 'L0_tok_wv': _L0_tok_in['wv'], 'L0_tok_bv': _L0_tok_in['bv'], 'L0_tok_wo': _L0_tok_in['wo'], 'L0_tok_bo': _L0_tok_in['bo'], 'L0_tok_w1': _L0_tok_in['w1'], 'L0_tok_b1': _L0_tok_in['b1'], 'L0_tok_w2': _L0_tok_in['w2'], 'L0_tok_b2': _L0_tok_in['b2'], 'L0_tok_gamma1': _L0_tok_in['gamma1'], 'L0_tok_beta1': _L0_tok_in['beta1'], 'L0_tok_gamma2': _L0_tok_in['gamma2'], 'L0_tok_beta2': _L0_tok_in['beta2'], 'L0_attn_ln1_g': _L0_attn_in['ln1_g'], 'L0_attn_ln1_b': _L0_attn_in['ln1_b'], 'L0_attn_qw': _L0_attn_in['qw'], 'L0_attn_qb': _L0_attn_in['qb'], 'L0_attn_kw': _L0_attn_in['kw'], 'L0_attn_kb': _L0_attn_in['kb'], 'L0_attn_vw': _L0_attn_in['vw'], 'L0_attn_vb': _L0_attn_in['vb'], 'L0_attn_ln2_g': _L0_attn_in['ln2_g'], 'L0_attn_ln2_b': _L0_attn_in['ln2_b'], 'L0_attn_w1': _L0_attn_in['w1'], 'L0_attn_b1': _L0_attn_in['b1'], 'L0_attn_w2': _L0_attn_in['w2'], 'L0_attn_b2': _L0_attn_in['b2'], 'L0_ffn_W1_w': _L0_ffn_in['W1_w'], 'L0_ffn_W1_b': _L0_ffn_in['W1_b'], 'L0_ffn_W2_w': _L0_ffn_in['W2_w'], 'L0_ffn_W2_b': _L0_ffn_in['W2_b'], 'L0_ffn_r_w': _L0_ffn_in['r_w'], 'L0_ffn_r_b': _L0_ffn_in['r_b'], 'L0_ffn_fc_w': _L0_ffn_in['fc_w'], 'L0_ffn_fc_b': _L0_ffn_in['fc_b'], 'L0_ffn_proj_w': _L0_ffn_in['proj_w'], 'L0_ffn_proj_b': _L0_ffn_in['proj_b'], 'L0_ffn_ln1_w': _L0_ffn_in['ln1_w'], 'L0_ffn_ln1_b': _L0_ffn_in['ln1_b'], 'L0_ffn_ln2_w': _L0_ffn_in['ln2_w'], 'L0_ffn_ln2_b': _L0_ffn_in['ln2_b'], 'L1_attn_W_qkv': _L1_attn_in['W_qkv'], 'L1_attn_W_proj': _L1_attn_in['W_proj'], 'L1_attn_b_proj': _L1_attn_in['b_proj'], 'L1_ffn_Wg': _L1_ffn_in['Wg'], 'L1_ffn_bg': _L1_ffn_in['bg'], 'L1_ffn_W1': _L1_ffn_in['W1'], 'L1_ffn_b1': _L1_ffn_in['b1'], 'L1_ffn_W2': _L1_ffn_in['W2'], 'L1_ffn_b2': _L1_ffn_in['b2']}

def reference(x, L0_tok_emb, L0_tok_wq, L0_tok_bq, L0_tok_wk, L0_tok_bk, L0_tok_wv, L0_tok_bv, L0_tok_wo, L0_tok_bo, L0_tok_w1, L0_tok_b1, L0_tok_w2, L0_tok_b2, L0_tok_gamma1, L0_tok_beta1, L0_tok_gamma2, L0_tok_beta2, L0_attn_ln1_g, L0_attn_ln1_b, L0_attn_qw, L0_attn_qb, L0_attn_kw, L0_attn_kb, L0_attn_vw, L0_attn_vb, L0_attn_ln2_g, L0_attn_ln2_b, L0_attn_w1, L0_attn_b1, L0_attn_w2, L0_attn_b2, L0_ffn_W1_w, L0_ffn_W1_b, L0_ffn_W2_w, L0_ffn_W2_b, L0_ffn_r_w, L0_ffn_r_b, L0_ffn_fc_w, L0_ffn_fc_b, L0_ffn_proj_w, L0_ffn_proj_b, L0_ffn_ln1_w, L0_ffn_ln1_b, L0_ffn_ln2_w, L0_ffn_ln2_b, L1_attn_W_qkv, L1_attn_W_proj, L1_attn_b_proj, L1_ffn_Wg, L1_ffn_bg, L1_ffn_W1, L1_ffn_b1, L1_ffn_W2, L1_ffn_b2):
    import jax
    import jax.numpy as jnp

    def _L0_tok_ref(tokens, emb, wq, bq, wk, bk, wv, bv, wo, bo, w1, b1, w2, b2, gamma1, beta1, gamma2, beta2):
        import jax, jax.numpy as jnp
        import numpy as np
        NUM_HEADS = 12
        EPS = 1e-05

        def _layer_norm(x, gamma, beta):
            mean = jnp.mean(x, axis=-1, keepdims=True)
            std = jnp.sqrt(jnp.mean((x - mean) ** 2, axis=-1, keepdims=True))
            return (x - mean) / (std + EPS) * gamma + beta

        def _pos_encoding(L, D, dtype):
            pos = jnp.arange(L, dtype=dtype)[:, None]
            i = jnp.arange(D, dtype=dtype)[None, :]
            ang = pos / jnp.power(jnp.asarray(10000.0, dtype), 2.0 * i / D)
            even = jnp.arange(D) % 2 == 0
            return jnp.where(even[None, :], jnp.cos(ang), jnp.sin(ang))
        B, L = tokens.shape
        D = emb.shape[1]
        H = NUM_HEADS
        dh = D // H
        x = emb[tokens] + _pos_encoding(L, D, emb.dtype)

        def heads(t):
            return t.reshape(B, L, H, dh).transpose(0, 2, 1, 3)
        q = heads(x @ wq + bq)
        k = heads(x @ wk + bk)
        v = heads(x @ wv + bv)
        scores = jnp.einsum('bhqd,bhkd->bhqk', q, k) / jnp.sqrt(jnp.asarray(dh, x.dtype))
        weights = jax.nn.softmax(scores, axis=-1)
        attn = jnp.einsum('bhqk,bhkd->bhqd', weights, v)
        attn = attn.transpose(0, 2, 1, 3).reshape(B, L, D)
        attn_out = attn @ wo + bo
        h1 = _layer_norm(x + attn_out, gamma1, beta1)
        ff = jax.nn.relu(h1 @ w1 + b1) @ w2 + b2
        return _layer_norm(h1 + ff, gamma2, beta2)

    def _L0_attn_ref(x, ln1_g, ln1_b, qw, qb, kw, kb, vw, vb, ln2_g, ln2_b, w1, b1, w2, b2):
        import jax, jax.numpy as jnp
        import numpy as np
        L = 8
        D = 192
        H = 12
        DH = D // H
        MLP_D = 4 * D
        B, S = (32, 577)
        EPS = 1e-05

        def _layernorm(x, g, b):
            m = jnp.mean(x, axis=-1, keepdims=True)
            v = jnp.mean((x - m) ** 2, axis=-1, keepdims=True)
            return (x - m) * jax.lax.rsqrt(v + EPS) * g + b

        def _msa(xn, qw, qb, kw, kb, vw, vb):
            xh = xn.reshape(xn.shape[0], xn.shape[1], H, DH)
            q = jnp.einsum('bshd,hed->bshe', xh, qw) + qb
            k = jnp.einsum('bshd,hed->bshe', xh, kw) + kb
            v = jnp.einsum('bshd,hed->bshe', xh, vw) + vb
            scores = jnp.einsum('bshe,bthe->bhst', q, k) / jnp.sqrt(jnp.float32(DH))
            attn = jax.nn.softmax(scores, axis=-1)
            out = jnp.einsum('bhst,bthd->bshd', attn, v)
            return out.reshape(xn.shape[0], xn.shape[1], D)
        out = x
        for l in range(L):
            out = out + _msa(_layernorm(out, ln1_g[l], ln1_b[l]), qw[l], qb[l], kw[l], kb[l], vw[l], vb[l])
            h = _layernorm(out, ln2_g[l], ln2_b[l])
            h = jax.nn.gelu(h @ w1[l].T + b1[l], approximate=False)
            out = out + (h @ w2[l].T + b2[l])
        return out

    def _L0_ffn_ref(x, W1_w, W1_b, W2_w, W2_b, r_w, r_b, fc_w, fc_b, proj_w, proj_b, ln1_w, ln1_b, ln2_w, ln2_b):
        import jax, jax.numpy as jnp
        import numpy as np
        N_HEAD = 8 * 0 + 12
        TOP_K = 2
        GELU_C = 0.7978845608028654

        def _gelu(x):
            return 0.5 * x * (1.0 + jnp.tanh(GELU_C * (x + 0.044715 * x * x * x)))

        def _layernorm_global(x, w, b, eps=1e-12):
            m = jnp.mean(x)
            v = jnp.var(x, ddof=1)
            return (x - m) / jnp.sqrt(v + eps) * w + b

        def _attn(x, W1_w, W1_b, W2_w, W2_b):
            B, N, D = x.shape
            h = N_HEAD
            dh = D // h
            qkv = x @ W1_w + W1_b
            Q, K, V = jnp.split(qkv, 3, axis=-1)
            q = Q.reshape(B, N, h, dh).transpose(0, 2, 3, 1)
            k = K.reshape(B, N, h, dh).transpose(0, 2, 1, 3)
            v = V.reshape(B, N, h, dh).transpose(0, 2, 3, 1)
            w = jax.nn.softmax(q @ k / jnp.sqrt(jnp.asarray(N, x.dtype)), axis=-1)
            out = (w @ v).reshape(B, N, h * dh)
            return out @ W2_w + W2_b

        def _moe(x, r_w, r_b, fc_w, fc_b, proj_w, proj_b):
            B, N, D = x.shape
            scores = x @ r_w + r_b
            gate = jax.nn.softmax(jnp.mean(scores, axis=1), axis=-1)
            vals, idx = jax.lax.top_k(gate, TOP_K)
            hmid = _gelu(jnp.einsum('bnd,edf->benf', x, fc_w) + fc_b[None, :, None, :])
            outs = jnp.einsum('benf,efd->bend', hmid, proj_w) + proj_b[None, :, None, :]
            k_outs = jnp.take_along_axis(outs, idx[:, :, None, None], axis=1)
            return jnp.sum(vals[:, :, None, None] * k_outs, axis=1)
        a = _attn(x, W1_w, W1_b, W2_w, W2_b)
        x = _layernorm_global(a + x, ln1_w, ln1_b)
        m = _moe(x, r_w, r_b, fc_w, fc_b, proj_w, proj_b)
        x = _layernorm_global(m + x, ln2_w, ln2_b)
        return x

    def _L1_attn_ref(x, W_qkv, W_proj, b_proj):
        import jax, jax.numpy as jnp
        import numpy as np
        NUM_HEADS = 12
        HEAD_DIM = 64
        B, N, D = x.shape
        H, hd = (NUM_HEADS, D // NUM_HEADS)
        scale = hd ** (-0.5)
        qkv = x @ W_qkv
        q, k, v = jnp.split(qkv, 3, axis=-1)
        q = q.reshape(B, N, H, hd).transpose(0, 2, 1, 3)
        k = k.reshape(B, N, H, hd).transpose(0, 2, 1, 3)
        v = v.reshape(B, N, H, hd).transpose(0, 2, 1, 3)
        attn = jnp.einsum('bhqd,bhkd->bhqk', q * scale, k)
        attn = jax.nn.softmax(attn, axis=-1)
        out = jnp.einsum('bhqk,bhkd->bhqd', attn, v)
        out = out.transpose(0, 2, 1, 3).reshape(B, N, D)
        return out @ W_proj + b_proj

    def _L1_ffn_ref(x, Wg, bg, W1, b1, W2, b2):
        import jax, jax.numpy as jnp
        import numpy as np
        B, T, E = (2, 256, 192)
        H = 768
        N_EXP = 4
        gate_logits = jnp.einsum('bte,en->btn', x, Wg) + bg
        top = jnp.argmax(gate_logits, axis=-1)
        h = jax.nn.gelu(jnp.einsum('bte,neh->nbth', x, W1) + b1[:, None, None, :], approximate=False)
        y = jnp.einsum('nbth,nhe->nbte', h, W2) + b2[:, None, None, :]
        onehot = jax.nn.one_hot(top, N_EXP, dtype=x.dtype)
        out = jnp.einsum('nbte,btn->bte', y, onehot)
        return out
    h = _L0_tok_ref(x, L0_tok_emb, L0_tok_wq, L0_tok_bq, L0_tok_wk, L0_tok_bk, L0_tok_wv, L0_tok_bv, L0_tok_wo, L0_tok_bo, L0_tok_w1, L0_tok_b1, L0_tok_w2, L0_tok_b2, L0_tok_gamma1, L0_tok_beta1, L0_tok_gamma2, L0_tok_beta2)
    h = h + _L0_attn_ref(_layernorm(h, axis=-1), L0_attn_ln1_g, L0_attn_ln1_b, L0_attn_qw, L0_attn_qb, L0_attn_kw, L0_attn_kb, L0_attn_vw, L0_attn_vb, L0_attn_ln2_g, L0_attn_ln2_b, L0_attn_w1, L0_attn_b1, L0_attn_w2, L0_attn_b2)
    h = h + _L0_ffn_ref(_layernorm(h, axis=-1), L0_ffn_W1_w, L0_ffn_W1_b, L0_ffn_W2_w, L0_ffn_W2_b, L0_ffn_r_w, L0_ffn_r_b, L0_ffn_fc_w, L0_ffn_fc_b, L0_ffn_proj_w, L0_ffn_proj_b, L0_ffn_ln1_w, L0_ffn_ln1_b, L0_ffn_ln2_w, L0_ffn_ln2_b)
    h = h + _L1_attn_ref(_layernorm(h, axis=-1), L1_attn_W_qkv, L1_attn_W_proj, L1_attn_b_proj)
    h = h + _L1_ffn_ref(_layernorm(h, axis=-1), L1_ffn_Wg, L1_ffn_bg, L1_ffn_W1, L1_ffn_b1, L1_ffn_W2, L1_ffn_b2)
    return h

_drawn_inputs = setup_inputs


def setup_inputs(seed=0):
    import zlib

    import numpy as np

    out = dict(_drawn_inputs(seed))
    spreads = {'L0_tok_bq': (0.0, 0.8),
     'L0_tok_bk': (0.0, 2.0),
     'L0_tok_bv': (0.0, 0.1),
     'L0_tok_bo': (0.0, 0.1),
     'L0_tok_b1': (0.0, 0.1),
     'L0_tok_b2': (0.0, 0.1),
     'L0_tok_gamma1': (1.0, 0.2),
     'L0_tok_beta1': (0.0, 0.1),
     'L0_tok_gamma2': (1.0, 0.2),
     'L0_tok_beta2': (0.0, 0.1),
     'L0_attn_ln1_g': (1.0, 0.6),
     'L0_attn_ln1_b': (0.0, 0.695),
     'L0_attn_ln2_g': (1.0, 0.6),
     'L0_attn_ln2_b': (0.0, 0.633),
     'L0_attn_b1': (0.0, 0.1),
     'L0_attn_b2': (0.0, 0.1),
     'L0_ffn_W1_b': (0.0, 0.8),
     'L0_ffn_W2_b': (0.0, 0.593),
     'L0_ffn_r_b': (0.0, 0.8),
     'L0_ffn_fc_b': (0.0, 0.8),
     'L0_ffn_proj_b': (0.0, 0.8),
     'L0_ffn_ln1_w': (1.0, 0.2),
     'L0_ffn_ln1_b': (0.0, 0.1),
     'L0_ffn_ln2_w': (1.0, 0.2),
     'L0_ffn_ln2_b': (0.0, 0.1)}
    factors = {'L0_tok_wq': 2.691,
     'L0_attn_qw': 8.0,
     'L0_attn_qb': 186.24,
     'L0_attn_kw': 8.0,
     'L0_attn_kb': 200.0,
     'L0_ffn_W1_w': 5.88,
     'L0_ffn_W2_w': 4.829,
     'L0_ffn_r_w': 5.76,
     'L0_ffn_fc_w': 8.0,
     'L0_ffn_proj_w': 8.0,
     'L1_attn_b_proj': 8.0,
     'L1_ffn_bg': 8.0,
     'L1_ffn_b1': 8.0,
     'L1_ffn_b2': 8.0}
    for name, (base, spread) in spreads.items():
        noise = np.random.default_rng([zlib.crc32(name.encode()), seed]).standard_normal(out[name].shape)
        drawn = base * np.exp(spread * noise) if base else spread * noise
        out[name] = jnp.asarray(drawn.astype(out[name].dtype))
    for name, factor in factors.items():
        out[name] = (out[name] * factor).astype(out[name].dtype)
    return out
```

```python
from contextlib import ExitStack, contextmanager

import numpy as np

import concourse.bass as bass
from concourse import mybir

F32 = mybir.dt.float32
F32R = mybir.dt.float32r
I32 = mybir.dt.int32
ALU = mybir.AluOpType
ACT = mybir.ActivationFunctionType
AX = mybir.AxisListType

B, S, D, F = 8, 256, 192, 768
H, DH = 12, 16
P = 128
T = S // P
D2 = D - P
KC = ((0, P), (1, D2))
FC = F // P
PAIRS = H // 2
GROUPS = H // 4
SLOT = 64
MROW = 48
VIT_LAYERS = 8
MOE_E, TOP_K, L1_E = 8, 2, 4
VOCAB = 8000
SCALE = 0.25


@contextmanager
def semaphores(nc, stage):
    taken = []

    def sem(name):
        taken.append(nc.alloc_semaphore(f"{stage}_{name}"))
        return taken[-1]

    yield sem
    nc.clear_and_free_semaphores(taken)
    nc.all_engine_barrier()


class chain:

    def __init__(self, eng, sem, it, per):
        self.eng, self.sem, self.it, self.per, self.done = eng, sem, it, per, 0

    def __call__(self, ins):
        self.done += 1
        ins.then_inc(self.sem, 1)
        self.eng.wait_ge(self.sem, self.it * self.per + self.done)

    def finished(self):
        assert self.done == self.per, (self.done, self.per)


RSQRT_SEED = float(0x5F3759DF)
NEWTON = 3


def norm_stats(nc, dve, link, x, st, mv, rt, var_ready, root_ready, turn, post=False):
    v = nc.vector
    v.bn_stats(st[:, 0, :], x[:, 0, :])
    link(v.bn_stats(st[:, 1, :], x[:, 1, :]))
    v.memset(rt[:, 5, :], 0.0)
    v.bn_aggr(mv[:, 0, :], st[:, 0, :])
    link(v.bn_aggr(mv[:, 1, :], st[:, 1, :]))
    if post:
        link(v.tensor_scalar(rt[:, 0, :], mv[:, :, 1], 1e-30, None, ALU.max))
    else:
        link(v.tensor_scalar(rt[:, 0, :], mv[:, :, 1], 1e-5, None, ALU.add))
    bits = rt[:, 1, :].bitcast(I32)
    v.tensor_scalar(rt[:, 4, :], rt[:, 0, :], -0.5, None, ALU.mult)
    link(v.tensor_scalar(bits, rt[:, 0, :].bitcast(I32), 1, None, ALU.logical_shift_right))
    v.tensor_scalar(bits, bits, -1.0, RSQRT_SEED, ALU.mult, ALU.add).then_inc(var_ready, 1)
    dve.wait_ge(root_ready, turn)


def root(nc, pool, link, rt, half3, eps, var_ready, root_ready, turn, post):
    g = nc.gpsimd
    pool.wait_ge(var_ready, turn)
    vv, y, s, out, vh = rt[:, 0, :], rt[:, 1, :], rt[:, 2, :], rt[:, 3, :], rt[:, 4, :]
    for n in range(NEWTON):
        link(g.tensor_tensor(s, y, y, ALU.mult))
        link(g.tensor_tensor(s, s, vh, ALU.mult))
        link(g.tensor_tensor(s, s, half3, ALU.add))
        if n < NEWTON - 1 or post:
            link(g.tensor_tensor(y, y, s, ALU.mult))
        else:
            g.tensor_tensor(out, y, s, ALU.mult).then_inc(root_ready, 1)
    if post:
        link(g.tensor_tensor(s, y, vv, ALU.mult))
        g.tensor_tensor(out, s, eps, ALU.add).then_inc(root_ready, 1)


def root_steps(post):
    return 4 * NEWTON + 1 if post else 4 * NEWTON - 1


def post_norm(nc, link, x, out, xh, mv, rt, gb, n):
    v = nc.vector
    link(v.reciprocal(rt[:, 3, :], rt[:, 3, :]))
    for t in range(T):
        last = v.tensor_scalar(xh[:, t, :], x[:, t, :], mv[:, t, 0:1], rt[:, 3, t:t + 1], ALU.subtract, ALU.mult)
    link(last)
    for t in range(T):
        last = v.tensor_tensor(xh[:, t, :], xh[:, t, :], gb[:, n, :], ALU.mult)
    link(last)
    for t in range(T):
        last = v.tensor_tensor(out(t), xh[:, t, :], gb[:, n + 1, :], ALU.add)
    return last


def attention_stage(nc, name, kind, h, x, wd, cst):
    vit, tok, l1 = kind == "vit", kind == "tok", kind == "l1"
    layers = VIT_LAYERS if vit else 1
    mlp = not l1
    proj = not vit
    res = h if l1 else x
    with ExitStack() as ctx:
        def sb(n, shape, dt=F32):
            return ctx.enter_context(nc.sbuf_tensor(f"{name}_{n}", shape, dt))

        sem = ctx.enter_context(semaphores(nc, name))

        ps = ctx.enter_context(nc.psum_tensor(f"{name}_ps", [P, 8, 512], F32))
        wq = sb("wq", [P, 2, PAIRS, P])
        wk = sb("wk", [P, 2, PAIRS, P])
        wv = sb("wv", [P, 2, D])
        bqk = sb("bqk", [P, 2, PAIRS])
        bqk_lo = sb("bqk_lo", [P, 2, PAIRS])
        bv = sb("bv", [P, D])
        ln1 = sb("ln1", [P, 2, 2])
        ln2 = sb("ln2", [P, 2, 2])
        wo = sb("wo", [P, 2, D])
        bo = sb("bo", [P, D])
        w1 = sb("w1", [P, 2, F])
        b1 = sb("b1", [P, FC])
        w2 = sb("w2", [P, FC, D])
        b2 = sb("b2", [P, D])
        gb = sb("gb", [P, 4, D])
        st, mv, rt = sb("st", [P, T, 6]), sb("mv", [P, T, 2]), sb("rt", [P, 6, T])
        xh = sb("xh", [P, T, D])
        xn = sb("xn", [P, 2, S])
        hm = sb("hm", [P, 2, S], F32R)
        qk = sb("qk", [P, 3, 2, S], F32R)
        q2 = sb("q2", [P, 2, S], F32R)
        mx = sb("mx", [P, 2, 2, T])
        mb = sb("mb", [P, 2, T, P], F32R)
        va = sb("va", [P, T, H, 32])
        pt = sb("pt", [P, 8, T, S])
        ot = sb("ot", [P, GROUPS, S])
        rcp = sb("rcp", [P, T, H])
        att = sb("att", [P, T, D])
        at = sb("at", [P, 2, S])
        r1 = sb("r1", [P, T, D])
        hid = sb("hid", [P, FC, S])

        w_ready, wm_ready = sem("attn_weights_ready"), sem("mlp_weights_ready")
        zeroed, cleared = sem("zeroed"), sem("cleared")
        dch, pch = sem("vector_chain"), sem("pool_chain")
        var_ready, root_ready = sem("var_ready"), sem("root_ready")
        xhat_ready, xT_done, xn_ready = sem("xhat_ready"), sem("xT_done"), sem("xn_ready")
        v_done, v_ready = sem("v_done"), sem("v_ready")
        proj_done, hm_ready, qk_ready = sem("proj_done"), sem("hm_ready"), sem("qk_ready")
        s_done, mx_done, m_ready = sem("s_done"), sem("mx_done"), sem("m_ready")
        mt_done, q2_ready, st_done = sem("mt_done"), sem("q2_ready"), sem("st_done")
        p_ready, pv_done, oT_ready = sem("p_ready"), sem("pv_done"), sem("oT_ready")
        ot_done, att_ready = sem("ot_done"), sem("att_ready")
        aT_done, aT_ready, op_done = sem("aT_done"), sem("aT_ready"), sem("op_done")
        xhat2_ready, xT2_done, xn2_ready = sem("xhat2_ready"), sem("xT2_done"), sem("xn2_ready")
        h_done, h_ready, y_done, x_ready = sem("h_done"), sem("h_ready"), sem("y_done"), sem("x_ready")

        ident, identr, maskqk = cst["ident"], cst["identr"], cst["maskqk"]

        def batches(eng):
            if layers > 1:
                with eng.Fori(0, layers) as l:
                    with eng.Fori(0, B) as b:
                        yield l * B + b, l, b
            else:
                with eng.Fori(0, B) as b:
                    yield b, 0, b

        def tile_of(t_, b):
            return lambda t: t_[:, bass.ds(b * T + t, 1), :].rearrange("p a d -> p (a d)")

        CH = {"tok": 25, "vit": 18, "l1": 13}[kind]
        NORMS = 1 if l1 else 2
        attn_loads = [(wq, wd["wq"]), (wk, wd["wk"]), (wv, wd["wv"]), (bqk, wd["bqk"]), (bqk_lo, wd["bqk_lo"]),
                      (bv, wd["bv"])]
        if vit:
            attn_loads += [(ln1, wd["ln1"]), (ln2, wd["ln2"])]
        if proj:
            attn_loads += [(wo, wd["wo"]), (bo, wd["bo"])]
        if tok:
            attn_loads += [(gb, wd["gb"])]
        mlp_loads = [(w1, wd["w1"]), (b1, wd["b1"]), (w2, wd["w2"]), (b2, wd["b2"])] if mlp else []
        NA, NM = 16 * len(attn_loads), 16 * len(mlp_loads)

        block = ctx.enter_context(nc.Block())

        def load(sp, dst, src, l, s):
            part = src[bass.ds(l, 1)].rearrange("a p n -> (a p) n")
            flat = dst[:, :] if len(dst.shape) == 2 else (
                dst[:, :, :].rearrange("p a b -> p (a b)") if len(dst.shape) == 3
                else dst[:, :, :, :].rearrange("p a b c -> p (a b c)"))
            sp.dma_start(flat[:, 0:src.shape[2]], part).then_inc(s, 16)

        @block.sync
        def _(sp):
            for dst, src in attn_loads:
                load(sp, dst, src, 0, w_ready)
            for dst, src in mlp_loads:
                load(sp, dst, src, 0, wm_ready)
            if layers > 1:
                with sp.Fori(1, layers) as l:
                    sp.wait_ge(xn2_ready, l * B * 2)
                    for dst, src in attn_loads:
                        load(sp, dst, src, l, w_ready)
                    sp.wait_ge(x_ready, l * B)
                    for dst, src in mlp_loads:
                        load(sp, dst, src, l, wm_ready)
            sp.wait_ge(w_ready, NA * layers)
            if mlp:
                sp.wait_ge(wm_ready, NM * layers)

        def layer_weights(eng, s, n, l):
            eng.wait_ge(s, (l + 1) * n)

        @block.gpsimd
        def _(pool):
            half3, eps = cst["newton"][:, 0, :], cst["newton"][:, 1, :]
            for it, l, b in batches(pool):
                link = chain(pool, pch, it, NORMS * root_steps(tok))
                for n in range(NORMS):
                    root(nc, pool, link, rt, half3, eps, var_ready, root_ready, it * NORMS + n + 1, tok)
                link.finished()

        @block.tensor
        def _(pe):
            mm, tr = nc.tensor.matmul, nc.tensor.transpose

            def transposes(src, bank):
                for t in range(T):
                    for c, k in KC:
                        last = tr(ps[0:k, bank, c * S + t * P:c * S + (t + 1) * P],
                                  src[:, t, c * P:c * P + k], ident[:, :])
                return last

            def project(p, it):
                for i, w in enumerate((wq, wk)):
                    out = ps[:, 2, i * S:(i + 1) * S]
                    if vit:
                        r, c = SLOT * ((p // 2) % 2), p // 4
                        last = mm(out, w[r:r + SLOT, 0, p, :], xn[r:r + SLOT, c, :], start=True, stop=True)
                    else:
                        for c, k in KC:
                            last = mm(out, w[0:k, c, p, :], xn[0:k, c, :], start=(c == 0), stop=(c == 1))
                last.then_inc(proj_done, 1)

            def scores(p, it):
                for a in range(2):
                    if p > 0:
                        pe.wait_ge(mx_done, it * H + 2 * (p - 1) + a + 1)
                    r = SLOT * a
                    for t in range(T):
                        last = mm(ps[:, a, t * S:(t + 1) * S], qk[r:r + SLOT, p % 3, 0, t * P:(t + 1) * P],
                                  qk[r:r + SLOT, p % 3, 1, :], start=True, stop=True)
                    last.then_inc(s_done, 1)

            def max_rows(p, it):
                pe.wait_ge(m_ready, it * PAIRS + p + 1)
                if p > 0:
                    pe.wait_ge(q2_ready, it * PAIRS + p)
                for t in range(T):
                    last = mm(ps[:, 5, t * P:(t + 1) * P], mb[:, p % 2, t, :], identr[:, :],
                              start=True, stop=True)
                last.then_inc(mt_done, 1)

            def scores_t(p, it):
                pe.wait_ge(q2_ready, it * PAIRS + p + 1)
                for a in range(2):
                    hd, r = 2 * p + a, SLOT * a
                    if hd >= 2:
                        pe.wait_ge(p_ready, it * H + hd - 1)
                    for t in range(T):
                        last = mm(ps[:, 3 + hd % 2, t * S:(t + 1) * S],
                                  qk[r:r + SLOT, p % 3, 1, t * P:(t + 1) * P], q2[r:r + SLOT, p % 2, :],
                                  start=True, stop=True)
                    last.then_inc(st_done, 1)

            def weighted(g, it):
                pe.wait_ge(p_ready, it * H + 4 * g + 4)
                if g > 0:
                    pe.wait_ge(oT_ready, it * GROUPS + g)
                for t in range(T):
                    for j in range(4):
                        hd = 4 * g + j
                        last = mm(ps[32 * j:32 * j + 32, 6, 0:S], va[:, t, hd, :], pt[:, hd % 8, t, :],
                                  start=(t == 0), stop=(t == T - 1), skip_group_check=True)
                last.then_inc(pv_done, 1)

            pe.wait_ge(cleared, 1)
            for it, l, b in batches(pe):
                pe.wait_ge(xhat_ready, it + 1)
                transposes(xh, 7).then_inc(xT_done, 1)
                layer_weights(pe, w_ready, NA, l)
                pe.wait_ge(xn_ready, 2 * it + 2)
                for t in range(T):
                    for c, k in KC:
                        out = ps[:, 7, t * D:(t + 1) * D]
                        lhs = xn[0:k, c, t * P:(t + 1) * P]
                        if vit:
                            last = mm(out[:, c * P:c * P + k], lhs, wv[0:k, c, c * P:c * P + k],
                                      start=True, stop=True)
                        else:
                            last = mm(out, lhs, wv[0:k, c, :], start=(c == 0), stop=(c == 1))
                last.then_inc(v_done, 1)
                project(0, it)
                for p in range(PAIRS + 2):
                    if p < PAIRS:
                        pe.wait_ge(qk_ready, it * PAIRS + p + 1)
                        scores(p, it)
                        if p + 1 < PAIRS:
                            project(p + 1, it)
                    if 1 <= p <= PAIRS:
                        max_rows(p - 1, it)
                        scores_t(p - 1, it)
                    if p == 2:
                        pe.wait_ge(v_ready, it + 1)
                    if p >= 3 and p % 2 == 1:
                        weighted((p - 3) // 2, it)
                pe.wait_ge(oT_ready, (it + 1) * GROUPS)
                for t in range(T):
                    for g in range(GROUPS):
                        last = tr(ps[:, 7 if t == 0 else 2, g * P:(g + 1) * P], ot[:, g, t * P:(t + 1) * P],
                                  ident[:, :])
                last.then_inc(ot_done, 1)
                if proj:
                    pe.wait_ge(att_ready, it + 1)
                    transposes(att, 0).then_inc(aT_done, 1)
                    pe.wait_ge(aT_ready, 2 * it + 2)
                    for t in range(T):
                        for c, k in KC:
                            last = mm(ps[:, 1, t * D:(t + 1) * D], at[0:k, c, t * P:(t + 1) * P], wo[0:k, c, :],
                                      start=(c == 0), stop=(c == 1))
                    last.then_inc(op_done, 1)
                if mlp:
                    pe.wait_ge(xhat2_ready, it + 1)
                    transposes(r1 if tok else xh, 7).then_inc(xT2_done, 1)
                    layer_weights(pe, wm_ready, NM, l)
                    pe.wait_ge(xn2_ready, 2 * it + 2)
                    for m in range(FC):
                        if m >= 2:
                            pe.wait_ge(h_ready, it * FC + m - 1)
                        for c, k in KC:
                            last = mm(ps[:, m % 2, 0:S], w1[0:k, c, m * P:(m + 1) * P], xn[0:k, c, :],
                                      start=(c == 0), stop=(c == 1))
                        last.then_inc(h_done, 1)
                    for t in range(T):
                        for m in range(FC):
                            if t == 0:
                                pe.wait_ge(h_ready, it * FC + m + 1)
                            last = mm(ps[:, 3 + t, 0:D], hid[:, m, t * P:(t + 1) * P], w2[:, m, :],
                                      start=(m == 0), stop=(m == FC - 1))
                    last.then_inc(y_done, 1)

        @block.scalar
        def _(act):
            go = nc.scalar.activation
            for it, l, b in batches(act):
                layer_weights(act, w_ready, NA, l)
                act.wait_ge(xT_done, it + 1)
                for c, k in KC:
                    src, dst = ps[0:k, 7, c * S:(c + 1) * S], xn[0:k, c, :]
                    if vit:
                        go(dst, src, ACT.Identity, bias=ln1[0:k, c, 1:2], scale=ln1[0:k, c, 0:1]).then_inc(xn_ready, 1)
                    else:
                        go(dst, src, ACT.Copy).then_inc(xn_ready, 1)

                def parts(p):
                    act.wait_ge(proj_done, it * PAIRS + p + 1)
                    for i in range(2):
                        last = go(hm[:, i, :], ps[:, 2, i * S:(i + 1) * S], ACT.Identity,
                                  bias=bqk_lo[:, i, p:p + 1], scale=maskqk[:, i:i + 1])
                    last.then_inc(hm_ready, 1)

                def exps(hd):
                    act.wait_ge(st_done, it * H + hd + 1)
                    if hd >= 8:
                        act.wait_ge(pv_done, it * GROUPS + (hd - 8) // 4 + 1)
                    go(pt[:, hd % 8, :, :].rearrange("p t s -> p (t s)"), ps[:, 3 + hd % 2, :], ACT.Exp,
                       scale=SCALE).then_inc(p_ready, 1)

                def out_t(g):
                    act.wait_ge(pv_done, it * GROUPS + g + 1)
                    go(ot[:, g, :], ps[:, 6, 0:S], ACT.Copy).then_inc(oT_ready, 1)

                parts(0)
                for p in range(PAIRS + 2):
                    if p + 1 < PAIRS:
                        parts(p + 1)
                    if 1 <= p <= PAIRS:
                        exps(2 * p - 2)
                        exps(2 * p - 1)
                    if p >= 3 and p % 2 == 1:
                        out_t((p - 3) // 2)
                if proj:
                    act.wait_ge(aT_done, it + 1)
                    for c, k in KC:
                        go(at[0:k, c, :], ps[0:k, 0, c * S:(c + 1) * S], ACT.Copy).then_inc(aT_ready, 1)
                if mlp:
                    act.wait_ge(xT2_done, it + 1)
                    for c, k in KC:
                        src, dst = ps[0:k, 7, c * S:(c + 1) * S], xn[0:k, c, :]
                        if vit:
                            go(dst, src, ACT.Identity, bias=ln2[0:k, c, 1:2],
                               scale=ln2[0:k, c, 0:1]).then_inc(xn2_ready, 1)
                        else:
                            go(dst, src, ACT.Copy).then_inc(xn2_ready, 1)
                    layer_weights(act, wm_ready, NM, l)
                    for m in range(FC):
                        act.wait_ge(h_done, it * FC + m + 1)
                        go(hid[:, m, :], ps[:, m % 2, 0:S], ACT.Relu if tok else ACT.Gelu,
                           bias=b1[:, m:m + 1]).then_inc(h_ready, 1)

        @block.vector
        def _(dve):
            v = nc.vector
            v.memset(mb[:, :, :, :].rearrange("p a t c -> p (a t c)").bitcast(F32), 0.0)
            v.memset(va[:, :, :, :].rearrange("p t h c -> p (t h c)"), 0.0).then_inc(zeroed, 1)
            dve.wait_ge(zeroed, 1)
            v.memset(va[:, :, :, DH:DH + 1].rearrange("p t h c -> p (t h) c"), 1.0).then_inc(cleared, 1)
            for it, l, b in batches(dve):
                link = chain(dve, dch, it, CH)
                layer_weights(dve, w_ready, NA, l)
                xt = res[:, bass.ds(b * T, T), :]
                if tok:
                    v.tensor_scalar(xh[:, :, :], xt, 1.0, None, ALU.mult).then_inc(xhat_ready, 1)
                else:
                    link(v.tensor_scalar(r1[:, :, :], xt, 1.0, None, ALU.mult))
                    norm_stats(nc, dve, link, r1, st, mv, rt, var_ready, root_ready, it * NORMS + 1, tok)
                    for t in range(T):
                        last = v.tensor_scalar(xh[:, t, :], r1[:, t, :], mv[:, t, 0:1], rt[:, 3, t:t + 1],
                                               ALU.subtract, ALU.mult)
                    last.then_inc(xhat_ready, 1)
                dve.wait_ge(v_done, it + 1)
                for t in range(T):
                    last = v.tensor_tensor(va[:, t, :, 0:DH],
                                           ps[:, 7, t * D:(t + 1) * D].rearrange("p (h d) -> p h d", h=H),
                                           bv[:, :].rearrange("p (h d) -> p h d", h=H), ALU.add)
                last.then_inc(v_ready, 1)

                def stack(p):
                    dve.wait_ge(hm_ready, it * PAIRS + p + 1)
                    if p >= 3:
                        dve.wait_ge(st_done, it * H + 2 * (p - 2))
                    for i in range(2):
                        last = v.scalar_tensor_tensor(out=qk[:, p % 3, i, :], in0=ps[:, 2, i * S:(i + 1) * S],
                                                      scalar=bqk[:, i, p:p + 1], in1=hm[:, i, :],
                                                      op0=ALU.add, op1=ALU.subtract)
                    last.then_inc(qk_ready, 1)

                def maxima(p):
                    for a in range(2):
                        dve.wait_ge(s_done, it * H + 2 * p + a + 1)
                        v.tensor_reduce(mx[:, p % 2, a, :], ps[:, a, :].rearrange("p (t s) -> p t s", t=T),
                                        AX.X, ALU.max).then_inc(mx_done, 1)
                    dve.wait_ge(mx_done, it * H + 2 * p + 2)
                    if p >= 2:
                        dve.wait_ge(mt_done, it * PAIRS + p - 1)
                    m = mx[:, p % 2, :, :].rearrange("p a t -> p t a")
                    hi = mb[:, p % 2, :, :].rearrange("p t (a c) -> p t a c", a=2)[:, :, :, MROW]
                    lo = mb[:, p % 2, :, :].rearrange("p t (a c) -> p t a c", a=2)[:, :, :, MROW + 1]
                    link(v.tensor_scalar(hi, m, -1.0, None, ALU.mult))
                    v.scalar_tensor_tensor(out=lo, in0=m, scalar=-1.0, in1=hi, op0=ALU.mult,
                                           op1=ALU.subtract).then_inc(m_ready, 1)

                def with_max(p):
                    dve.wait_ge(mt_done, it * PAIRS + p + 1)
                    if p >= 2:
                        dve.wait_ge(st_done, it * H + 2 * (p - 1))
                    v.tensor_tensor(q2[:, p % 2, :], ps[:, 5, 0:S], qk[:, p % 3, 0, :],
                                    ALU.add).then_inc(q2_ready, 1)

                stack(0)
                for p in range(PAIRS + 1):
                    if p + 1 < PAIRS:
                        stack(p + 1)
                    if p < PAIRS:
                        maxima(p)
                    if p >= 1:
                        with_max(p - 1)
                dve.wait_ge(ot_done, it + 1)
                for t in range(T):
                    o = ps[:, 7 if t == 0 else 2, 0:GROUPS * P].rearrange("p (h c) -> p h c", h=H)
                    last = v.reciprocal(rcp[:, t, :], o[:, :, DH])
                link(last)
                for t in range(T):
                    o = ps[:, 7 if t == 0 else 2, 0:GROUPS * P].rearrange("p (h c) -> p h c", h=H)
                    last = v.tensor_tensor(att[:, t, :].rearrange("p (h d) -> p h d", h=H), o[:, :, 0:DH],
                                           rcp[:, t, :].unsqueeze(2).to_broadcast([P, H, DH]), ALU.mult)
                last.then_inc(att_ready, 1)
                if proj:
                    dve.wait_ge(op_done, it + 1)
                    for t in range(T):
                        last = v.tensor_tensor(r1[:, t, :], ps[:, 1, t * D:(t + 1) * D], bo[:, :], ALU.add)
                    link(last)
                    add = r1
                else:
                    dve.wait_ge(att_ready, it + 1)
                    add = att
                if l1:
                    v.tensor_tensor(xt, xt, add[:, :, :], ALU.add).then_inc(x_ready, 1)
                else:
                    link(v.tensor_tensor(r1[:, :, :], xt, add[:, :, :], ALU.add))
                if tok:
                    norm_stats(nc, dve, link, r1, st, mv, rt, var_ready, root_ready, it * NORMS + 1, tok)
                    post_norm(nc, link, r1, lambda t: r1[:, t, :], xh, mv, rt, gb, 0).then_inc(xhat2_ready, 1)
                if vit:
                    norm_stats(nc, dve, link, r1, st, mv, rt, var_ready, root_ready, it * NORMS + 2, tok)
                    for t in range(T):
                        last = v.tensor_scalar(xh[:, t, :], r1[:, t, :], mv[:, t, 0:1], rt[:, 3, t:t + 1],
                                               ALU.subtract, ALU.mult)
                    last.then_inc(xhat2_ready, 1)
                if mlp:
                    dve.wait_ge(y_done, it + 1)
                    layer_weights(dve, wm_ready, NM, l)
                    for t in range(T):
                        last = v.tensor_tensor(att[:, t, :], ps[:, 3 + t, 0:D], b2[:, :], ALU.add)
                    link(last)
                    if tok:
                        link(v.tensor_tensor(r1[:, :, :], r1[:, :, :], att[:, :, :], ALU.add))
                        norm_stats(nc, dve, link, r1, st, mv, rt, var_ready, root_ready, it * NORMS + 2, tok)
                        post_norm(nc, link, r1, tile_of(h, b), xh, mv, rt, gb, 2).then_inc(x_ready, 1)
                    else:
                        v.tensor_tensor(xt, r1[:, :, :], att[:, :, :], ALU.add).then_inc(x_ready, 1)
                dve.wait_ge(x_ready, it + 1)
                link.finished()


def embedding_stage(nc, x, a, cst):
    with ExitStack() as ctx:
        sem = ctx.enter_context(semaphores(nc, "emb"))
        tok_i = ctx.enter_context(nc.sbuf_tensor("emb_tok_i", [P, B * T], I32))
        tok_f = ctx.enter_context(nc.sbuf_tensor("emb_tok_f", [P, B * T], F32))
        neg = ctx.enter_context(nc.sbuf_tensor("emb_neg", [P, B * T], F32))
        idx = ctx.enter_context(nc.sbuf_tensor("emb_idx", [P, B * T], mybir.dt.uint32))
        pos = ctx.enter_context(nc.sbuf_tensor("emb_pos", [P, T, D], F32))
        loaded = sem("loaded")
        const_loaded = sem("const_loaded")
        steps = sem("steps")
        gathered = sem("gathered")
        block = ctx.enter_context(nc.Block())

        @block.sync
        def _(sp):
            sp.dma_start(tok_i[:, :], a["tokens"]).then_inc(loaded, 16)
            sp.dma_start(pos[:, :, :].rearrange("p t d -> p (t d)"), a["pos"]).then_inc(const_loaded, 16)
            sp.dma_start(cst["ident"][:, :], a["ident"]).then_inc(const_loaded, 16)
            sp.dma_start(cst["maskqk"][:, :], a["maskqk"]).then_inc(const_loaded, 16)
            sp.dma_start(cst["blockmask"][:, :], a["blockmask"]).then_inc(const_loaded, 16)
            sp.wait_ge(const_loaded, 64)

        @block.vector
        def _(dve):
            v = nc.vector
            dve.wait_ge(loaded, 16)
            v.tensor_copy(tok_f[:, :], tok_i[:, :]).then_inc(steps, 1)
            dve.wait_ge(steps, 1)
            v.tensor_scalar(neg[:, :], tok_f[:, :], 0.0, float(VOCAB), ALU.is_lt, ALU.mult).then_inc(steps, 1)
            dve.wait_ge(steps, 2)
            v.tensor_tensor(tok_f[:, :], tok_f[:, :], neg[:, :], ALU.add).then_inc(steps, 1)
            dve.wait_ge(steps, 3)
            v.tensor_scalar(idx[:, :], tok_f[:, :], 0.0, float(VOCAB - 1), ALU.max, ALU.min).then_inc(steps, 1)
            dve.wait_ge(const_loaded, 64)
            v.tensor_copy(cst["identr"][:, :], cst["ident"][:, :])
            dve.wait_ge(gathered, 16 * T * B)
            for b in range(B):
                v.tensor_tensor(x[:, b * T:(b + 1) * T, :], x[:, b * T:(b + 1) * T, :], pos[:, :, :], ALU.add)

        @block.gpsimd
        def _(pool):
            nc.gpsimd.memset(cst["newton"][:, 0, :], 1.5)
            nc.gpsimd.memset(cst["newton"][:, 1, :], 1e-5)
            pool.wait_ge(steps, 4)
            for n in range(B * T):
                pool.indirect_dma_start(out=x[:, n, :], out_offset=None, in_=a["emb"],
                                        in_offset=bass.IndirectOffsetOnAxis(ap=idx[:, n:n + 1], axis=0)
                                        ).then_inc(gathered, 16)
            pool.wait_ge(gathered, 16 * B * T)


def glue_stage(nc, name, h, x, cst, add):
    with ExitStack() as ctx:
        sem = ctx.enter_context(semaphores(nc, name))
        r = ctx.enter_context(nc.sbuf_tensor(f"{name}_r", [P, T, D], F32))
        st = ctx.enter_context(nc.sbuf_tensor(f"{name}_st", [P, T, 6], F32))
        mv = ctx.enter_context(nc.sbuf_tensor(f"{name}_mv", [P, T, 2], F32))
        rt = ctx.enter_context(nc.sbuf_tensor(f"{name}_rt", [P, 6, T], F32))
        steps = sem("steps")
        pool_steps = sem("pool_steps")
        var_ready = sem("var_ready")
        root_ready = sem("root_ready")
        block = ctx.enter_context(nc.Block())

        @block.gpsimd
        def _(pool):
            half3, eps = cst["newton"][:, 0, :], cst["newton"][:, 1, :]
            with pool.Fori(0, B) as b:
                link = chain(pool, pool_steps, b, root_steps(False))
                root(nc, pool, link, rt, half3, eps, var_ready, root_ready, b + 1, False)
                link.finished()

        @block.vector
        def _(dve):
            v = nc.vector
            with dve.Fori(0, B) as b:
                link = chain(dve, steps, b, 7)
                ht, xt = h[:, bass.ds(b * T, T), :], x[:, bass.ds(b * T, T), :]
                if add:
                    link(v.tensor_tensor(r[:, :, :], ht, xt, ALU.add))
                else:
                    link(v.tensor_scalar(r[:, :, :], ht, 1.0, None, ALU.mult))
                norm_stats(nc, dve, link, r, st, mv, rt, var_ready, root_ready, b + 1)
                for t in range(T):
                    last = v.tensor_scalar(x[:, bass.ds(b * T + t, 1), :].rearrange("p a d -> p (a d)"), r[:, t, :],
                                           mv[:, t, 0:1], rt[:, 3, t:t + 1], ALU.subtract, ALU.mult)
                link(last)
                if add:
                    last = v.tensor_scalar(ht, r[:, :, :], 1.0, None, ALU.mult)
                else:
                    last = v.memset(rt[:, 5, :], 0.0)
                link(last)
                link.finished()


def channel_attention_stage(nc, x, wd, cst, scratch):
    with ExitStack() as ctx:
        def sb(n, shape, dt=F32):
            return ctx.enter_context(nc.sbuf_tensor(f"ca_{n}", shape, dt))

        sem = ctx.enter_context(semaphores(nc, "ca"))

        ps = ctx.enter_context(nc.psum_tensor("ca_ps", [P, 8, 512], F32))
        w = sb("w", [P, 2, 3 * D])
        bqk = sb("bqk", [P, 2 * D])
        bv = sb("bv", [P, 2])
        xh, xn = sb("xh", [P, T, D]), sb("xn", [P, 2, S])
        qk = sb("qk", [P, T, 2 * D])
        vt = sb("vt", [P, 2, S])
        gm, ex, wt = sb("gm", [P, 2, P]), sb("ex", [P, 2, P]), sb("wt", [P, 2, P])
        mx, sm = sb("mx", [P, 2]), sb("sm", [P, 2])
        osb = sb("osb", [P, 2, S])
        loaded, dch = sem("weights_loaded"), sem("vector_chain")
        xhat_ready, xT_done, xn_ready = sem("xhat_ready"), sem("xT_done"), sem("xn_ready")
        qk_done, v_done, qk_ready, vt_ready = sem("qk_done"), sem("v_done"), sem("qk_ready"), sem("vt_ready")
        gram_done, logit_ready, e_ready, w_ready = sem("gram_done"), sem("logit_ready"), sem("e_ready"), sem("w_ready")
        wT_done, wT_ready, o_done, o_ready = sem("wT_done"), sem("wT_ready"), sem("o_done"), sem("o_ready")
        stored = sem("stored")
        block = ctx.enter_context(nc.Block())
        ident, bmask = cst["ident"], cst["blockmask"]

        @block.sync
        def _(sp):
            sp.dma_start(w[:, :, :].rearrange("p c n -> p (c n)"), wd["w1"]).then_inc(loaded, 16)
            sp.dma_start(bqk[:, :], wd["bqk"]).then_inc(loaded, 16)
            sp.dma_start(bv[:, :], wd["bv"]).then_inc(loaded, 16)
            with sp.Fori(0, B) as b:
                sp.wait_ge(o_ready, 2 * b + 2)
                for c, k in KC:
                    dst = scratch[bass.ds(b, 1), c * P:c * P + k, :].rearrange("a c n -> (a c) n")
                    sp.dma_start(dst, osb[0:k, c, :]).then_inc(stored, 16)
            sp.wait_ge(stored, 32 * B)
            sp.wait_ge(loaded, 48)

        @block.tensor
        def _(pe):
            mm, tr = nc.tensor.matmul, nc.tensor.transpose
            pe.wait_ge(loaded, 48)
            with pe.Fori(0, B) as b:
                pe.wait_ge(xhat_ready, b + 1)
                for t in range(T):
                    for c, k in KC:
                        last = tr(ps[0:k, 7, c * S + t * P:c * S + (t + 1) * P], xh[:, t, c * P:c * P + k], ident[:, :])
                last.then_inc(xT_done, 1)
                pe.wait_ge(xn_ready, 2 * b + 2)
                for t in range(T):
                    for c, k in KC:
                        last = mm(ps[:, t, 0:2 * D], xn[0:k, c, t * P:(t + 1) * P], w[0:k, c, 0:2 * D],
                                  start=(c == 0), stop=(c == 1))
                last.then_inc(qk_done, 1)
                for o, n in KC:
                    for c, k in KC:
                        last = mm(ps[0:n, 2 + o, 0:S], w[0:k, c, 2 * D + o * P:2 * D + o * P + n], xn[0:k, c, :],
                                  start=(c == 0), stop=(c == 1))
                last.then_inc(v_done, 1)
                pe.wait_ge(qk_ready, b + 1)
                for c, k in KC:
                    for t in range(T):
                        last = mm(ps[0:k, 4 + c, 0:k], qk[:, t, c * P:c * P + k], qk[:, t, D + c * P:D + c * P + k],
                                  start=(t == 0), stop=(t == 1))
                last.then_inc(gram_done, 1)
                pe.wait_ge(w_ready, b + 1)
                for c, k in KC:
                    last = tr(ps[0:k, 6, c * P:c * P + k], ex[0:k, c, 0:k], ident[0:k, 0:k])
                last.then_inc(wT_done, 1)
                pe.wait_ge(wT_ready, 2 * b + 2)
                pe.wait_ge(vt_ready, 2 * b + 2)
                for c, k in KC:
                    last = mm(ps[0:k, c, 0:S], wt[0:k, c, 0:k], vt[0:k, c, :], start=True, stop=True)
                last.then_inc(o_done, 1)

        @block.scalar
        def _(act):
            go = nc.scalar.activation
            act.wait_ge(loaded, 48)
            with act.Fori(0, B) as b:
                act.wait_ge(xT_done, b + 1)
                for c, k in KC:
                    go(xn[0:k, c, :], ps[0:k, 7, c * S:(c + 1) * S], ACT.Copy).then_inc(xn_ready, 1)
                act.wait_ge(v_done, b + 1)
                for c, k in KC:
                    go(vt[0:k, c, :], ps[0:k, 2 + c, 0:S], ACT.Identity, bias=bv[0:k, c:c + 1]).then_inc(vt_ready, 1)
                act.wait_ge(logit_ready, b + 1)
                for c, k in KC:
                    go(ex[0:k, c, 0:k], gm[0:k, c, 0:k], ACT.Exp, bias=mx[0:k, c:c + 1],
                       accum_out=sm[0:k, c:c + 1]).then_inc(e_ready, 1)
                act.wait_ge(wT_done, b + 1)
                for c, k in KC:
                    go(wt[0:k, c, 0:k], ps[0:k, 6, c * P:c * P + k], ACT.Copy).then_inc(wT_ready, 1)
                act.wait_ge(o_done, b + 1)
                for c, k in KC:
                    go(osb[0:k, c, :], ps[0:k, c, 0:S], ACT.Copy).then_inc(o_ready, 1)
                act.wait_ge(stored, 32 * (b + 1))

        @block.vector
        def _(dve):
            v = nc.vector
            dve.wait_ge(loaded, 48)
            with dve.Fori(0, B) as b:
                link = chain(dve, dch, b, 3)
                v.tensor_copy(xh[:, :, :], x[:, bass.ds(b * T, T), :]).then_inc(xhat_ready, 1)
                dve.wait_ge(qk_done, b + 1)
                for t in range(T):
                    last = v.tensor_tensor(qk[:, t, :], ps[:, t, 0:2 * D], bqk[:, :], ALU.add)
                last.then_inc(qk_ready, 1)
                dve.wait_ge(gram_done, b + 1)
                for c, k in KC:
                    last = v.scalar_tensor_tensor(out=gm[0:k, c, 0:k], in0=ps[0:k, 4 + c, 0:k], scalar=1.0 / 16,
                                                  in1=bmask[0:k, 0:k], op0=ALU.mult, op1=ALU.add)
                link(last)
                for c, k in KC:
                    last = v.tensor_reduce(mx[0:k, c:c + 1], gm[0:k, c, 0:k], AX.X, ALU.max)
                link(last)
                for c, k in KC:
                    last = v.tensor_scalar(mx[0:k, c:c + 1], mx[0:k, c:c + 1], -1.0, None, ALU.mult)
                last.then_inc(logit_ready, 1)
                dve.wait_ge(e_ready, 2 * b + 2)
                for c, k in KC:
                    last = v.reciprocal(sm[0:k, c:c + 1], sm[0:k, c:c + 1])
                link(last)
                for c, k in KC:
                    last = v.tensor_scalar(ex[0:k, c, 0:k], ex[0:k, c, 0:k], sm[0:k, c:c + 1], None, ALU.mult)
                last.then_inc(w_ready, 1)
                link.finished()


def channel_projection_stage(nc, x, wd, cst, scratch):
    with ExitStack() as ctx:
        def sb(n, shape, dt=F32):
            return ctx.enter_context(nc.sbuf_tensor(f"cp_{n}", shape, dt))

        sem = ctx.enter_context(semaphores(nc, "cp"))

        ps = ctx.enter_context(nc.psum_tensor("cp_ps", [P, 8, 512], F32))
        a2 = sb("a2", [P, B * T, D])
        w, bo = sb("w", [P, 2, D]), sb("bo", [P, D])
        xh, xn, r = sb("xh", [P, T, D]), sb("xn", [P, 2, S]), sb("r", [P, T, D])
        loaded, dch = sem("loaded"), sem("vector_chain")
        xhat_ready, xT_done, xn_ready = sem("xhat_ready"), sem("xT_done"), sem("xn_ready")
        op_done, x_ready = sem("op_done"), sem("x_ready")
        block = ctx.enter_context(nc.Block())
        ident = cst["ident"]

        @block.sync
        def _(sp):
            sp.dma_start(w[:, :, :].rearrange("p c n -> p (c n)"), wd["w2"]).then_inc(loaded, 16)
            sp.dma_start(bo[:, :], wd["b2"]).then_inc(loaded, 16)
            flat = scratch.rearrange("b c n -> b (c n)").rearrange("b (t p d) -> p (b t) d", t=T, p=P)
            sp.dma_start(a2[:, :, :], flat).then_inc(loaded, 16)
            sp.wait_ge(loaded, 48)

        @block.tensor
        def _(pe):
            mm, tr = nc.tensor.matmul, nc.tensor.transpose
            pe.wait_ge(loaded, 48)
            with pe.Fori(0, B) as b:
                pe.wait_ge(xhat_ready, b + 1)
                for t in range(T):
                    for c, k in KC:
                        last = tr(ps[0:k, 7, c * S + t * P:c * S + (t + 1) * P], xh[:, t, c * P:c * P + k], ident[:, :])
                last.then_inc(xT_done, 1)
                pe.wait_ge(xn_ready, 2 * b + 2)
                for t in range(T):
                    for c, k in KC:
                        last = mm(ps[:, 1, t * D:(t + 1) * D], xn[0:k, c, t * P:(t + 1) * P], w[0:k, c, :],
                                  start=(c == 0), stop=(c == 1))
                last.then_inc(op_done, 1)

        @block.scalar
        def _(act):
            with act.Fori(0, B) as b:
                act.wait_ge(xT_done, b + 1)
                for c, k in KC:
                    nc.scalar.activation(xn[0:k, c, :], ps[0:k, 7, c * S:(c + 1) * S], ACT.Copy).then_inc(xn_ready, 1)

        @block.vector
        def _(dve):
            v = nc.vector
            dve.wait_ge(loaded, 48)
            with dve.Fori(0, B) as b:
                link = chain(dve, dch, b, 1)
                v.tensor_copy(xh[:, :, :], a2[:, bass.ds(b * T, T), :]).then_inc(xhat_ready, 1)
                dve.wait_ge(op_done, b + 1)
                for t in range(T):
                    last = v.tensor_tensor(r[:, t, :], ps[:, 1, t * D:(t + 1) * D], bo[:, :], ALU.add)
                link(last)
                xt = x[:, bass.ds(b * T, T), :]
                v.tensor_tensor(xt, xt, r[:, :, :], ALU.add).then_inc(x_ready, 1)
                dve.wait_ge(x_ready, b + 1)
                link.finished()


def global_norm_stage(nc, name, x, h, wd, cst):
    N = B * S * D
    with ExitStack() as ctx:
        def sb(n, shape, dt=F32):
            return ctx.enter_context(nc.sbuf_tensor(f"{name}_{n}", shape, dt))

        sem = ctx.enter_context(semaphores(nc, name))

        ps = ctx.enter_context(nc.psum_tensor(f"{name}_ps", [P, 2, 512], F32))
        wb = sb("wb", [P, 2, D])
        ones = sb("ones", [P, P])
        part, stat = sb("part", [P, 2]), sb("stat", [P, 2])
        tsum = sb("tsum", [P, B * T])
        sq = sb("sq", [P, B * T * D])
        rt = sb("rt", [P, 6, T])
        loaded, dch, pch = sem("loaded"), sem("vector_chain"), sem("pool_chain")
        ones_ready, sum_ready, sum_all, centred = sem("ones_ready"), sem("sum_ready"), sem("sum_all"), sem("centred")
        sq_ready, sq_all, var_ready, root_ready = sem("sq_ready"), sem("sq_all"), sem("var_ready"), sem("root_ready")
        block = ctx.enter_context(nc.Block())
        flat = x[:, :, :].rearrange("p a d -> p (a d)")

        @block.sync
        def _(sp):
            sp.dma_start(wb[:, :, :].rearrange("p a d -> p (a d)"), wd).then_inc(loaded, 16)
            sp.wait_ge(loaded, 16)

        @block.tensor
        def _(pe):
            pe.wait_ge(ones_ready, 1)
            pe.wait_ge(sum_ready, 1)
            nc.tensor.matmul(ps[:, 0, 0:1], ones[:, :], part[:, 0:1], start=True, stop=True).then_inc(sum_all, 1)
            pe.wait_ge(sq_ready, 1)
            nc.tensor.matmul(ps[:, 1, 0:1], ones[:, :], part[:, 1:2], start=True, stop=True).then_inc(sq_all, 1)

        @block.scalar
        def _(act):
            act.wait_ge(centred, 1)
            nc.scalar.activation(sq[:, :], flat, ACT.Square, accum_out=part[:, 1:2]).then_inc(sq_ready, 1)

        @block.gpsimd
        def _(pool):
            nc.gpsimd.memset(ones[:, :], 1.0).then_inc(ones_ready, 1)
            half3, eps = cst["newton"][:, 0, :], cst["newton"][:, 1, :]
            link = chain(pool, pch, 0, root_steps(False))
            root(nc, pool, link, rt, half3, eps, var_ready, root_ready, 1, False)
            link.finished()

        @block.vector
        def _(dve):
            v = nc.vector
            link = chain(dve, dch, 0, 7 + (1 if h is not None else 0))
            link(v.tensor_reduce(tsum[:, :], x[:, :, :], AX.X, ALU.add))
            v.tensor_reduce(part[:, 0:1], tsum[:, :], AX.X, ALU.add).then_inc(sum_ready, 1)
            dve.wait_ge(sum_all, 1)
            link(v.tensor_scalar(stat[:, 0:1], ps[:, 0, 0:1], 1.0 / N, None, ALU.mult))
            v.tensor_scalar(flat, flat, stat[:, 0:1], None, ALU.subtract).then_inc(centred, 1)
            dve.wait_ge(centred, 1)
            dve.wait_ge(sq_all, 1)
            for t in range(T):
                last = v.tensor_scalar(rt[:, 0, t:t + 1], ps[:, 1, 0:1], 1.0 / (N - 1), 1e-12, ALU.mult, ALU.add)
            link(last)
            bits = rt[:, 1, :].bitcast(I32)
            v.tensor_scalar(rt[:, 4, :], rt[:, 0, :], -0.5, None, ALU.mult)
            link(v.tensor_scalar(bits, rt[:, 0, :].bitcast(I32), 1, None, ALU.logical_shift_right))
            v.tensor_scalar(bits, bits, -1.0, RSQRT_SEED, ALU.mult, ALU.add).then_inc(var_ready, 1)
            dve.wait_ge(root_ready, 1)
            link(v.tensor_scalar(flat, flat, rt[:, 3, 0:1], None, ALU.mult))
            dve.wait_ge(loaded, 16)
            every = lambda n: wb[:, n:n + 1, :].to_broadcast([P, B * T, D])
            link(v.tensor_tensor(x[:, :, :], x[:, :, :], every(0), ALU.mult))
            link(v.tensor_tensor(x[:, :, :], x[:, :, :], every(1), ALU.add))
            if h is not None:
                link(v.tensor_tensor(h[:, :, :], h[:, :, :], x[:, :, :], ALU.add))
            link.finished()


def gate_stage(nc, x, wd, cst, vals, picks):
    E = MOE_E
    with ExitStack() as ctx:
        def sb(n, shape, dt=F32):
            return ctx.enter_context(nc.sbuf_tensor(f"gate_{n}", shape, dt))

        sem = ctx.enter_context(semaphores(nc, "gate"))

        ps = ctx.enter_context(nc.psum_tensor("gate_ps", [P, 8, 512], F32))
        rw, rb, iota = sb("rw", [P, 2, E]), sb("rb", [P, E]), sb("iota", [P, E])
        ones = sb("ones", [P, P])
        xh, xn = sb("xh", [P, T, D]), sb("xn", [P, 2, S])
        sc, z = sb("sc", [P, T, E]), sb("z", [P, B, E])
        m, g, eq, cand = sb("m", [P, B]), sb("g", [P, B, E]), sb("eq", [P, B, E]), sb("cand", [P, B, E])
        pf = sb("pf", [P, TOP_K, B])
        loaded, dch = sem("loaded"), sem("vector_chain")
        ones_ready, xhat_ready, xT_done, xn_ready = sem("ones_ready"), sem("xhat_ready"), sem("xT_done"), sem("xn_ready")
        sc_done, sc_ready, mean_done, z_ready = sem("sc_done"), sem("sc_ready"), sem("mean_done"), sem("z_ready")
        logits_ready, exp_ready = sem("logits_ready"), sem("exp_ready")
        block = ctx.enter_context(nc.Block())
        ident = cst["ident"]

        @block.sync
        def _(sp):
            sp.dma_start(rw[:, :, :].rearrange("p c e -> p (c e)"), wd["rw"]).then_inc(loaded, 16)
            sp.dma_start(rb[:, :], wd["rb"]).then_inc(loaded, 16)
            sp.dma_start(iota[:, :], wd["iota"]).then_inc(loaded, 16)
            sp.wait_ge(loaded, 48)

        @block.gpsimd
        def _(pool):
            nc.gpsimd.memset(ones[:, :], 1.0).then_inc(ones_ready, 1)

        @block.tensor
        def _(pe):
            mm, tr = nc.tensor.matmul, nc.tensor.transpose
            pe.wait_ge(loaded, 48)
            pe.wait_ge(ones_ready, 1)
            with pe.Fori(0, B) as b:
                pe.wait_ge(xhat_ready, b + 1)
                for t in range(T):
                    for c, k in KC:
                        last = tr(ps[0:k, 7, c * S + t * P:c * S + (t + 1) * P], xh[:, t, c * P:c * P + k], ident[:, :])
                last.then_inc(xT_done, 1)
                pe.wait_ge(xn_ready, 2 * b + 2)
                for t in range(T):
                    for c, k in KC:
                        last = mm(ps[:, 0, t * E:(t + 1) * E], xn[0:k, c, t * P:(t + 1) * P], rw[0:k, c, :],
                                  start=(c == 0), stop=(c == 1))
                last.then_inc(sc_done, 1)
                pe.wait_ge(sc_ready, b + 1)
                for t in range(T):
                    last = mm(ps[:, 1, 0:E], ones[:, :], sc[:, t, :], start=(t == 0), stop=(t == 1))
                last.then_inc(mean_done, 1)

        @block.scalar
        def _(act):
            with act.Fori(0, B) as b:
                act.wait_ge(xT_done, b + 1)
                for c, k in KC:
                    nc.scalar.activation(xn[0:k, c, :], ps[0:k, 7, c * S:(c + 1) * S], ACT.Copy).then_inc(xn_ready, 1)
            act.wait_ge(logits_ready, 1)
            nc.scalar.activation(g[:, :, :].rearrange("p b e -> p (b e)"), z[:, :, :].rearrange("p b e -> p (b e)"),
                                 ACT.Exp).then_inc(exp_ready, 1)

        @block.vector
        def _(dve):
            v = nc.vector
            dve.wait_ge(loaded, 48)
            with dve.Fori(0, B) as b:
                v.tensor_copy(xh[:, :, :], x[:, bass.ds(b * T, T), :]).then_inc(xhat_ready, 1)
                dve.wait_ge(sc_done, b + 1)
                v.tensor_copy(sc[:, :, :].rearrange("p t e -> p (t e)"), ps[:, 0, 0:T * E]).then_inc(sc_ready, 1)
                dve.wait_ge(mean_done, b + 1)
                v.scalar_tensor_tensor(out=z[:, bass.ds(b, 1), :].rearrange("p a e -> p (a e)"), in0=ps[:, 1, 0:E],
                                       scalar=1.0 / S, in1=rb[:, :], op0=ALU.mult, op1=ALU.add).then_inc(z_ready, 1)
                dve.wait_ge(z_ready, b + 1)
            link = chain(dve, dch, 0, 14)
            over = lambda a: a.unsqueeze(2).to_broadcast([P, B, E])
            io = iota[:, :].unsqueeze(1).to_broadcast([P, B, E])
            link(v.tensor_reduce(m[:, :], z[:, :, :], AX.X, ALU.max))
            v.tensor_tensor(z[:, :, :], z[:, :, :], over(m[:, :]), ALU.subtract).then_inc(logits_ready, 1)
            dve.wait_ge(exp_ready, 1)
            link(v.tensor_reduce(m[:, :], g[:, :, :], AX.X, ALU.add))
            link(v.reciprocal(m[:, :], m[:, :]))
            link(v.tensor_tensor(g[:, :, :], g[:, :, :], over(m[:, :]), ALU.mult))
            for k in range(TOP_K):
                link(v.tensor_reduce(vals[:, k, :], g[:, :, :], AX.X, ALU.max))
                link(v.tensor_tensor(eq[:, :, :], g[:, :, :], over(vals[:, k, :]), ALU.is_ge))
                link(v.scalar_tensor_tensor(out=cand[:, :, :], in0=eq[:, :, :], scalar=-float(E), in1=io,
                                            op0=ALU.mult, op1=ALU.add))
                link(v.tensor_reduce(pf[:, k, :], cand[:, :, :], AX.X, ALU.min))
                if k == 0:
                    link(v.tensor_tensor(eq[:, :, :], cand[:, :, :], over(pf[:, k, :]), ALU.is_equal))
                    link(v.scalar_tensor_tensor(out=g[:, :, :], in0=eq[:, :, :], scalar=-2.0, in1=g[:, :, :],
                                                op0=ALU.mult, op1=ALU.add))
            v.tensor_scalar(picks[:, :, :], pf[:, :, :].rearrange("p k b -> p b k"), float(E), None, ALU.add)
            link.finished()


def expert_stage(nc, name, x, dst, n, func, wd, cst, moe):
    with ExitStack() as ctx:
        def sb(nm, shape, dt=F32):
            return ctx.enter_context(nc.sbuf_tensor(f"{name}_{nm}", shape, dt))

        sem = ctx.enter_context(semaphores(nc, name))

        ps = ctx.enter_context(nc.psum_tensor(f"{name}_ps", [P, 8, 512], F32))
        w1, w2 = sb("w1", [P, n, 2 * F]), sb("w2", [P, n, FC * D])
        b1, b2 = sb("b1", [P, n, FC]), sb("b2", [P, n, D])
        xh, xn = sb("xh", [P, T, D]), sb("xn", [P, 2, S])
        hid = sb("hid", [P, 2, FC, S])
        yb = sb("yb", [P, T, D])
        wg, bg, iota = sb("wg", [P, 2, n]), sb("bg", [P, n]), sb("iota", [P, MOE_E])
        lg, eq, m, hot = sb("lg", [P, T, n]), sb("eq", [P, T, n]), sb("m", [P, T]), sb("hot", [P, T, n])
        loaded = [sem(f"loaded{j}") for j in range(n)]
        gate_loaded, dch = sem("gate_loaded"), sem("vector_chain")
        xhat_ready, xT_done, xn_ready = sem("xhat_ready"), sem("xT_done"), sem("xn_ready")
        lg_done, h_done, h_ready = sem("lg_done"), sem("h_done"), sem("h_ready")
        y_done, acc_ready = sem("y_done"), sem("acc_ready")
        block = ctx.enter_context(nc.Block())
        ident = cst["ident"]
        LOADS = 64

        def wait_weights(eng, j, b):
            eng.wait_ge(loaded[j], (b + 1) * LOADS if moe else LOADS)

        @block.sync
        def _(sp):
            def fetch(j, e):
                for d, s in ((w1, wd["w1"]), (w2, wd["w2"]), (b1, wd["b1"]), (b2, wd["b2"])):
                    sp.dma_start(d[:, j, :], s[bass.ds(e, 1)].rearrange("a p n -> (a p) n")).then_inc(loaded[j], 16)

            if moe:
                def pick(b, j):
                    fetch(j, sp.value_load(moe[1][0:1, bass.ds(b, 1), j:j + 1].rearrange("p a k -> p (a k)"),
                                           min_val=0, max_val=MOE_E - 1))

                for j in range(n):
                    pick(0, j)
                with sp.Fori(1, B) as b:
                    for j in range(n):
                        sp.wait_ge(acc_ready, n * (b - 1) + j + 1)
                        pick(b, j)
            else:
                for d, s in ((wg[:, :, :].rearrange("p c e -> p (c e)"), wd["wg"]), (bg[:, :], wd["bg"]),
                             (iota[:, :], wd["iota"])):
                    sp.dma_start(d, s).then_inc(gate_loaded, 16)
                for j in range(n):
                    fetch(j, j)
                sp.wait_ge(gate_loaded, 48)
            for j in range(n):
                sp.wait_ge(loaded[j], LOADS * (B if moe else 1))

        @block.tensor
        def _(pe):
            mm, tr = nc.tensor.matmul, nc.tensor.transpose
            if not moe:
                pe.wait_ge(gate_loaded, 48)
            with pe.Fori(0, B) as b:
                pe.wait_ge(xhat_ready, b + 1)
                for t in range(T):
                    for c, k in KC:
                        last = tr(ps[0:k, 7, c * S + t * P:c * S + (t + 1) * P], xh[:, t, c * P:c * P + k], ident[:, :])
                last.then_inc(xT_done, 1)
                pe.wait_ge(xn_ready, 2 * b + 2)
                if not moe:
                    for t in range(T):
                        for c, k in KC:
                            last = mm(ps[:, 6, t * n:(t + 1) * n], xn[0:k, c, t * P:(t + 1) * P], wg[0:k, c, :],
                                      start=(c == 0), stop=(c == 1))
                    last.then_inc(lg_done, 1)

                def up(j):
                    wait_weights(pe, j, b)
                    w = w1[:, j, :].rearrange("p (c f) -> p c f", c=2)
                    for q in range(FC):
                        i = j * FC + q
                        if i >= 2:
                            pe.wait_ge(h_ready, b * n * FC + i - 1)
                        for c, k in KC:
                            last = mm(ps[:, q % 2, 0:S], w[0:k, c, q * P:(q + 1) * P], xn[0:k, c, :],
                                      start=(c == 0), stop=(c == 1))
                        last.then_inc(h_done, 1)

                def down(j):
                    if j >= 2:
                        pe.wait_ge(acc_ready, b * n + j - 1)
                    w = w2[:, j, :].rearrange("p (q d) -> p q d", q=FC)
                    for t in range(T):
                        for q in range(FC):
                            if t == 0:
                                pe.wait_ge(h_ready, b * n * FC + j * FC + q + 1)
                            last = mm(ps[:, 2 + 2 * (j % 2) + t, 0:D], hid[:, j % 2, q, t * P:(t + 1) * P], w[:, q, :],
                                      start=(q == 0), stop=(q == FC - 1))
                    last.then_inc(y_done, 1)

                up(0)
                for j in range(n):
                    if j + 1 < n:
                        up(j + 1)
                    down(j)

        @block.scalar
        def _(act):
            go = nc.scalar.activation
            with act.Fori(0, B) as b:
                act.wait_ge(xT_done, b + 1)
                for c, k in KC:
                    go(xn[0:k, c, :], ps[0:k, 7, c * S:(c + 1) * S], ACT.Copy).then_inc(xn_ready, 1)
                for j in range(n):
                    wait_weights(act, j, b)
                    if j >= 2:
                        act.wait_ge(y_done, b * n + j - 1)
                    for q in range(FC):
                        act.wait_ge(h_done, b * n * FC + j * FC + q + 1)
                        go(hid[:, j % 2, q, :], ps[:, q % 2, 0:S], func, bias=b1[:, j, q:q + 1]).then_inc(h_ready, 1)

        @block.vector
        def _(dve):
            v = nc.vector
            if not moe:
                dve.wait_ge(gate_loaded, 48)
            with dve.Fori(0, B) as b:
                link = chain(dve, dch, b, n + (0 if moe else 5))
                v.tensor_copy(xh[:, :, :], x[:, bass.ds(b * T, T), :]).then_inc(xhat_ready, 1)
                if not moe:
                    dve.wait_ge(lg_done, b + 1)
                    over = lambda a: a.unsqueeze(2).to_broadcast([P, T, n])
                    bgt = bg[:, :].unsqueeze(1).to_broadcast([P, T, n])
                    io = iota[:, 0:n].unsqueeze(1).to_broadcast([P, T, n])
                    link(v.tensor_tensor(lg[:, :, :], ps[:, 6, 0:T * n].rearrange("p (t e) -> p t e", t=T), bgt,
                                         ALU.add))
                    link(v.tensor_reduce(m[:, :], lg[:, :, :], AX.X, ALU.max))
                    link(v.tensor_tensor(eq[:, :, :], lg[:, :, :], over(m[:, :]), ALU.is_ge))
                    link(v.scalar_tensor_tensor(out=lg[:, :, :], in0=eq[:, :, :], scalar=-8.0, in1=io, op0=ALU.mult,
                                                op1=ALU.add))
                    link(v.tensor_reduce(m[:, :], lg[:, :, :], AX.X, ALU.min))
                    v.tensor_tensor(hot[:, :, :], lg[:, :, :], over(m[:, :]), ALU.is_equal)
                for j in range(n):
                    dve.wait_ge(y_done, b * n + j + 1)
                    wait_weights(dve, j, b)
                    for t in range(T):
                        last = v.tensor_tensor(yb[:, t, :], ps[:, 2 + 2 * (j % 2) + t, 0:D], b2[:, j, :], ALU.add)
                    link(last)
                    for t in range(T):
                        dt = dst[:, bass.ds(b * T + t, 1), :].rearrange("p a d -> p (a d)")
                        co = (moe[0][:, j, bass.ds(b, 1)] if moe else hot[:, t, j:j + 1])
                        last = v.scalar_tensor_tensor(out=dt, in0=yb[:, t, :], scalar=co, in1=dt, op0=ALU.mult,
                                                      op1=ALU.add)
                    last.then_inc(acc_ready, 1)
                    dve.wait_ge(acc_ready, b * n + j + 1)
                link.finished()


def store_stage(nc, h, out):
    with nc.semaphore("out_stored") as stored, nc.Block() as block:
        @block.sync
        def _(sp):
            dst = out.rearrange("b s d -> (b s) d").rearrange("(n p) d -> p n d", p=P)
            sp.dma_start(dst, h[:, :, :]).then_inc(stored, 16)
            sp.wait_ge(stored, 16)


def lm_tower(nc, a, out, upto="all"):
    part = lambda prefix: {k[len(prefix):]: v for k, v in a.items() if k.startswith(prefix)}
    with ExitStack() as ctx:
        def sb(n, shape, dt=F32):
            return ctx.enter_context(nc.sbuf_tensor(n, shape, dt))

        h = sb("h_stream", [P, B * T, D])
        x = sb("x_stream", [P, B * T, D])
        vals, picks = sb("vals", [P, TOP_K, B]), sb("picks", [P, B, TOP_K], I32)
        cst = {"ident": sb("ident", [P, P]), "identr": sb("identr", [P, P], F32R), "maskqk": sb("maskqk", [P, 2]),
               "blockmask": sb("blockmask", [P, P]), "newton": sb("newton", [P, 2, T])}
        scratch = nc.dram_tensor("channel_attention", [B, D, S], F32, kind="Internal").ap()
        embedding_stage(nc, x, a, cst)
        attention_stage(nc, "tok", "tok", h, x, part("tok_"), cst)
        glue_stage(nc, "to_vit", h, x, cst, False)
        attention_stage(nc, "vit", "vit", h, x, part("vit_"), cst)
        glue_stage(nc, "to_ffn", h, x, cst, True)
        if upto != "h2":
            f = part("ffn_")
            channel_attention_stage(nc, x, f, cst, scratch)
            channel_projection_stage(nc, x, f, cst, scratch)
            global_norm_stage(nc, "gn1", x, None, f["ln1"], cst)
            gate_stage(nc, x, f, cst, vals, picks)
            expert_stage(nc, "moe", x, x, TOP_K, ACT.Gelu_apprx_tanh, part("moe_"), cst, (vals, picks))
            global_norm_stage(nc, "gn2", x, h, f["ln2"], cst)
            if upto != "h3":
                attention_stage(nc, "l1", "l1", h, x, part("l1_"), cst)
                glue_stage(nc, "to_experts", h, x, cst, False)
                expert_stage(nc, "ex", x, h, L1_E, ACT.Gelu, part("ex_"), cst, None)
        store_stage(nc, h, out)


def positions():
    f = np.float32
    pos = np.arange(S, dtype=f)[:, None]
    i = np.arange(D, dtype=f)[None, :]
    ang = (pos / np.power(f(10000.0), (f(2.0) * i / f(D)).astype(f)).astype(f)).astype(f)
    tab = np.where(np.arange(D)[None, :] % 2 == 0, np.cos(ang), np.sin(ang)).astype(f)
    return np.ascontiguousarray(tab.reshape(T, P, D).transpose(1, 0, 2).reshape(P, T * D))


def rows(w):
    lead, n = w.shape[:-2], w.shape[-1]
    out = np.zeros(lead + (P, 2, n), np.float32)
    out[..., :, 0, :] = w[..., 0:P, :]
    out[..., 0:D2, 1, :] = w[..., P:D, :]
    return out.reshape(lead + (P, 2 * n))


def hidden_rows(w):
    lead, n = w.shape[:-2], w.shape[-1]
    w = w.reshape(lead + (FC, P, n))
    return np.ascontiguousarray(np.moveaxis(w, -3, -2)).reshape(lead + (P, FC * n))


def spread(v):
    return np.ascontiguousarray(np.broadcast_to(v[..., None, :], v.shape[:-1] + (P, v.shape[-1])))


def stacked(w):
    out = np.zeros((D, PAIRS, 2, SLOT), np.float32)
    cols = w.reshape(D, PAIRS, 2, DH)
    for s in range(3):
        out[:, :, :, s * DH:(s + 1) * DH] = cols
    return rows(out.reshape(D, PAIRS * P))


def stacked_heads(w):
    out = np.zeros((w.shape[0], P, PAIRS, 2, SLOT), np.float32)
    for p in range(PAIRS):
        for a in range(2):
            hd = 2 * p + a
            r = SLOT * ((p // 2) % 2) + DH * (hd % 4)
            for s in range(3):
                out[:, r:r + DH, p, a, s * DH:(s + 1) * DH] = w[:, hd].transpose(0, 2, 1)
    return out.reshape(w.shape[0], P, PAIRS * P)


LO_ROWS = ((2,), (1,))


def stacked_bias(bq, bk):
    L = bq.shape[0]
    full = np.zeros((L, 2, SLOT, 2, PAIRS), np.float32)
    low = np.zeros_like(full)
    for i, bias in enumerate((bq, bk)):
        bb = bias.reshape(L, PAIRS, 2, DH).transpose(0, 2, 3, 1)
        for s in range(3):
            full[:, :, s * DH:(s + 1) * DH, i, :] = bb
            if s in LO_ROWS[i]:
                low[:, :, s * DH:(s + 1) * DH, i, :] = bb
    full[:, :, MROW:MROW + 2, 1, :] = 1.0
    return full.reshape(L, P, 2 * PAIRS), low.reshape(L, P, 2 * PAIRS)


def feature_pairs(g, b):
    gb = np.stack([g, b], -1)
    return rows(gb)


def block_diagonal(w):
    out = np.zeros((w.shape[0], D, D), np.float32)
    for hd in range(H):
        out[:, hd * DH:(hd + 1) * DH, hd * DH:(hd + 1) * DH] = w[:, hd].transpose(0, 2, 1)
    return out


def pack(i):
    f = {k: np.asarray(v) for k, v in i.items()}
    one = lambda v: v[None]
    n = {}
    n["tokens"] = np.ascontiguousarray(f["x"].reshape(B * T, P).T)
    n["pos"] = positions()
    n["ident"] = np.eye(P, dtype=np.float32)
    mask = np.zeros((2, SLOT, 2), np.float32)
    for j in range(2):
        for s in LO_ROWS[j]:
            mask[:, s * DH:(s + 1) * DH, j] = 1.0
    n["maskqk"] = mask.reshape(P, 2)
    r = np.arange(P) // DH
    n["blockmask"] = np.where(r[:, None] == r[None, :], 0.0, -1e30).astype(np.float32)
    n["emb"] = f["L0_tok_emb"]
    t = "L0_tok_"
    n["tok_wq"], n["tok_wk"], n["tok_wv"] = (one(stacked(f[t + "wq"])), one(stacked(f[t + "wk"])),
                                             one(rows(f[t + "wv"])))
    n["tok_bqk"], n["tok_bqk_lo"] = stacked_bias(one(f[t + "bq"]), one(f[t + "bk"]))
    n["tok_bv"], n["tok_wo"], n["tok_bo"] = one(spread(f[t + "bv"])), one(rows(f[t + "wo"])), one(spread(f[t + "bo"]))
    n["tok_w1"], n["tok_w2"] = one(rows(f[t + "w1"])), one(hidden_rows(f[t + "w2"]))
    n["tok_b1"], n["tok_b2"] = one(f[t + "b1"].reshape(FC, P).T), one(spread(f[t + "b2"]))
    n["tok_gb"] = one(spread(np.stack([f[t + "gamma1"], f[t + "beta1"], f[t + "gamma2"], f[t + "beta2"]])
                             .transpose(0, 1)).transpose(1, 0, 2).reshape(P, 4 * D))
    t = "L0_attn_"
    n["vit_wq"], n["vit_wk"] = stacked_heads(f[t + "qw"]), stacked_heads(f[t + "kw"])
    n["vit_wv"] = rows(block_diagonal(f[t + "vw"]))
    L = VIT_LAYERS
    n["vit_bqk"], n["vit_bqk_lo"] = stacked_bias(f[t + "qb"].reshape(L, D), f[t + "kb"].reshape(L, D))
    n["vit_bv"] = spread(f[t + "vb"].reshape(L, D))
    n["vit_ln1"] = feature_pairs(f[t + "ln1_g"], f[t + "ln1_b"])
    n["vit_ln2"] = feature_pairs(f[t + "ln2_g"], f[t + "ln2_b"])
    n["vit_w1"], n["vit_w2"] = rows(f[t + "w1"].transpose(0, 2, 1)), hidden_rows(f[t + "w2"].transpose(0, 2, 1))
    n["vit_b1"], n["vit_b2"] = f[t + "b1"].reshape(L, FC, P).transpose(0, 2, 1), spread(f[t + "b2"])
    t = "L1_attn_"
    w, z = f[t + "W_qkv"], np.zeros((1, D), np.float32)
    n["l1_wq"], n["l1_wk"], n["l1_wv"] = (one(stacked(w[:, 0:D])), one(stacked(w[:, D:2 * D])),
                                          one(rows(w[:, 2 * D:3 * D])))
    n["l1_bqk"], n["l1_bqk_lo"] = stacked_bias(z, z)
    n["l1_bv"] = spread(z)
    n["l1_wo"], n["l1_bo"] = one(rows(f[t + "W_proj"])), one(spread(f[t + "b_proj"]))
    t = "L0_ffn_"
    n["ffn_w1"] = rows(f[t + "W1_w"])
    n["ffn_bqk"] = spread(f[t + "W1_b"][0:2 * D])
    bv = np.zeros((P, 2), np.float32)
    bv[:, 0], bv[0:D2, 1] = f[t + "W1_b"][2 * D:2 * D + P], f[t + "W1_b"][2 * D + P:]
    n["ffn_bv"] = bv
    n["ffn_w2"], n["ffn_b2"] = rows(f[t + "W2_w"]), spread(f[t + "W2_b"])
    for ln in ("ln1", "ln2"):
        n["ffn_" + ln] = np.concatenate([spread(f[t + ln + "_w"]), spread(f[t + ln + "_b"])], 1)
    n["ffn_rw"], n["ffn_rb"] = rows(f[t + "r_w"]), spread(f[t + "r_b"])
    iota = spread(np.arange(MOE_E, dtype=np.float32))
    n["ffn_iota"] = n["ex_iota"] = iota
    n["moe_w1"], n["moe_w2"] = rows(f[t + "fc_w"]), hidden_rows(f[t + "proj_w"])
    n["moe_b1"], n["moe_b2"] = f[t + "fc_b"].reshape(MOE_E, FC, P).transpose(0, 2, 1), spread(f[t + "proj_b"])
    t = "L1_ffn_"
    n["ex_w1"], n["ex_w2"] = rows(f[t + "W1"]), hidden_rows(f[t + "W2"])
    n["ex_b1"], n["ex_b2"] = f[t + "b1"].reshape(L1_E, FC, P).transpose(0, 2, 1), spread(f[t + "b2"])
    n["ex_wg"], n["ex_bg"] = rows(f[t + "Wg"]), spread(f[t + "bg"])
    return {k: np.ascontiguousarray(v) for k, v in n.items()}


def kernel(**inputs):
    import concourse.bacc as bacc
    from concourse.bass_utils import run_bass_kernel_spmd

    nc = bacc.Bacc("TRN2", target_bir_lowering=False, num_devices=1)
    arrays, aps = {}, {}
    for name, value in pack(inputs).items():
        arrays[f"in_{name}_dram"] = value
        aps[name] = nc.dram_tensor(f"in_{name}_dram", value.shape, mybir.dt.from_np(value.dtype),
                                   kind="ExternalInput").ap()
    out = nc.dram_tensor("out_0_dram", (B, S, D), F32, kind="ExternalOutput").ap()
    lm_tower(nc, aps, out)
    return run_bass_kernel_spmd(nc, [arrays], core_ids=[0]).results[0]["out_0_dram"]
```

```python
from contextlib import ExitStack, contextmanager

import numpy as np

import concourse.bass as bass
from concourse import mybir

F32 = mybir.dt.float32
F32R = mybir.dt.float32r
I32 = mybir.dt.int32
ALU = mybir.AluOpType
ACT = mybir.ActivationFunctionType
AX = mybir.AxisListType

B, S, D, F = 8, 256, 192, 768
H, DH = 12, 16
P = 128
T = S // P
D2 = D - P
KC = ((0, P), (1, D2))
FC = F // P
PAIRS = H // 2
GROUPS = H // 4
SLOT = 64
MROW = 48
VIT_LAYERS = 8
MOE_E, TOP_K, L1_E = 8, 2, 4
VOCAB = 8000
SCALE = 0.25


@contextmanager
def semaphores(nc, stage):
    taken = []

    def sem(name):
        taken.append(nc.alloc_semaphore(f"{stage}_{name}"))
        return taken[-1]

    yield sem
    nc.clear_and_free_semaphores(taken)
    nc.all_engine_barrier()


class chain:

    def __init__(self, eng, sem, it, per):
        self.eng, self.sem, self.it, self.per, self.done = eng, sem, it, per, 0

    def __call__(self, ins):
        self.done += 1
        ins.then_inc(self.sem, 1)
        self.eng.wait_ge(self.sem, self.it * self.per + self.done)

    def finished(self):
        assert self.done == self.per, (self.done, self.per)


RSQRT_SEED = float(0x5F3759DF)
NEWTON = 3


def norm_stats(nc, dve, link, x, st, mv, rt, var_ready, root_ready, turn, post=False):
    v = nc.vector
    v.bn_stats(st[:, 0, :], x[:, 0, :])
    link(v.bn_stats(st[:, 1, :], x[:, 1, :]))
    v.memset(rt[:, 5, :], 0.0)
    v.bn_aggr(mv[:, 0, :], st[:, 0, :])
    link(v.bn_aggr(mv[:, 1, :], st[:, 1, :]))
    if post:
        link(v.tensor_scalar(rt[:, 0, :], mv[:, :, 1], 1e-30, None, ALU.max))
    else:
        link(v.tensor_scalar(rt[:, 0, :], mv[:, :, 1], 1e-5, None, ALU.add))
    bits = rt[:, 1, :].bitcast(I32)
    v.tensor_scalar(rt[:, 4, :], rt[:, 0, :], -0.5, None, ALU.mult)
    link(v.tensor_scalar(bits, rt[:, 0, :].bitcast(I32), 1, None, ALU.logical_shift_right))
    v.tensor_scalar(bits, bits, -1.0, RSQRT_SEED, ALU.mult, ALU.add).then_inc(var_ready, 1)
    dve.wait_ge(root_ready, turn)


def root(nc, pool, link, rt, half3, eps, var_ready, root_ready, turn, post):
    g = nc.gpsimd
    pool.wait_ge(var_ready, turn)
    vv, y, s, out, vh = rt[:, 0, :], rt[:, 1, :], rt[:, 2, :], rt[:, 3, :], rt[:, 4, :]
    for n in range(NEWTON):
        link(g.tensor_tensor(s, y, y, ALU.mult))
        link(g.tensor_tensor(s, s, vh, ALU.mult))
        link(g.tensor_tensor(s, s, half3, ALU.add))
        if n < NEWTON - 1 or post:
            link(g.tensor_tensor(y, y, s, ALU.mult))
        else:
            g.tensor_tensor(out, y, s, ALU.mult).then_inc(root_ready, 1)
    if post:
        link(g.tensor_tensor(s, y, vv, ALU.mult))
        g.tensor_tensor(out, s, eps, ALU.add).then_inc(root_ready, 1)


def root_steps(post):
    return 4 * NEWTON + 1 if post else 4 * NEWTON - 1


def wait_from(eng, sem, n):
    if isinstance(n, int) and n < 1:
        return
    eng.wait_ge(sem, n)


def turns(eng, units, body):
    body(0)
    body(1)
    with eng.Fori(2, units - 1) as i:
        body(i)
    for i in range(units - 1, units + 2):
        body(i)


def attention_stage(nc, name, kind, h, x, wd, cst):
    vit, tok, l1 = kind == "vit", kind == "tok", kind == "l1"
    layers = VIT_LAYERS if vit else 1
    N = layers * B
    mlp = not l1
    proj = not vit
    res = h if l1 else x
    with ExitStack() as ctx:
        def sb(n, shape, dt=F32):
            return ctx.enter_context(nc.sbuf_tensor(f"{name}_{n}", shape, dt))

        sem = ctx.enter_context(semaphores(nc, name))

        ps = ctx.enter_context(nc.psum_tensor(f"{name}_ps", [P, 8, 512], F32))
        wq = sb("wq", [P, 2, PAIRS, P])
        wk = sb("wk", [P, 2, PAIRS, P])
        wv = sb("wv", [P, 2, D])
        bqk = sb("bqk", [P, 2, PAIRS])
        bqk_lo = sb("bqk_lo", [P, 2, PAIRS])
        bv = sb("bv", [P, D])
        ln1 = sb("ln1", [P, 2, 2])
        ln2 = sb("ln2", [P, 2, 2])
        wo = sb("wo", [P, 2, D])
        bo = sb("bo", [P, D])
        w1 = sb("w1", [P, 2, F])
        b1 = sb("b1", [P, FC])
        w2 = sb("w2", [P, FC, D])
        b2 = sb("b2", [P, D])
        gb = sb("gb", [P, 4, D])
        st, mv = sb("st", [P, 3, T, 6]), sb("mv", [P, 3, T, 2])
        rt = [sb(f"rt{n}", [P, 6, T]) for n in range(3)]
        xh, xh2, xg = sb("xh", [P, T, D]), sb("xh2", [P, T, D]), sb("xg", [P, T, D])
        xn, xn2 = sb("xn", [P, 2, S]), sb("xn2", [P, 2, S])
        hm = sb("hm", [P, 2, S], F32R)
        qk = sb("qk", [P, 3, 2, S], F32R)
        q2 = sb("q2", [P, 2, S], F32R)
        mx = sb("mx", [P, 2, 2, T])
        mb = sb("mb", [P, 2, T, P], F32R)
        va = sb("va", [P, T, H, 32])
        pt = sb("pt", [P, H, T, S])
        ot = sb("ot", [P, GROUPS, S])
        rcp = sb("rcp", [P, T, H])
        att = sb("att", [P, T, D])
        at = sb("at", [P, 2, S])
        r1, r2 = sb("r1", [P, T, D]), sb("r2", [P, T, D])
        yb = sb("yb", [P, T, D])
        hid = sb("hid", [P, FC, S])

        ln_loaded, w_loaded, wm_loaded = sem("ln1_loaded"), sem("attn_weights_loaded"), sem("mlp_weights_loaded")
        zeroed, cleared = sem("zeroed"), sem("cleared")
        ln1_step, mb_step, out_step, y_step, pool_step = (sem("ln1_step"), sem("mb_step"), sem("out_step"),
                                                          sem("y_step"), sem("pool_step"))
        last_step, pool2_step, pool3_step = sem("last_norm_step"), sem("pool2_step"), sem("pool3_step")
        att_added = sem("att_added")
        out2_step, out3_step, h1_kept = sem("h1_step"), sem("result_step"), sem("h1_kept")
        var_ready = [sem(f"var_ready{n}") for n in range(3)]
        root_ready = [sem(f"root_ready{n}") for n in range(3)]
        xhat_ready, xT_done, xn_ready = sem("xhat_ready"), sem("xT_done"), sem("xn_ready")
        v_done, v_ready = sem("v_done"), sem("v_ready")
        proj_done, hm_ready, qk_ready = sem("proj_done"), sem("hm_ready"), sem("qk_ready")
        s_done, mx_done, m_ready = sem("s_done"), sem("mx_done"), sem("m_ready")
        mt_done, q2_ready, st_done = sem("mt_done"), sem("q2_ready"), sem("st_done")
        p_ready, pv_done, oT_ready = sem("p_ready"), sem("pv_done"), sem("oT_ready")
        ot_done, att_ready = sem("ot_done"), sem("att_ready")
        aT_done, aT_ready, op_done, op_read = sem("aT_done"), sem("aT_ready"), sem("op_done"), sem("op_read")
        xhat2_ready, xT2_done, xn2_ready = sem("xhat2_ready"), sem("xT2_done"), sem("xn2_ready")
        h_done, h_ready, y_done, y_read, x_ready = (sem("h_done"), sem("h_ready"), sem("y_done"), sem("y_read"),
                                                    sem("x_ready"))

        ident, identr, maskqk = cst["ident"], cst["identr"], cst["maskqk"]
        half3, eps = cst["newton"][:, 0, :], cst["newton"][:, 1, :]

        def at_unit(t_, u):
            return t_[:, bass.ds((u % B) * T, T), :]

        def at_tile(t_, u, t):
            return t_[:, bass.ds((u % B) * T + t, 1), :].rearrange("p a d -> p (a d)")

        ln_loads = [(ln1, wd["ln1"])] if vit else []
        attn_loads = [(wq, wd["wq"]), (wk, wd["wk"]), (wv, wd["wv"]), (bqk, wd["bqk"]), (bqk_lo, wd["bqk_lo"]),
                      (bv, wd["bv"])]
        if proj:
            attn_loads += [(wo, wd["wo"]), (bo, wd["bo"])]
        mlp_loads = [(w1, wd["w1"]), (b1, wd["b1"]), (w2, wd["w2"]), (b2, wd["b2"])] if mlp else []
        mlp_loads += [(ln2, wd["ln2"])] if vit else []
        mlp_loads += [(gb, wd["gb"])] if tok else []
        NL, NA, NM = 16 * len(ln_loads), 16 * len(attn_loads), 16 * len(mlp_loads)

        def loads_of(u, n):
            return (u // B + 1) * n if layers > 1 else n

        block = ctx.enter_context(nc.Block())

        def load(sp, loads, l, s):
            for dst, src in loads:
                part = src[bass.ds(l, 1)].rearrange("a p n -> (a p) n")
                flat = dst[:, :] if len(dst.shape) == 2 else (
                    dst[:, :, :].rearrange("p a b -> p (a b)") if len(dst.shape) == 3
                    else dst[:, :, :, :].rearrange("p a b c -> p (a b c)"))
                sp.dma_start(flat[:, 0:src.shape[2]], part).then_inc(s, 16)

        @block.sync
        def _(sp):
            load(sp, ln_loads, 0, ln_loaded)
            load(sp, attn_loads, 0, w_loaded)
            load(sp, mlp_loads, 0, wm_loaded)
            if layers > 1:
                with sp.Fori(1, layers) as l:
                    sp.wait_ge(xn_ready, l * B * 2)
                    load(sp, ln_loads, l, ln_loaded)
                    sp.wait_ge(qk_ready, l * B * PAIRS)
                    sp.wait_ge(v_ready, l * B)
                    load(sp, attn_loads, l, w_loaded)
                    sp.wait_ge(y_read, l * B)
                    load(sp, mlp_loads, l, wm_loaded)
                sp.wait_ge(ln_loaded, NL * layers)
            sp.wait_ge(w_loaded, NA * layers)
            if mlp:
                sp.wait_ge(wm_loaded, NM * layers)

        @block.gpsimd
        def _(pool):
            def add(u, src, ready, added):
                pool.wait_ge(ready, u + 1)
                nc.gpsimd.tensor_tensor(at_unit(x, u), at_unit(x, u), src[:, :, :], ALU.add).then_inc(added, 1)

            def norm(n, step, u, post):
                link = chain(pool, step, u, root_steps(post))
                root(nc, pool, link, rt[n], half3, eps, var_ready[n], root_ready[n], u + 1, post)
                link.finished()

            def body(i):
                loop = not isinstance(i, int)
                if not tok and (loop or i + 1 < N):
                    norm(0, pool_step, i + 1, False)
                if tok and (loop or i >= 2):
                    norm(2, pool3_step, i - 2, True)
                if vit and (loop or i >= 2):
                    add(i - 2, yb, y_read, x_ready)
                if vit and (loop or 1 <= i <= N):
                    add(i - 1, att, att_ready, att_added)
                if mlp and (loop or 1 <= i <= N):
                    norm(1, pool2_step, i - 1, tok)

            if vit:
                nc.gpsimd.memset(rt[1][:, 5, :], 0.0).then_inc(x_ready, B)
            if not tok:
                norm(0, pool_step, 0, False)
            turns(pool, N, body)

        @block.tensor
        def _(pe):
            mm, tr = nc.tensor.matmul, nc.tensor.transpose

            def transposes(src, bank):
                for t in range(T):
                    for c, k in KC:
                        last = tr(ps[0:k, bank, c * S + t * P:c * S + (t + 1) * P],
                                  src[:, t, c * P:c * P + k], ident[:, :])
                return last

            def project(u, p):
                if p == 0:
                    pe.wait_ge(w_loaded, loads_of(u, NA))
                    pe.wait_ge(xn_ready, 2 * u + 2)
                wait_from(pe, qk_ready, u * PAIRS + p)
                for i, w in enumerate((wq, wk)):
                    out = ps[:, 2, i * S:(i + 1) * S]
                    if vit:
                        r, c = SLOT * ((p // 2) % 2), p // 4
                        last = mm(out, w[r:r + SLOT, 0, p, :], xn[r:r + SLOT, c, :], start=True, stop=True)
                    else:
                        for c, k in KC:
                            last = mm(out, w[0:k, c, p, :], xn[0:k, c, :], start=(c == 0), stop=(c == 1))
                last.then_inc(proj_done, 1)

            def scores(u, p):
                pe.wait_ge(qk_ready, u * PAIRS + p + 1)
                wait_from(pe, q2_ready, u * PAIRS + p)
                for a in range(2):
                    wait_from(pe, mx_done, u * H + 2 * (p - 1) + a + 1)
                    r = SLOT * a
                    for t in range(T):
                        last = mm(ps[:, a, t * S:(t + 1) * S], qk[r:r + SLOT, p % 3, 0, t * P:(t + 1) * P],
                                  qk[r:r + SLOT, p % 3, 1, :], start=True, stop=True)
                    last.then_inc(s_done, 1)

            def max_rows(u, p):
                pe.wait_ge(m_ready, u * PAIRS + p + 1)
                for t in range(T):
                    last = mm(ps[:, 0, t * P:(t + 1) * P], mb[:, p % 2, t, :], identr[:, :], start=True, stop=True)
                last.then_inc(mt_done, 1)

            def scores_t(u, p):
                pe.wait_ge(q2_ready, u * PAIRS + p + 1)
                for a in range(2):
                    hd, r = 2 * p + a, SLOT * a
                    wait_from(pe, p_ready, u * H + hd - 1)
                    for t in range(T):
                        last = mm(ps[:, 3 + a, t * S:(t + 1) * S],
                                  qk[r:r + SLOT, p % 3, 1, t * P:(t + 1) * P], q2[r:r + SLOT, p % 2, :],
                                  start=True, stop=True)
                    last.then_inc(st_done, 1)

            def weighted(u, g):
                if g == 0:
                    pe.wait_ge(v_ready, u + 1)
                pe.wait_ge(p_ready, u * H + 4 * g + 4)
                wait_from(pe, oT_ready, u * GROUPS + g)
                for t in range(T):
                    for j in range(4):
                        hd = 4 * g + j
                        last = mm(ps[32 * j:32 * j + 32, 6, 0:S], va[:, t, hd, :], pt[:, hd, t, :],
                                  start=(t == 0), stop=(t == T - 1), skip_group_check=True)
                last.then_inc(pv_done, 1)

            def input_t(u):
                pe.wait_ge(xhat_ready, u + 1)
                wait_from(pe, v_ready, u)
                transposes(xh, 6).then_inc(xT_done, 1)

            def values(u):
                wait_from(pe, oT_ready, u * GROUPS)
                for t in range(T):
                    for c, k in KC:
                        out = ps[:, 6, t * D:(t + 1) * D]
                        lhs = xn[0:k, c, t * P:(t + 1) * P]
                        if vit:
                            last = mm(out[:, c * P:c * P + k], lhs, wv[0:k, c, c * P:c * P + k],
                                      start=True, stop=True)
                        else:
                            last = mm(out, lhs, wv[0:k, c, :], start=(c == 0), stop=(c == 1))
                last.then_inc(v_done, 1)

            def output_t(u):
                pe.wait_ge(oT_ready, (u + 1) * GROUPS)
                if mlp:
                    wait_from(pe, y_read, u)
                if l1:
                    wait_from(pe, op_read, u)
                for t in range(T):
                    for g in range(GROUPS):
                        last = tr(ps[:, 5 + 2 * t, g * P:(g + 1) * P], ot[:, g, t * P:(t + 1) * P], ident[:, :])
                last.then_inc(ot_done, 1)

            def normed_t(u):
                pe.wait_ge(att_ready, u + 1)
                transposes(att, 5).then_inc(aT_done, 1)

            def project_out(u):
                pe.wait_ge(aT_ready, 2 * u + 2)
                for t in range(T):
                    for c, k in KC:
                        last = mm(ps[:, 7, t * D:(t + 1) * D], at[0:k, c, t * P:(t + 1) * P], wo[0:k, c, :],
                                  start=(c == 0), stop=(c == 1))
                last.then_inc(op_done, 1)

            def mlp_input_t(u):
                pe.wait_ge(xhat2_ready, u + 1)
                pe.wait_ge(oT_ready, (u + 2) * GROUPS - 1 if not isinstance(u, int) or u + 2 <= N
                           else N * GROUPS)
                transposes(xh2, 6).then_inc(xT2_done, 1)

            def mlp_up(u, chunks):
                if 0 in chunks:
                    pe.wait_ge(wm_loaded, loads_of(u, NM))
                    pe.wait_ge(xn2_ready, 2 * u + 2)
                for m in chunks:
                    if m >= 2:
                        pe.wait_ge(h_ready, u * FC + m - 1)
                    for c, k in KC:
                        last = mm(ps[:, 5 + 2 * (m % 2), 0:S], w1[0:k, c, m * P:(m + 1) * P], xn2[0:k, c, :],
                                  start=(c == 0), stop=(c == 1))
                    last.then_inc(h_done, 1)

            def mlp_down(u, t):
                pe.wait_ge(h_ready, (u + 1) * FC)
                for m in range(FC):
                    last = mm(ps[:, 5, t * D:(t + 1) * D], hid[:, m, t * P:(t + 1) * P], w2[:, m, :],
                              start=(m == 0), stop=(m == FC - 1))
                last.then_inc(y_done, 1)

            def body(i):
                loop = not isinstance(i, int)
                now, nxt = loop or i < N, loop or i + 1 < N
                prev, old = loop or 1 <= i <= N, loop or i >= 2
                mlp_old = old and mlp
                for s in range(PAIRS):
                    if s == (1 if tok else 0) and mlp_old:
                        mlp_input_t(i - 2)
                    if now:
                        scores(i, s)
                    if s == 1 and mlp_old:
                        mlp_up(i - 2, range(0 if tok else FC // 2, FC))
                    if s == 2 and now:
                        values(i)
                    if s == 3 and mlp_old:
                        mlp_down(i - 2, 1)
                    if s == 4 and nxt:
                        input_t(i + 1)
                    if s > 0 and now:
                        scores_t(i, s - 1)
                    if s == 0 and prev:
                        scores_t(i - 1, PAIRS - 1)
                    if s < PAIRS - 2 and now:
                        project(i, s + 2)
                    if s == PAIRS - 1 and nxt:
                        project(i + 1, 1)
                    if s == 1 and prev:
                        weighted(i - 1, 2)
                    if s == 4 and prev:
                        output_t(i - 1)
                    if s == 5 and now:
                        weighted(i, 1)
                    if s == 5 and prev and proj:
                        project_out(i - 1)
                    if now:
                        max_rows(i, s)
                    if s == 0 and mlp_old and not tok:
                        mlp_up(i - 2, range(0, FC // 2))
                    if s == 2 and mlp_old:
                        mlp_down(i - 2, 0)
                    if s == 4 and prev and proj:
                        normed_t(i - 1)
                    if s == 4 and nxt:
                        project(i + 1, 0)
                    if s == 4 and now:
                        weighted(i, 0)

            pe.wait_ge(cleared, 1)
            input_t(0)
            project(0, 0)
            project(0, 1)
            turns(pe, N, body)

        @block.scalar
        def _(act):
            go = nc.scalar.activation

            def input_scaled(u):
                if vit:
                    act.wait_ge(ln_loaded, loads_of(u, NL))
                act.wait_ge(xT_done, u + 1)
                wait_from(act, proj_done, u * PAIRS)
                for c, k in KC:
                    src, dst = ps[0:k, 6, c * S:(c + 1) * S], xn[0:k, c, :]
                    if vit:
                        go(dst, src, ACT.Identity, bias=ln1[0:k, c, 1:2], scale=ln1[0:k, c, 0:1]).then_inc(xn_ready, 1)
                    else:
                        go(dst, src, ACT.Copy).then_inc(xn_ready, 1)

            def parts(u, p):
                if p == 0:
                    act.wait_ge(w_loaded, loads_of(u, NA))
                act.wait_ge(proj_done, u * PAIRS + p + 1)
                for i in range(2):
                    last = go(hm[:, i, :], ps[:, 2, i * S:(i + 1) * S], ACT.Identity,
                              bias=bqk_lo[:, i, p:p + 1], scale=maskqk[:, i:i + 1])
                last.then_inc(hm_ready, 1)

            def exps(u, p):
                for a in range(2):
                    hd = 2 * p + a
                    act.wait_ge(st_done, u * H + hd + 1)
                    wait_from(act, pv_done, u * GROUPS + hd // 4 - GROUPS + 1)
                    go(pt[:, hd, :, :].rearrange("p t s -> p (t s)"), ps[:, 3 + a, :], ACT.Exp,
                       scale=SCALE).then_inc(p_ready, 1)

            def out_t(u, g):
                act.wait_ge(pv_done, u * GROUPS + g + 1)
                wait_from(act, ot_done, u)
                go(ot[:, g, :], ps[:, 6, 0:S], ACT.Copy).then_inc(oT_ready, 1)

            def normed(u):
                act.wait_ge(aT_done, u + 1)
                for c, k in KC:
                    go(at[0:k, c, :], ps[0:k, 5, c * S:(c + 1) * S], ACT.Copy).then_inc(aT_ready, 1)

            def mlp_input_scaled(u):
                act.wait_ge(wm_loaded, loads_of(u, NM))
                act.wait_ge(xT2_done, u + 1)
                for c, k in KC:
                    src, dst = ps[0:k, 6, c * S:(c + 1) * S], xn2[0:k, c, :]
                    if vit:
                        go(dst, src, ACT.Identity, bias=ln2[0:k, c, 1:2], scale=ln2[0:k, c, 0:1]).then_inc(xn2_ready, 1)
                    else:
                        go(dst, src, ACT.Copy).then_inc(xn2_ready, 1)

            def hidden(u):
                for m in range(FC):
                    act.wait_ge(h_done, u * FC + m + 1)
                    go(hid[:, m, :], ps[:, 5 + 2 * (m % 2), 0:S], ACT.Relu if tok else ACT.Gelu,
                       bias=b1[:, m:m + 1]).then_inc(h_ready, 1)

            def body(i):
                loop = not isinstance(i, int)
                now, nxt = loop or i < N, loop or i + 1 < N
                prev, old = loop or 1 <= i <= N, loop or i >= 2
                for s in range(PAIRS):
                    if s == 0 and old and vit:
                        mlp_input_scaled(i - 2)
                    if s == 1 and old and tok:
                        mlp_input_scaled(i - 2)
                        hidden(i - 2)
                    if s == 4 and nxt:
                        input_scaled(i + 1)
                    if s > 0 and now:
                        exps(i, s - 1)
                    if s == 0 and prev:
                        exps(i - 1, PAIRS - 1)
                    if s < PAIRS - 2 and now:
                        parts(i, s + 2)
                    if s == PAIRS - 1 and nxt:
                        parts(i + 1, 1)
                    if s == 0 and old and vit:
                        hidden(i - 2)
                    if s == 1 and prev:
                        out_t(i - 1, 2)
                    if s == 4 and prev and proj:
                        normed(i - 1)
                    if s == 4 and nxt:
                        parts(i + 1, 0)
                    if s == 4 and now:
                        out_t(i, 0)
                    if s == 5 and now:
                        out_t(i, 1)

            input_scaled(0)
            parts(0, 0)
            parts(0, 1)
            turns(act, N, body)

        @block.vector
        def _(dve):
            v = nc.vector

            def stats(link, n, src):
                post = n == 2 or (tok and n == 1)
                r = rt[n]
                v.memset(r[:, 5, :], 0.0)
                v.bn_stats(st[:, n, 0, :], src(0))
                link(v.bn_stats(st[:, n, 1, :], src(1)))
                v.memset(r[:, 5, :], 0.0)
                v.bn_aggr(mv[:, n, 0, :], st[:, n, 0, :])
                link(v.bn_aggr(mv[:, n, 1, :], st[:, n, 1, :]))
                if post:
                    link(v.tensor_scalar(r[:, 0, :], mv[:, n, :, 1], 1e-30, None, ALU.max))
                else:
                    link(v.tensor_scalar(r[:, 0, :], mv[:, n, :, 1], 1e-5, None, ALU.add))
                bits = r[:, 1, :].bitcast(I32)
                v.tensor_scalar(r[:, 4, :], r[:, 0, :], -0.5, None, ALU.mult)
                link(v.tensor_scalar(bits, r[:, 0, :].bitcast(I32), 1, None, ALU.logical_shift_right))
                v.tensor_scalar(bits, bits, -1.0, RSQRT_SEED, ALU.mult, ALU.add).then_inc(var_ready[n], 1)

            def normed(n, dst, src, u, link=None):
                dve.wait_ge(root_ready[n], u + 1)
                if link is not None:
                    link(v.reciprocal(rt[n][:, 3, :], rt[n][:, 3, :]))
                for t in range(T):
                    last = v.tensor_scalar(dst[:, t, :], src(t), mv[:, n, t, 0:1], rt[n][:, 3, t:t + 1],
                                           ALU.subtract, ALU.mult)
                return last

            def affine(link, n, dst, src, out, k):
                for t in range(T):
                    last = v.tensor_tensor(dst[:, t, :], src[:, t, :], gb[:, k, :], ALU.mult)
                link(last)
                for t in range(T):
                    last = v.tensor_tensor(out(t), dst[:, t, :], gb[:, k + 1, :], ALU.add)
                return last

            def input_stats(u):
                if not tok:
                    link = chain(dve, ln1_step, u, 4)
                    if vit:
                        dve.wait_ge(x_ready, u + 1)
                    stats(link, 0, lambda t: at_tile(res, u, t))
                    link.finished()

            def input_normed(u):
                wait_from(dve, xT_done, u)
                if tok:
                    v.tensor_scalar(xh[:, :, :], at_unit(res, u), 1.0, None, ALU.mult).then_inc(xhat_ready, 1)
                else:
                    normed(0, xh, lambda t: at_tile(res, u, t), u).then_inc(xhat_ready, 1)

            def values(u):
                if layers > 1:
                    dve.wait_ge(w_loaded, loads_of(u, NA))
                dve.wait_ge(v_done, u + 1)
                wait_from(dve, pv_done, u * GROUPS)
                for t in range(T):
                    last = v.tensor_tensor(va[:, t, :, 0:DH],
                                           ps[:, 6, t * D:(t + 1) * D].rearrange("p (h d) -> p h d", h=H),
                                           bv[:, :].rearrange("p (h d) -> p h d", h=H), ALU.add)
                last.then_inc(v_ready, 1)

            def stack(u, p):
                if p == 0:
                    dve.wait_ge(w_loaded, loads_of(u, NA))
                dve.wait_ge(hm_ready, u * PAIRS + p + 1)
                wait_from(dve, st_done, u * H + 2 * (p - 2))
                for i in range(2):
                    last = v.scalar_tensor_tensor(out=qk[:, p % 3, i, :], in0=ps[:, 2, i * S:(i + 1) * S],
                                                  scalar=bqk[:, i, p:p + 1], in1=hm[:, i, :],
                                                  op0=ALU.add, op1=ALU.subtract)
                last.then_inc(qk_ready, 1)

            def maxima(u, p):
                for a in range(2):
                    dve.wait_ge(s_done, u * H + 2 * p + a + 1)
                    v.tensor_reduce(mx[:, p % 2, a, :], ps[:, a, :].rearrange("p (t s) -> p t s", t=T),
                                    AX.X, ALU.max).then_inc(mx_done, 1)
                dve.wait_ge(mx_done, u * H + 2 * p + 2)
                wait_from(dve, mt_done, u * PAIRS + p - 1)
                m = mx[:, p % 2, :, :].rearrange("p a t -> p t a")
                hi = mb[:, p % 2, :, :].rearrange("p t (a c) -> p t a c", a=2)[:, :, :, MROW]
                lo = mb[:, p % 2, :, :].rearrange("p t (a c) -> p t a c", a=2)[:, :, :, MROW + 1]
                v.tensor_scalar(hi, m, -1.0, None, ALU.mult).then_inc(mb_step, 1)
                dve.wait_ge(mb_step, u * PAIRS + p + 1)
                v.scalar_tensor_tensor(out=lo, in0=m, scalar=-1.0, in1=hi, op0=ALU.mult,
                                       op1=ALU.subtract).then_inc(m_ready, 1)

            def with_max(u, p):
                dve.wait_ge(mt_done, u * PAIRS + p + 1)
                wait_from(dve, st_done, u * H + 2 * (p - 1))
                v.tensor_tensor(q2[:, p % 2, :], ps[:, 0, 0:S], qk[:, p % 3, 0, :], ALU.add).then_inc(q2_ready, 1)

            def output(u):
                link = chain(dve, out_step, u, 1)
                dve.wait_ge(ot_done, u + 1)
                if proj:
                    wait_from(dve, aT_done, u)
                heads = lambda t: ps[:, 5 + 2 * t, 0:GROUPS * P].rearrange("p (h c) -> p h c", h=H)
                for t in range(T):
                    last = v.reciprocal(rcp[:, t, :], heads(t)[:, :, DH])
                link(last)
                for t in range(T):
                    last = v.tensor_tensor(att[:, t, :].rearrange("p (h d) -> p h d", h=H), heads(t)[:, :, 0:DH],
                                           rcp[:, t, :].unsqueeze(2).to_broadcast([P, H, DH]), ALU.mult)
                last.then_inc(att_ready, 1)
                link.finished()

            def output_stats(u):
                link = chain(dve, y_step, u, 4)
                dve.wait_ge(att_added, u + 1)
                stats(link, 1, lambda t: at_tile(x, u, t))
                link.finished()

            def output_normed(u):
                wait_from(dve, xT2_done, u)
                normed(1, xh2, lambda t: at_tile(x, u, t), u).then_inc(xhat2_ready, 1)

            def projected(u):
                link = chain(dve, y_step, u, 1 if l1 else 6)
                dve.wait_ge(op_done, u + 1)
                for t in range(T):
                    last = v.tensor_tensor(r1[:, t, :], ps[:, 7, t * D:(t + 1) * D], bo[:, :], ALU.add)
                link(last)
                if l1:
                    v.tensor_tensor(at_unit(res, u), at_unit(res, u), r1[:, :, :], ALU.add).then_inc(op_read, 1)
                else:
                    link(v.tensor_tensor(r1[:, :, :], at_unit(res, u), r1[:, :, :], ALU.add))
                    stats(link, 1, lambda t: r1[:, t, :])
                link.finished()

            def projected_normed(u):
                link = chain(dve, out2_step, u, 3)
                dve.wait_ge(wm_loaded, NM)
                link(normed(1, xg, lambda t: r1[:, t, :], u, link))
                wait_from(dve, xT2_done, u)
                affine(link, 1, xg, xg, lambda t: xh2[:, t, :], 0).then_inc(xhat2_ready, 1)
                dve.wait_ge(xhat2_ready, u + 1)
                v.tensor_scalar(at_unit(x, u), xh2[:, :, :], 1.0, None, ALU.mult).then_inc(h1_kept, 1)
                link.finished()

            def mlp_out(u):
                if vit:
                    dve.wait_ge(x_ready, u + B)
                dve.wait_ge(y_done, T * (u + 1))
                dve.wait_ge(wm_loaded, loads_of(u, NM))
                for t in range(T):
                    last = v.tensor_tensor(yb[:, t, :], ps[:, 5, t * D:(t + 1) * D], b2[:, :], ALU.add)
                last.then_inc(y_read, 1)
                if tok:
                    dve.wait_ge(y_read, u + 1)
                    link = chain(dve, last_step, u, 5)
                    dve.wait_ge(h1_kept, u + 1)
                    link(v.tensor_tensor(r2[:, :, :], at_unit(x, u), yb[:, :, :], ALU.add))
                    stats(link, 2, lambda t: r2[:, t, :])
                    link.finished()

            def mlp_normed(u):
                link = chain(dve, out3_step, u, 4)
                link(normed(2, r2, lambda t: r2[:, t, :], u, link))
                link(affine(link, 2, r2, r2, lambda t: at_tile(h, u, t), 2))
                link.finished()

            def body(i):
                loop = not isinstance(i, int)
                now, nxt = loop or i < N, loop or i + 1 < N
                prev, old = loop or 1 <= i <= N, loop or i >= 2
                for s in range(PAIRS):
                    if now:
                        maxima(i, s)
                    if s == 4 and prev:
                        output(i - 1)
                    if s == 2 and now:
                        values(i)
                    if now:
                        with_max(i, s)
                    if s == 0 and old and tok:
                        projected_normed(i - 2)
                    if s == 0 and nxt:
                        input_stats(i + 1)
                    if s == 1 and nxt:
                        input_normed(i + 1)
                    if s == 3 and old and mlp:
                        mlp_out(i - 2)
                    if s == 4 and old and tok:
                        mlp_normed(i - 2)
                    if s == 4 and prev and vit:
                        output_stats(i - 1)
                    if s == 5 and prev and vit:
                        output_normed(i - 1)
                    if s == 5 and prev and proj:
                        projected(i - 1)
                    if s < PAIRS - 2 and now:
                        stack(i, s + 2)
                    if s >= PAIRS - 2 and nxt:
                        stack(i + 1, s + 2 - PAIRS)

            v.memset(mb[:, :, :, :].rearrange("p a t c -> p (a t c)").bitcast(F32), 0.0)
            v.memset(va[:, :, :, :].rearrange("p t h c -> p (t h c)"), 0.0).then_inc(zeroed, 1)
            dve.wait_ge(zeroed, 1)
            v.memset(va[:, :, :, DH:DH + 1].rearrange("p t h c -> p (t h) c"), 1.0).then_inc(cleared, 1)
            input_stats(0)
            input_normed(0)
            stack(0, 0)
            stack(0, 1)
            turns(dve, N, body)


def embedding_stage(nc, x, a, cst):
    with ExitStack() as ctx:
        sem = ctx.enter_context(semaphores(nc, "emb"))
        tok_i = ctx.enter_context(nc.sbuf_tensor("emb_tok_i", [P, B * T], I32))
        tok_f = ctx.enter_context(nc.sbuf_tensor("emb_tok_f", [P, B * T], F32))
        neg = ctx.enter_context(nc.sbuf_tensor("emb_neg", [P, B * T], F32))
        idx = ctx.enter_context(nc.sbuf_tensor("emb_idx", [P, B * T], mybir.dt.uint32))
        pos = ctx.enter_context(nc.sbuf_tensor("emb_pos", [P, T, D], F32))
        loaded = sem("loaded")
        const_loaded = sem("const_loaded")
        steps = sem("steps")
        gathered = sem("gathered")
        block = ctx.enter_context(nc.Block())

        @block.sync
        def _(sp):
            sp.dma_start(tok_i[:, :], a["tokens"]).then_inc(loaded, 16)
            sp.dma_start(pos[:, :, :].rearrange("p t d -> p (t d)"), a["pos"]).then_inc(const_loaded, 16)
            sp.dma_start(cst["ident"][:, :], a["ident"]).then_inc(const_loaded, 16)
            sp.dma_start(cst["maskqk"][:, :], a["maskqk"]).then_inc(const_loaded, 16)
            sp.dma_start(cst["blockmask"][:, :], a["blockmask"]).then_inc(const_loaded, 16)
            sp.wait_ge(const_loaded, 64)

        @block.vector
        def _(dve):
            v = nc.vector
            dve.wait_ge(loaded, 16)
            v.tensor_copy(tok_f[:, :], tok_i[:, :]).then_inc(steps, 1)
            dve.wait_ge(steps, 1)
            v.tensor_scalar(neg[:, :], tok_f[:, :], 0.0, float(VOCAB), ALU.is_lt, ALU.mult).then_inc(steps, 1)
            dve.wait_ge(steps, 2)
            v.tensor_tensor(tok_f[:, :], tok_f[:, :], neg[:, :], ALU.add).then_inc(steps, 1)
            dve.wait_ge(steps, 3)
            v.tensor_scalar(idx[:, :], tok_f[:, :], 0.0, float(VOCAB - 1), ALU.max, ALU.min).then_inc(steps, 1)
            dve.wait_ge(const_loaded, 64)
            v.tensor_copy(cst["identr"][:, :], cst["ident"][:, :])
            dve.wait_ge(gathered, 16 * T * B)
            for b in range(B):
                v.tensor_tensor(x[:, b * T:(b + 1) * T, :], x[:, b * T:(b + 1) * T, :], pos[:, :, :], ALU.add)

        @block.gpsimd
        def _(pool):
            nc.gpsimd.memset(cst["newton"][:, 0, :], 1.5)
            nc.gpsimd.memset(cst["newton"][:, 1, :], 1e-5)
            pool.wait_ge(steps, 4)
            for n in range(B * T):
                pool.indirect_dma_start(out=x[:, n, :], out_offset=None, in_=a["emb"],
                                        in_offset=bass.IndirectOffsetOnAxis(ap=idx[:, n:n + 1], axis=0)
                                        ).then_inc(gathered, 16)
            pool.wait_ge(gathered, 16 * B * T)


def glue_stage(nc, name, h, x, cst, add):
    with ExitStack() as ctx:
        sem = ctx.enter_context(semaphores(nc, name))
        r = ctx.enter_context(nc.sbuf_tensor(f"{name}_r", [P, T, D], F32))
        st = ctx.enter_context(nc.sbuf_tensor(f"{name}_st", [P, T, 6], F32))
        mv = ctx.enter_context(nc.sbuf_tensor(f"{name}_mv", [P, T, 2], F32))
        rt = ctx.enter_context(nc.sbuf_tensor(f"{name}_rt", [P, 6, T], F32))
        steps = sem("steps")
        pool_steps = sem("pool_steps")
        var_ready = sem("var_ready")
        root_ready = sem("root_ready")
        block = ctx.enter_context(nc.Block())

        @block.gpsimd
        def _(pool):
            half3, eps = cst["newton"][:, 0, :], cst["newton"][:, 1, :]
            with pool.Fori(0, B) as b:
                link = chain(pool, pool_steps, b, root_steps(False))
                root(nc, pool, link, rt, half3, eps, var_ready, root_ready, b + 1, False)
                link.finished()

        @block.vector
        def _(dve):
            v = nc.vector
            with dve.Fori(0, B) as b:
                link = chain(dve, steps, b, 7)
                ht, xt = h[:, bass.ds(b * T, T), :], x[:, bass.ds(b * T, T), :]
                if add:
                    link(v.tensor_tensor(r[:, :, :], ht, xt, ALU.add))
                else:
                    link(v.tensor_scalar(r[:, :, :], ht, 1.0, None, ALU.mult))
                norm_stats(nc, dve, link, r, st, mv, rt, var_ready, root_ready, b + 1)
                for t in range(T):
                    last = v.tensor_scalar(x[:, bass.ds(b * T + t, 1), :].rearrange("p a d -> p (a d)"), r[:, t, :],
                                           mv[:, t, 0:1], rt[:, 3, t:t + 1], ALU.subtract, ALU.mult)
                link(last)
                if add:
                    last = v.tensor_scalar(ht, r[:, :, :], 1.0, None, ALU.mult)
                else:
                    last = v.memset(rt[:, 5, :], 0.0)
                link(last)
                link.finished()


def channel_attention_stage(nc, x, wd, cst, scratch):
    with ExitStack() as ctx:
        def sb(n, shape, dt=F32):
            return ctx.enter_context(nc.sbuf_tensor(f"ca_{n}", shape, dt))

        sem = ctx.enter_context(semaphores(nc, "ca"))

        ps = ctx.enter_context(nc.psum_tensor("ca_ps", [P, 8, 512], F32))
        w = sb("w", [P, 2, 3 * D])
        bqk = sb("bqk", [P, 2 * D])
        bv = sb("bv", [P, 2])
        xh, xn = sb("xh", [P, T, D]), sb("xn", [P, 2, S])
        qk = sb("qk", [P, T, 2 * D])
        vt = sb("vt", [P, 2, S])
        gm, ex, wt = sb("gm", [P, 2, P]), sb("ex", [P, 2, P]), sb("wt", [P, 2, P])
        mx, sm = sb("mx", [P, 2]), sb("sm", [P, 2])
        osb = sb("osb", [P, 2, S])
        loaded, dch = sem("weights_loaded"), sem("vector_chain")
        xhat_ready, xT_done, xn_ready = sem("xhat_ready"), sem("xT_done"), sem("xn_ready")
        qk_done, v_done, qk_ready, vt_ready = sem("qk_done"), sem("v_done"), sem("qk_ready"), sem("vt_ready")
        gram_done, logit_ready, e_ready, w_ready = sem("gram_done"), sem("logit_ready"), sem("e_ready"), sem("w_ready")
        wT_done, wT_ready, o_done, o_ready = sem("wT_done"), sem("wT_ready"), sem("o_done"), sem("o_ready")
        stored = sem("stored")
        block = ctx.enter_context(nc.Block())
        ident, bmask = cst["ident"], cst["blockmask"]

        @block.sync
        def _(sp):
            sp.dma_start(w[:, :, :].rearrange("p c n -> p (c n)"), wd["w1"]).then_inc(loaded, 16)
            sp.dma_start(bqk[:, :], wd["bqk"]).then_inc(loaded, 16)
            sp.dma_start(bv[:, :], wd["bv"]).then_inc(loaded, 16)
            with sp.Fori(0, B) as b:
                sp.wait_ge(o_ready, 2 * b + 2)
                for c, k in KC:
                    dst = scratch[bass.ds(b, 1), c * P:c * P + k, :].rearrange("a c n -> (a c) n")
                    sp.dma_start(dst, osb[0:k, c, :]).then_inc(stored, 16)
            sp.wait_ge(stored, 32 * B)
            sp.wait_ge(loaded, 48)

        @block.tensor
        def _(pe):
            mm, tr = nc.tensor.matmul, nc.tensor.transpose
            pe.wait_ge(loaded, 48)
            with pe.Fori(0, B) as b:
                pe.wait_ge(xhat_ready, b + 1)
                for t in range(T):
                    for c, k in KC:
                        last = tr(ps[0:k, 7, c * S + t * P:c * S + (t + 1) * P], xh[:, t, c * P:c * P + k], ident[:, :])
                last.then_inc(xT_done, 1)
                pe.wait_ge(xn_ready, 2 * b + 2)
                for t in range(T):
                    for c, k in KC:
                        last = mm(ps[:, t, 0:2 * D], xn[0:k, c, t * P:(t + 1) * P], w[0:k, c, 0:2 * D],
                                  start=(c == 0), stop=(c == 1))
                last.then_inc(qk_done, 1)
                for o, n in KC:
                    for c, k in KC:
                        last = mm(ps[0:n, 2 + o, 0:S], w[0:k, c, 2 * D + o * P:2 * D + o * P + n], xn[0:k, c, :],
                                  start=(c == 0), stop=(c == 1))
                last.then_inc(v_done, 1)
                pe.wait_ge(qk_ready, b + 1)
                for c, k in KC:
                    for t in range(T):
                        last = mm(ps[0:k, 4 + c, 0:k], qk[:, t, c * P:c * P + k], qk[:, t, D + c * P:D + c * P + k],
                                  start=(t == 0), stop=(t == 1))
                last.then_inc(gram_done, 1)
                pe.wait_ge(w_ready, b + 1)
                for c, k in KC:
                    last = tr(ps[0:k, 6, c * P:c * P + k], ex[0:k, c, 0:k], ident[0:k, 0:k])
                last.then_inc(wT_done, 1)
                pe.wait_ge(wT_ready, 2 * b + 2)
                pe.wait_ge(vt_ready, 2 * b + 2)
                for c, k in KC:
                    last = mm(ps[0:k, c, 0:S], wt[0:k, c, 0:k], vt[0:k, c, :], start=True, stop=True)
                last.then_inc(o_done, 1)

        @block.scalar
        def _(act):
            go = nc.scalar.activation
            act.wait_ge(loaded, 48)
            with act.Fori(0, B) as b:
                act.wait_ge(xT_done, b + 1)
                for c, k in KC:
                    go(xn[0:k, c, :], ps[0:k, 7, c * S:(c + 1) * S], ACT.Copy).then_inc(xn_ready, 1)
                act.wait_ge(v_done, b + 1)
                for c, k in KC:
                    go(vt[0:k, c, :], ps[0:k, 2 + c, 0:S], ACT.Identity, bias=bv[0:k, c:c + 1]).then_inc(vt_ready, 1)
                act.wait_ge(logit_ready, b + 1)
                for c, k in KC:
                    go(ex[0:k, c, 0:k], gm[0:k, c, 0:k], ACT.Exp, bias=mx[0:k, c:c + 1],
                       accum_out=sm[0:k, c:c + 1]).then_inc(e_ready, 1)
                act.wait_ge(wT_done, b + 1)
                for c, k in KC:
                    go(wt[0:k, c, 0:k], ps[0:k, 6, c * P:c * P + k], ACT.Copy).then_inc(wT_ready, 1)
                act.wait_ge(o_done, b + 1)
                for c, k in KC:
                    go(osb[0:k, c, :], ps[0:k, c, 0:S], ACT.Copy).then_inc(o_ready, 1)
                act.wait_ge(stored, 32 * (b + 1))

        @block.vector
        def _(dve):
            v = nc.vector
            dve.wait_ge(loaded, 48)
            with dve.Fori(0, B) as b:
                link = chain(dve, dch, b, 3)
                v.tensor_copy(xh[:, :, :], x[:, bass.ds(b * T, T), :]).then_inc(xhat_ready, 1)
                dve.wait_ge(qk_done, b + 1)
                for t in range(T):
                    last = v.tensor_tensor(qk[:, t, :], ps[:, t, 0:2 * D], bqk[:, :], ALU.add)
                last.then_inc(qk_ready, 1)
                dve.wait_ge(gram_done, b + 1)
                for c, k in KC:
                    last = v.scalar_tensor_tensor(out=gm[0:k, c, 0:k], in0=ps[0:k, 4 + c, 0:k], scalar=1.0 / 16,
                                                  in1=bmask[0:k, 0:k], op0=ALU.mult, op1=ALU.add)
                link(last)
                for c, k in KC:
                    last = v.tensor_reduce(mx[0:k, c:c + 1], gm[0:k, c, 0:k], AX.X, ALU.max)
                link(last)
                for c, k in KC:
                    last = v.tensor_scalar(mx[0:k, c:c + 1], mx[0:k, c:c + 1], -1.0, None, ALU.mult)
                last.then_inc(logit_ready, 1)
                dve.wait_ge(e_ready, 2 * b + 2)
                for c, k in KC:
                    last = v.reciprocal(sm[0:k, c:c + 1], sm[0:k, c:c + 1])
                link(last)
                for c, k in KC:
                    last = v.tensor_scalar(ex[0:k, c, 0:k], ex[0:k, c, 0:k], sm[0:k, c:c + 1], None, ALU.mult)
                last.then_inc(w_ready, 1)
                link.finished()


def channel_projection_stage(nc, x, wd, cst, scratch):
    with ExitStack() as ctx:
        def sb(n, shape, dt=F32):
            return ctx.enter_context(nc.sbuf_tensor(f"cp_{n}", shape, dt))

        sem = ctx.enter_context(semaphores(nc, "cp"))

        ps = ctx.enter_context(nc.psum_tensor("cp_ps", [P, 8, 512], F32))
        a2 = sb("a2", [P, B * T, D])
        w, bo = sb("w", [P, 2, D]), sb("bo", [P, D])
        xh, xn, r = sb("xh", [P, T, D]), sb("xn", [P, 2, S]), sb("r", [P, T, D])
        loaded, dch = sem("loaded"), sem("vector_chain")
        xhat_ready, xT_done, xn_ready = sem("xhat_ready"), sem("xT_done"), sem("xn_ready")
        op_done, x_ready = sem("op_done"), sem("x_ready")
        block = ctx.enter_context(nc.Block())
        ident = cst["ident"]

        @block.sync
        def _(sp):
            sp.dma_start(w[:, :, :].rearrange("p c n -> p (c n)"), wd["w2"]).then_inc(loaded, 16)
            sp.dma_start(bo[:, :], wd["b2"]).then_inc(loaded, 16)
            flat = scratch.rearrange("b c n -> b (c n)").rearrange("b (t p d) -> p (b t) d", t=T, p=P)
            sp.dma_start(a2[:, :, :], flat).then_inc(loaded, 16)
            sp.wait_ge(loaded, 48)

        @block.tensor
        def _(pe):
            mm, tr = nc.tensor.matmul, nc.tensor.transpose
            pe.wait_ge(loaded, 48)
            with pe.Fori(0, B) as b:
                pe.wait_ge(xhat_ready, b + 1)
                for t in range(T):
                    for c, k in KC:
                        last = tr(ps[0:k, 7, c * S + t * P:c * S + (t + 1) * P], xh[:, t, c * P:c * P + k], ident[:, :])
                last.then_inc(xT_done, 1)
                pe.wait_ge(xn_ready, 2 * b + 2)
                for t in range(T):
                    for c, k in KC:
                        last = mm(ps[:, 1, t * D:(t + 1) * D], xn[0:k, c, t * P:(t + 1) * P], w[0:k, c, :],
                                  start=(c == 0), stop=(c == 1))
                last.then_inc(op_done, 1)

        @block.scalar
        def _(act):
            with act.Fori(0, B) as b:
                act.wait_ge(xT_done, b + 1)
                for c, k in KC:
                    nc.scalar.activation(xn[0:k, c, :], ps[0:k, 7, c * S:(c + 1) * S], ACT.Copy).then_inc(xn_ready, 1)

        @block.vector
        def _(dve):
            v = nc.vector
            dve.wait_ge(loaded, 48)
            with dve.Fori(0, B) as b:
                link = chain(dve, dch, b, 1)
                v.tensor_copy(xh[:, :, :], a2[:, bass.ds(b * T, T), :]).then_inc(xhat_ready, 1)
                dve.wait_ge(op_done, b + 1)
                for t in range(T):
                    last = v.tensor_tensor(r[:, t, :], ps[:, 1, t * D:(t + 1) * D], bo[:, :], ALU.add)
                link(last)
                xt = x[:, bass.ds(b * T, T), :]
                v.tensor_tensor(xt, xt, r[:, :, :], ALU.add).then_inc(x_ready, 1)
                dve.wait_ge(x_ready, b + 1)
                link.finished()


def global_norm_stage(nc, name, x, h, wd, cst):
    N = B * S * D
    with ExitStack() as ctx:
        def sb(n, shape, dt=F32):
            return ctx.enter_context(nc.sbuf_tensor(f"{name}_{n}", shape, dt))

        sem = ctx.enter_context(semaphores(nc, name))

        ps = ctx.enter_context(nc.psum_tensor(f"{name}_ps", [P, 2, 512], F32))
        wb = sb("wb", [P, 2, D])
        ones = sb("ones", [P, P])
        part, stat = sb("part", [P, 2]), sb("stat", [P, 2])
        tsum = sb("tsum", [P, B * T])
        sq = sb("sq", [P, B * T * D])
        rt = sb("rt", [P, 6, T])
        loaded, dch, pch = sem("loaded"), sem("vector_chain"), sem("pool_chain")
        ones_ready, sum_ready, sum_all, centred = sem("ones_ready"), sem("sum_ready"), sem("sum_all"), sem("centred")
        sq_ready, sq_all, var_ready, root_ready = sem("sq_ready"), sem("sq_all"), sem("var_ready"), sem("root_ready")
        block = ctx.enter_context(nc.Block())
        flat = x[:, :, :].rearrange("p a d -> p (a d)")

        @block.sync
        def _(sp):
            sp.dma_start(wb[:, :, :].rearrange("p a d -> p (a d)"), wd).then_inc(loaded, 16)
            sp.wait_ge(loaded, 16)

        @block.tensor
        def _(pe):
            pe.wait_ge(ones_ready, 1)
            pe.wait_ge(sum_ready, 1)
            nc.tensor.matmul(ps[:, 0, 0:1], ones[:, :], part[:, 0:1], start=True, stop=True).then_inc(sum_all, 1)
            pe.wait_ge(sq_ready, 1)
            nc.tensor.matmul(ps[:, 1, 0:1], ones[:, :], part[:, 1:2], start=True, stop=True).then_inc(sq_all, 1)

        @block.scalar
        def _(act):
            act.wait_ge(centred, 1)
            nc.scalar.activation(sq[:, :], flat, ACT.Square, accum_out=part[:, 1:2]).then_inc(sq_ready, 1)

        @block.gpsimd
        def _(pool):
            nc.gpsimd.memset(ones[:, :], 1.0).then_inc(ones_ready, 1)
            half3, eps = cst["newton"][:, 0, :], cst["newton"][:, 1, :]
            link = chain(pool, pch, 0, root_steps(False))
            root(nc, pool, link, rt, half3, eps, var_ready, root_ready, 1, False)
            link.finished()

        @block.vector
        def _(dve):
            v = nc.vector
            link = chain(dve, dch, 0, 7 + (1 if h is not None else 0))
            link(v.tensor_reduce(tsum[:, :], x[:, :, :], AX.X, ALU.add))
            v.tensor_reduce(part[:, 0:1], tsum[:, :], AX.X, ALU.add).then_inc(sum_ready, 1)
            dve.wait_ge(sum_all, 1)
            link(v.tensor_scalar(stat[:, 0:1], ps[:, 0, 0:1], 1.0 / N, None, ALU.mult))
            v.tensor_scalar(flat, flat, stat[:, 0:1], None, ALU.subtract).then_inc(centred, 1)
            dve.wait_ge(centred, 1)
            dve.wait_ge(sq_all, 1)
            for t in range(T):
                last = v.tensor_scalar(rt[:, 0, t:t + 1], ps[:, 1, 0:1], 1.0 / (N - 1), 1e-12, ALU.mult, ALU.add)
            link(last)
            bits = rt[:, 1, :].bitcast(I32)
            v.tensor_scalar(rt[:, 4, :], rt[:, 0, :], -0.5, None, ALU.mult)
            link(v.tensor_scalar(bits, rt[:, 0, :].bitcast(I32), 1, None, ALU.logical_shift_right))
            v.tensor_scalar(bits, bits, -1.0, RSQRT_SEED, ALU.mult, ALU.add).then_inc(var_ready, 1)
            dve.wait_ge(root_ready, 1)
            link(v.tensor_scalar(flat, flat, rt[:, 3, 0:1], None, ALU.mult))
            dve.wait_ge(loaded, 16)
            every = lambda n: wb[:, n:n + 1, :].to_broadcast([P, B * T, D])
            link(v.tensor_tensor(x[:, :, :], x[:, :, :], every(0), ALU.mult))
            link(v.tensor_tensor(x[:, :, :], x[:, :, :], every(1), ALU.add))
            if h is not None:
                link(v.tensor_tensor(h[:, :, :], h[:, :, :], x[:, :, :], ALU.add))
            link.finished()


def gate_stage(nc, x, wd, cst, vals, picks):
    E = MOE_E
    with ExitStack() as ctx:
        def sb(n, shape, dt=F32):
            return ctx.enter_context(nc.sbuf_tensor(f"gate_{n}", shape, dt))

        sem = ctx.enter_context(semaphores(nc, "gate"))

        ps = ctx.enter_context(nc.psum_tensor("gate_ps", [P, 8, 512], F32))
        rw, rb, iota = sb("rw", [P, 2, E]), sb("rb", [P, E]), sb("iota", [P, E])
        ones = sb("ones", [P, P])
        xh, xn = sb("xh", [P, T, D]), sb("xn", [P, 2, S])
        sc, z = sb("sc", [P, T, E]), sb("z", [P, B, E])
        m, g, eq, cand = sb("m", [P, B]), sb("g", [P, B, E]), sb("eq", [P, B, E]), sb("cand", [P, B, E])
        pf = sb("pf", [P, TOP_K, B])
        loaded, dch = sem("loaded"), sem("vector_chain")
        ones_ready, xhat_ready, xT_done, xn_ready = sem("ones_ready"), sem("xhat_ready"), sem("xT_done"), sem("xn_ready")
        sc_done, sc_ready, mean_done, z_ready = sem("sc_done"), sem("sc_ready"), sem("mean_done"), sem("z_ready")
        logits_ready, exp_ready = sem("logits_ready"), sem("exp_ready")
        block = ctx.enter_context(nc.Block())
        ident = cst["ident"]

        @block.sync
        def _(sp):
            sp.dma_start(rw[:, :, :].rearrange("p c e -> p (c e)"), wd["rw"]).then_inc(loaded, 16)
            sp.dma_start(rb[:, :], wd["rb"]).then_inc(loaded, 16)
            sp.dma_start(iota[:, :], wd["iota"]).then_inc(loaded, 16)
            sp.wait_ge(loaded, 48)

        @block.gpsimd
        def _(pool):
            nc.gpsimd.memset(ones[:, :], 1.0).then_inc(ones_ready, 1)

        @block.tensor
        def _(pe):
            mm, tr = nc.tensor.matmul, nc.tensor.transpose
            pe.wait_ge(loaded, 48)
            pe.wait_ge(ones_ready, 1)
            with pe.Fori(0, B) as b:
                pe.wait_ge(xhat_ready, b + 1)
                for t in range(T):
                    for c, k in KC:
                        last = tr(ps[0:k, 7, c * S + t * P:c * S + (t + 1) * P], xh[:, t, c * P:c * P + k], ident[:, :])
                last.then_inc(xT_done, 1)
                pe.wait_ge(xn_ready, 2 * b + 2)
                for t in range(T):
                    for c, k in KC:
                        last = mm(ps[:, 0, t * E:(t + 1) * E], xn[0:k, c, t * P:(t + 1) * P], rw[0:k, c, :],
                                  start=(c == 0), stop=(c == 1))
                last.then_inc(sc_done, 1)
                pe.wait_ge(sc_ready, b + 1)
                for t in range(T):
                    last = mm(ps[:, 1, 0:E], ones[:, :], sc[:, t, :], start=(t == 0), stop=(t == 1))
                last.then_inc(mean_done, 1)

        @block.scalar
        def _(act):
            with act.Fori(0, B) as b:
                act.wait_ge(xT_done, b + 1)
                for c, k in KC:
                    nc.scalar.activation(xn[0:k, c, :], ps[0:k, 7, c * S:(c + 1) * S], ACT.Copy).then_inc(xn_ready, 1)
            act.wait_ge(logits_ready, 1)
            nc.scalar.activation(g[:, :, :].rearrange("p b e -> p (b e)"), z[:, :, :].rearrange("p b e -> p (b e)"),
                                 ACT.Exp).then_inc(exp_ready, 1)

        @block.vector
        def _(dve):
            v = nc.vector
            dve.wait_ge(loaded, 48)
            with dve.Fori(0, B) as b:
                v.tensor_copy(xh[:, :, :], x[:, bass.ds(b * T, T), :]).then_inc(xhat_ready, 1)
                dve.wait_ge(sc_done, b + 1)
                v.tensor_copy(sc[:, :, :].rearrange("p t e -> p (t e)"), ps[:, 0, 0:T * E]).then_inc(sc_ready, 1)
                dve.wait_ge(mean_done, b + 1)
                v.scalar_tensor_tensor(out=z[:, bass.ds(b, 1), :].rearrange("p a e -> p (a e)"), in0=ps[:, 1, 0:E],
                                       scalar=1.0 / S, in1=rb[:, :], op0=ALU.mult, op1=ALU.add).then_inc(z_ready, 1)
                dve.wait_ge(z_ready, b + 1)
            link = chain(dve, dch, 0, 14)
            over = lambda a: a.unsqueeze(2).to_broadcast([P, B, E])
            io = iota[:, :].unsqueeze(1).to_broadcast([P, B, E])
            link(v.tensor_reduce(m[:, :], z[:, :, :], AX.X, ALU.max))
            v.tensor_tensor(z[:, :, :], z[:, :, :], over(m[:, :]), ALU.subtract).then_inc(logits_ready, 1)
            dve.wait_ge(exp_ready, 1)
            link(v.tensor_reduce(m[:, :], g[:, :, :], AX.X, ALU.add))
            link(v.reciprocal(m[:, :], m[:, :]))
            link(v.tensor_tensor(g[:, :, :], g[:, :, :], over(m[:, :]), ALU.mult))
            for k in range(TOP_K):
                link(v.tensor_reduce(vals[:, k, :], g[:, :, :], AX.X, ALU.max))
                link(v.tensor_tensor(eq[:, :, :], g[:, :, :], over(vals[:, k, :]), ALU.is_ge))
                link(v.scalar_tensor_tensor(out=cand[:, :, :], in0=eq[:, :, :], scalar=-float(E), in1=io,
                                            op0=ALU.mult, op1=ALU.add))
                link(v.tensor_reduce(pf[:, k, :], cand[:, :, :], AX.X, ALU.min))
                if k == 0:
                    link(v.tensor_tensor(eq[:, :, :], cand[:, :, :], over(pf[:, k, :]), ALU.is_equal))
                    link(v.scalar_tensor_tensor(out=g[:, :, :], in0=eq[:, :, :], scalar=-2.0, in1=g[:, :, :],
                                                op0=ALU.mult, op1=ALU.add))
            v.tensor_scalar(picks[:, :, :], pf[:, :, :].rearrange("p k b -> p b k"), float(E), None, ALU.add)
            link.finished()


def expert_stage(nc, name, x, dst, n, func, wd, cst, moe):
    with ExitStack() as ctx:
        def sb(nm, shape, dt=F32):
            return ctx.enter_context(nc.sbuf_tensor(f"{name}_{nm}", shape, dt))

        sem = ctx.enter_context(semaphores(nc, name))

        ps = ctx.enter_context(nc.psum_tensor(f"{name}_ps", [P, 8, 512], F32))
        w1, w2 = sb("w1", [P, n, 2 * F]), sb("w2", [P, n, FC * D])
        b1, b2 = sb("b1", [P, n, FC]), sb("b2", [P, n, D])
        xh, xn = sb("xh", [P, T, D]), sb("xn", [P, 2, S])
        hid = sb("hid", [P, 2, FC, S])
        yb = sb("yb", [P, T, D])
        wg, bg, iota = sb("wg", [P, 2, n]), sb("bg", [P, n]), sb("iota", [P, MOE_E])
        lg, eq, m, hot = sb("lg", [P, T, n]), sb("eq", [P, T, n]), sb("m", [P, T]), sb("hot", [P, T, n])
        loaded = [sem(f"loaded{j}") for j in range(n)]
        gate_loaded, dch = sem("gate_loaded"), sem("vector_chain")
        xhat_ready, xT_done, xn_ready = sem("xhat_ready"), sem("xT_done"), sem("xn_ready")
        lg_done, h_done, h_ready = sem("lg_done"), sem("h_done"), sem("h_ready")
        y_done, acc_ready = sem("y_done"), sem("acc_ready")
        block = ctx.enter_context(nc.Block())
        ident = cst["ident"]
        LOADS = 64

        def wait_weights(eng, j, b):
            eng.wait_ge(loaded[j], (b + 1) * LOADS if moe else LOADS)

        @block.sync
        def _(sp):
            def fetch(j, e):
                for d, s in ((w1, wd["w1"]), (w2, wd["w2"]), (b1, wd["b1"]), (b2, wd["b2"])):
                    sp.dma_start(d[:, j, :], s[bass.ds(e, 1)].rearrange("a p n -> (a p) n")).then_inc(loaded[j], 16)

            if moe:
                def pick(b, j):
                    fetch(j, sp.value_load(moe[1][0:1, bass.ds(b, 1), j:j + 1].rearrange("p a k -> p (a k)"),
                                           min_val=0, max_val=MOE_E - 1))

                for j in range(n):
                    pick(0, j)
                with sp.Fori(1, B) as b:
                    for j in range(n):
                        sp.wait_ge(acc_ready, n * (b - 1) + j + 1)
                        pick(b, j)
            else:
                for d, s in ((wg[:, :, :].rearrange("p c e -> p (c e)"), wd["wg"]), (bg[:, :], wd["bg"]),
                             (iota[:, :], wd["iota"])):
                    sp.dma_start(d, s).then_inc(gate_loaded, 16)
                for j in range(n):
                    fetch(j, j)
                sp.wait_ge(gate_loaded, 48)
            for j in range(n):
                sp.wait_ge(loaded[j], LOADS * (B if moe else 1))

        @block.tensor
        def _(pe):
            mm, tr = nc.tensor.matmul, nc.tensor.transpose
            if not moe:
                pe.wait_ge(gate_loaded, 48)
            with pe.Fori(0, B) as b:
                pe.wait_ge(xhat_ready, b + 1)
                for t in range(T):
                    for c, k in KC:
                        last = tr(ps[0:k, 7, c * S + t * P:c * S + (t + 1) * P], xh[:, t, c * P:c * P + k], ident[:, :])
                last.then_inc(xT_done, 1)
                pe.wait_ge(xn_ready, 2 * b + 2)
                if not moe:
                    for t in range(T):
                        for c, k in KC:
                            last = mm(ps[:, 6, t * n:(t + 1) * n], xn[0:k, c, t * P:(t + 1) * P], wg[0:k, c, :],
                                      start=(c == 0), stop=(c == 1))
                    last.then_inc(lg_done, 1)

                def up(j):
                    wait_weights(pe, j, b)
                    w = w1[:, j, :].rearrange("p (c f) -> p c f", c=2)
                    for q in range(FC):
                        i = j * FC + q
                        if i >= 2:
                            pe.wait_ge(h_ready, b * n * FC + i - 1)
                        for c, k in KC:
                            last = mm(ps[:, q % 2, 0:S], w[0:k, c, q * P:(q + 1) * P], xn[0:k, c, :],
                                      start=(c == 0), stop=(c == 1))
                        last.then_inc(h_done, 1)

                def down(j):
                    if j >= 2:
                        pe.wait_ge(acc_ready, b * n + j - 1)
                    w = w2[:, j, :].rearrange("p (q d) -> p q d", q=FC)
                    for t in range(T):
                        for q in range(FC):
                            if t == 0:
                                pe.wait_ge(h_ready, b * n * FC + j * FC + q + 1)
                            last = mm(ps[:, 2 + 2 * (j % 2) + t, 0:D], hid[:, j % 2, q, t * P:(t + 1) * P], w[:, q, :],
                                      start=(q == 0), stop=(q == FC - 1))
                    last.then_inc(y_done, 1)

                up(0)
                for j in range(n):
                    if j + 1 < n:
                        up(j + 1)
                    down(j)

        @block.scalar
        def _(act):
            go = nc.scalar.activation
            with act.Fori(0, B) as b:
                act.wait_ge(xT_done, b + 1)
                for c, k in KC:
                    go(xn[0:k, c, :], ps[0:k, 7, c * S:(c + 1) * S], ACT.Copy).then_inc(xn_ready, 1)
                for j in range(n):
                    wait_weights(act, j, b)
                    if j >= 2:
                        act.wait_ge(y_done, b * n + j - 1)
                    for q in range(FC):
                        act.wait_ge(h_done, b * n * FC + j * FC + q + 1)
                        go(hid[:, j % 2, q, :], ps[:, q % 2, 0:S], func, bias=b1[:, j, q:q + 1]).then_inc(h_ready, 1)

        @block.vector
        def _(dve):
            v = nc.vector
            if not moe:
                dve.wait_ge(gate_loaded, 48)
            with dve.Fori(0, B) as b:
                link = chain(dve, dch, b, n + (0 if moe else 5))
                v.tensor_copy(xh[:, :, :], x[:, bass.ds(b * T, T), :]).then_inc(xhat_ready, 1)
                if not moe:
                    dve.wait_ge(lg_done, b + 1)
                    over = lambda a: a.unsqueeze(2).to_broadcast([P, T, n])
                    bgt = bg[:, :].unsqueeze(1).to_broadcast([P, T, n])
                    io = iota[:, 0:n].unsqueeze(1).to_broadcast([P, T, n])
                    link(v.tensor_tensor(lg[:, :, :], ps[:, 6, 0:T * n].rearrange("p (t e) -> p t e", t=T), bgt,
                                         ALU.add))
                    link(v.tensor_reduce(m[:, :], lg[:, :, :], AX.X, ALU.max))
                    link(v.tensor_tensor(eq[:, :, :], lg[:, :, :], over(m[:, :]), ALU.is_ge))
                    link(v.scalar_tensor_tensor(out=lg[:, :, :], in0=eq[:, :, :], scalar=-8.0, in1=io, op0=ALU.mult,
                                                op1=ALU.add))
                    link(v.tensor_reduce(m[:, :], lg[:, :, :], AX.X, ALU.min))
                    v.tensor_tensor(hot[:, :, :], lg[:, :, :], over(m[:, :]), ALU.is_equal)
                for j in range(n):
                    dve.wait_ge(y_done, b * n + j + 1)
                    wait_weights(dve, j, b)
                    for t in range(T):
                        last = v.tensor_tensor(yb[:, t, :], ps[:, 2 + 2 * (j % 2) + t, 0:D], b2[:, j, :], ALU.add)
                    link(last)
                    for t in range(T):
                        dt = dst[:, bass.ds(b * T + t, 1), :].rearrange("p a d -> p (a d)")
                        co = (moe[0][:, j, bass.ds(b, 1)] if moe else hot[:, t, j:j + 1])
                        last = v.scalar_tensor_tensor(out=dt, in0=yb[:, t, :], scalar=co, in1=dt, op0=ALU.mult,
                                                      op1=ALU.add)
                    last.then_inc(acc_ready, 1)
                    dve.wait_ge(acc_ready, b * n + j + 1)
                link.finished()


def store_stage(nc, h, out):
    with nc.semaphore("out_stored") as stored, nc.Block() as block:
        @block.sync
        def _(sp):
            dst = out.rearrange("b s d -> (b s) d").rearrange("(n p) d -> p n d", p=P)
            sp.dma_start(dst, h[:, :, :]).then_inc(stored, 16)
            sp.wait_ge(stored, 16)


def lm_tower(nc, a, out, upto="all"):
    part = lambda prefix: {k[len(prefix):]: v for k, v in a.items() if k.startswith(prefix)}
    with ExitStack() as ctx:
        def sb(n, shape, dt=F32):
            return ctx.enter_context(nc.sbuf_tensor(n, shape, dt))

        h = sb("h_stream", [P, B * T, D])
        x = sb("x_stream", [P, B * T, D])
        vals, picks = sb("vals", [P, TOP_K, B]), sb("picks", [P, B, TOP_K], I32)
        cst = {"ident": sb("ident", [P, P]), "identr": sb("identr", [P, P], F32R), "maskqk": sb("maskqk", [P, 2]),
               "blockmask": sb("blockmask", [P, P]), "newton": sb("newton", [P, 2, T])}
        scratch = nc.dram_tensor("channel_attention", [B, D, S], F32, kind="Internal").ap()
        embedding_stage(nc, x, a, cst)
        attention_stage(nc, "tok", "tok", h, x, part("tok_"), cst)
        glue_stage(nc, "to_vit", h, x, cst, False)
        attention_stage(nc, "vit", "vit", h, x, part("vit_"), cst)
        glue_stage(nc, "to_ffn", h, x, cst, True)
        if upto != "h2":
            f = part("ffn_")
            channel_attention_stage(nc, x, f, cst, scratch)
            channel_projection_stage(nc, x, f, cst, scratch)
            global_norm_stage(nc, "gn1", x, None, f["ln1"], cst)
            gate_stage(nc, x, f, cst, vals, picks)
            expert_stage(nc, "moe", x, x, TOP_K, ACT.Gelu_apprx_tanh, part("moe_"), cst, (vals, picks))
            global_norm_stage(nc, "gn2", x, h, f["ln2"], cst)
            if upto != "h3":
                attention_stage(nc, "l1", "l1", h, x, part("l1_"), cst)
                glue_stage(nc, "to_experts", h, x, cst, False)
                expert_stage(nc, "ex", x, h, L1_E, ACT.Gelu, part("ex_"), cst, None)
        store_stage(nc, h, out)


def positions():
    f = np.float32
    pos = np.arange(S, dtype=f)[:, None]
    i = np.arange(D, dtype=f)[None, :]
    ang = (pos / np.power(f(10000.0), (f(2.0) * i / f(D)).astype(f)).astype(f)).astype(f)
    tab = np.where(np.arange(D)[None, :] % 2 == 0, np.cos(ang), np.sin(ang)).astype(f)
    return np.ascontiguousarray(tab.reshape(T, P, D).transpose(1, 0, 2).reshape(P, T * D))


def rows(w):
    lead, n = w.shape[:-2], w.shape[-1]
    out = np.zeros(lead + (P, 2, n), np.float32)
    out[..., :, 0, :] = w[..., 0:P, :]
    out[..., 0:D2, 1, :] = w[..., P:D, :]
    return out.reshape(lead + (P, 2 * n))


def hidden_rows(w):
    lead, n = w.shape[:-2], w.shape[-1]
    w = w.reshape(lead + (FC, P, n))
    return np.ascontiguousarray(np.moveaxis(w, -3, -2)).reshape(lead + (P, FC * n))


def spread(v):
    return np.ascontiguousarray(np.broadcast_to(v[..., None, :], v.shape[:-1] + (P, v.shape[-1])))


def stacked(w):
    out = np.zeros((D, PAIRS, 2, SLOT), np.float32)
    cols = w.reshape(D, PAIRS, 2, DH)
    for s in range(3):
        out[:, :, :, s * DH:(s + 1) * DH] = cols
    return rows(out.reshape(D, PAIRS * P))


def stacked_heads(w):
    out = np.zeros((w.shape[0], P, PAIRS, 2, SLOT), np.float32)
    for p in range(PAIRS):
        for a in range(2):
            hd = 2 * p + a
            r = SLOT * ((p // 2) % 2) + DH * (hd % 4)
            for s in range(3):
                out[:, r:r + DH, p, a, s * DH:(s + 1) * DH] = w[:, hd].transpose(0, 2, 1)
    return out.reshape(w.shape[0], P, PAIRS * P)


LO_ROWS = ((2,), (1,))


def stacked_bias(bq, bk):
    L = bq.shape[0]
    full = np.zeros((L, 2, SLOT, 2, PAIRS), np.float32)
    low = np.zeros_like(full)
    for i, bias in enumerate((bq, bk)):
        bb = bias.reshape(L, PAIRS, 2, DH).transpose(0, 2, 3, 1)
        for s in range(3):
            full[:, :, s * DH:(s + 1) * DH, i, :] = bb
            if s in LO_ROWS[i]:
                low[:, :, s * DH:(s + 1) * DH, i, :] = bb
    full[:, :, MROW:MROW + 2, 1, :] = 1.0
    return full.reshape(L, P, 2 * PAIRS), low.reshape(L, P, 2 * PAIRS)


def feature_pairs(g, b):
    gb = np.stack([g, b], -1)
    return rows(gb)


def block_diagonal(w):
    out = np.zeros((w.shape[0], D, D), np.float32)
    for hd in range(H):
        out[:, hd * DH:(hd + 1) * DH, hd * DH:(hd + 1) * DH] = w[:, hd].transpose(0, 2, 1)
    return out


def pack(i):
    f = {k: np.asarray(v) for k, v in i.items()}
    one = lambda v: v[None]
    n = {}
    n["tokens"] = np.ascontiguousarray(f["x"].reshape(B * T, P).T)
    n["pos"] = positions()
    n["ident"] = np.eye(P, dtype=np.float32)
    mask = np.zeros((2, SLOT, 2), np.float32)
    for j in range(2):
        for s in LO_ROWS[j]:
            mask[:, s * DH:(s + 1) * DH, j] = 1.0
    n["maskqk"] = mask.reshape(P, 2)
    r = np.arange(P) // DH
    n["blockmask"] = np.where(r[:, None] == r[None, :], 0.0, -1e30).astype(np.float32)
    n["emb"] = f["L0_tok_emb"]
    t = "L0_tok_"
    n["tok_wq"], n["tok_wk"], n["tok_wv"] = (one(stacked(f[t + "wq"])), one(stacked(f[t + "wk"])),
                                             one(rows(f[t + "wv"])))
    n["tok_bqk"], n["tok_bqk_lo"] = stacked_bias(one(f[t + "bq"]), one(f[t + "bk"]))
    n["tok_bv"], n["tok_wo"], n["tok_bo"] = one(spread(f[t + "bv"])), one(rows(f[t + "wo"])), one(spread(f[t + "bo"]))
    n["tok_w1"], n["tok_w2"] = one(rows(f[t + "w1"])), one(hidden_rows(f[t + "w2"]))
    n["tok_b1"], n["tok_b2"] = one(f[t + "b1"].reshape(FC, P).T), one(spread(f[t + "b2"]))
    n["tok_gb"] = one(spread(np.stack([f[t + "gamma1"], f[t + "beta1"], f[t + "gamma2"], f[t + "beta2"]])
                             .transpose(0, 1)).transpose(1, 0, 2).reshape(P, 4 * D))
    t = "L0_attn_"
    n["vit_wq"], n["vit_wk"] = stacked_heads(f[t + "qw"]), stacked_heads(f[t + "kw"])
    n["vit_wv"] = rows(block_diagonal(f[t + "vw"]))
    L = VIT_LAYERS
    n["vit_bqk"], n["vit_bqk_lo"] = stacked_bias(f[t + "qb"].reshape(L, D), f[t + "kb"].reshape(L, D))
    n["vit_bv"] = spread(f[t + "vb"].reshape(L, D))
    n["vit_ln1"] = feature_pairs(f[t + "ln1_g"], f[t + "ln1_b"])
    n["vit_ln2"] = feature_pairs(f[t + "ln2_g"], f[t + "ln2_b"])
    n["vit_w1"], n["vit_w2"] = rows(f[t + "w1"].transpose(0, 2, 1)), hidden_rows(f[t + "w2"].transpose(0, 2, 1))
    n["vit_b1"], n["vit_b2"] = f[t + "b1"].reshape(L, FC, P).transpose(0, 2, 1), spread(f[t + "b2"])
    t = "L1_attn_"
    w, z = f[t + "W_qkv"], np.zeros((1, D), np.float32)
    n["l1_wq"], n["l1_wk"], n["l1_wv"] = (one(stacked(w[:, 0:D])), one(stacked(w[:, D:2 * D])),
                                          one(rows(w[:, 2 * D:3 * D])))
    n["l1_bqk"], n["l1_bqk_lo"] = stacked_bias(z, z)
    n["l1_bv"] = spread(z)
    n["l1_wo"], n["l1_bo"] = one(rows(f[t + "W_proj"])), one(spread(f[t + "b_proj"]))
    t = "L0_ffn_"
    n["ffn_w1"] = rows(f[t + "W1_w"])
    n["ffn_bqk"] = spread(f[t + "W1_b"][0:2 * D])
    bv = np.zeros((P, 2), np.float32)
    bv[:, 0], bv[0:D2, 1] = f[t + "W1_b"][2 * D:2 * D + P], f[t + "W1_b"][2 * D + P:]
    n["ffn_bv"] = bv
    n["ffn_w2"], n["ffn_b2"] = rows(f[t + "W2_w"]), spread(f[t + "W2_b"])
    for ln in ("ln1", "ln2"):
        n["ffn_" + ln] = np.concatenate([spread(f[t + ln + "_w"]), spread(f[t + ln + "_b"])], 1)
    n["ffn_rw"], n["ffn_rb"] = rows(f[t + "r_w"]), spread(f[t + "r_b"])
    iota = spread(np.arange(MOE_E, dtype=np.float32))
    n["ffn_iota"] = n["ex_iota"] = iota
    n["moe_w1"], n["moe_w2"] = rows(f[t + "fc_w"]), hidden_rows(f[t + "proj_w"])
    n["moe_b1"], n["moe_b2"] = f[t + "fc_b"].reshape(MOE_E, FC, P).transpose(0, 2, 1), spread(f[t + "proj_b"])
    t = "L1_ffn_"
    n["ex_w1"], n["ex_w2"] = rows(f[t + "W1"]), hidden_rows(f[t + "W2"])
    n["ex_b1"], n["ex_b2"] = f[t + "b1"].reshape(L1_E, FC, P).transpose(0, 2, 1), spread(f[t + "b2"])
    n["ex_wg"], n["ex_bg"] = rows(f[t + "Wg"]), spread(f[t + "bg"])
    return {k: np.ascontiguousarray(v) for k, v in n.items()}


def kernel(**inputs):
    import concourse.bacc as bacc
    from concourse.bass_utils import run_bass_kernel_spmd

    nc = bacc.Bacc("TRN2", target_bir_lowering=False, num_devices=1)
    arrays, aps = {}, {}
    for name, value in pack(inputs).items():
        arrays[f"in_{name}_dram"] = value
        aps[name] = nc.dram_tensor(f"in_{name}_dram", value.shape, mybir.dt.from_np(value.dtype),
                                   kind="ExternalInput").ap()
    out = nc.dram_tensor("out_0_dram", (B, S, D), F32, kind="ExternalOutput").ap()
    lm_tower(nc, aps, out)
    return run_bass_kernel_spmd(nc, [arrays], core_ids=[0]).results[0]["out_0_dram"]
```

```python
from contextlib import ExitStack, contextmanager

import numpy as np

import concourse.bass as bass
from concourse import mybir

F32 = mybir.dt.float32
F32R = mybir.dt.float32r
I32 = mybir.dt.int32
ALU = mybir.AluOpType
ACT = mybir.ActivationFunctionType
AX = mybir.AxisListType

B, S, D, F = 8, 256, 192, 768
H, DH = 12, 16
P = 128
T = S // P
D2 = D - P
KC = ((0, P), (1, D2))
FC = F // P
PAIRS = H // 2
GROUPS = H // 4
SLOT = 64
MROW = 48
VIT_LAYERS = 8
MOE_E, TOP_K, L1_E = 8, 2, 4
VOCAB = 8000
SCALE = 0.25


@contextmanager
def semaphores(nc, stage):
    taken = []

    def sem(name):
        taken.append(nc.alloc_semaphore(f"{stage}_{name}"))
        return taken[-1]

    yield sem
    nc.clear_and_free_semaphores(taken)
    nc.all_engine_barrier()


class chain:

    def __init__(self, eng, sem, it, per):
        self.eng, self.sem, self.it, self.per, self.done = eng, sem, it, per, 0

    def __call__(self, ins):
        self.done += 1
        ins.then_inc(self.sem, 1)
        self.eng.wait_ge(self.sem, self.it * self.per + self.done)

    def finished(self):
        assert self.done == self.per, (self.done, self.per)


RSQRT_SEED = float(0x5F3759DF)
NEWTON = 3


def root(nc, pool, link, rt, half3, eps, var_ready, root_ready, turn, post):
    g = nc.gpsimd
    pool.wait_ge(var_ready, turn)
    vv, y, s, out, vh = rt[:, 0, :], rt[:, 1, :], rt[:, 2, :], rt[:, 3, :], rt[:, 4, :]
    for n in range(NEWTON):
        link(g.tensor_tensor(s, y, y, ALU.mult))
        link(g.tensor_tensor(s, s, vh, ALU.mult))
        link(g.tensor_tensor(s, s, half3, ALU.add))
        if n < NEWTON - 1 or post:
            link(g.tensor_tensor(y, y, s, ALU.mult))
        else:
            g.tensor_tensor(out, y, s, ALU.mult).then_inc(root_ready, 1)
    if post:
        link(g.tensor_tensor(s, y, vv, ALU.mult))
        g.tensor_tensor(out, s, eps, ALU.add).then_inc(root_ready, 1)


def root_steps(post):
    return 4 * NEWTON + 1 if post else 4 * NEWTON - 1


def wait_from(eng, sem, n):
    if isinstance(n, int) and n < 1:
        return
    eng.wait_ge(sem, n)


def turns(eng, units, body):
    body(0)
    body(1)
    with eng.Fori(2, units - 1) as i:
        body(i)
    for i in range(units - 1, units + 2):
        body(i)


def attention_stage(nc, name, kind, h, x, wd, cst):
    vit, tok, l1 = kind == "vit", kind == "tok", kind == "l1"
    layers = VIT_LAYERS if vit else 1
    N = layers * B
    mlp = not l1
    proj = not vit
    res = h if l1 else x
    with ExitStack() as ctx:
        def sb(n, shape, dt=F32):
            return ctx.enter_context(nc.sbuf_tensor(f"{name}_{n}", shape, dt))

        sem = ctx.enter_context(semaphores(nc, name))

        ps = ctx.enter_context(nc.psum_tensor(f"{name}_ps", [P, 8, 512], F32))
        wq = sb("wq", [P, 2, PAIRS, P])
        wk = sb("wk", [P, 2, PAIRS, P])
        wv = sb("wv", [P, 2, D])
        bqk = sb("bqk", [P, 2, PAIRS])
        bqk_lo = sb("bqk_lo", [P, 2, PAIRS])
        bv = sb("bv", [P, D])
        ln1 = sb("ln1", [P, 2, 2])
        ln2 = sb("ln2", [P, 2, 2])
        wo = sb("wo", [P, 2, D])
        bo = sb("bo", [P, D])
        w1 = sb("w1", [P, 2, F])
        b1 = sb("b1", [P, FC])
        w2 = sb("w2", [P, FC, D])
        b2 = sb("b2", [P, D])
        gb = sb("gb", [P, 4, D])
        st, mv = sb("st", [P, 3, T, 6]), sb("mv", [P, 3, T, 2])
        rt = [sb(f"rt{n}", [P, 6, T]) for n in range(3)]
        xh, xh2, xg = sb("xh", [P, T, D]), sb("xh2", [P, T, D]), sb("xg", [P, T, D])
        xn, xn2 = sb("xn", [P, 2, S]), sb("xn2", [P, 2, S])
        hm = sb("hm", [P, 2, S], F32R)
        qk = sb("qk", [P, 3, 2, S], F32R)
        q2 = sb("q2", [P, 2, S], F32R)
        mx = sb("mx", [P, 2, 2, T])
        mb = sb("mb", [P, 2, T, P], F32R)
        va = sb("va", [P, T, H, 32])
        pt = sb("pt", [P, H, T, S])
        ot = sb("ot", [P, GROUPS, S])
        rcp = sb("rcp", [P, T, H])
        att = sb("att", [P, T, D])
        at = sb("at", [P, 2, S])
        r1, r2 = sb("r1", [P, T, D]), sb("r2", [P, T, D])
        yb = sb("yb", [P, T, D])
        hid = sb("hid", [P, FC, S])

        ln_loaded, w_loaded, wm_loaded = sem("ln1_loaded"), sem("attn_weights_loaded"), sem("mlp_weights_loaded")
        w2_loaded = sem("mlp_out_weights_loaded")
        zeroed, cleared = sem("zeroed"), sem("cleared")
        ln1_step, mb_step, out_step, y_step, pool_step = (sem("ln1_step"), sem("mb_step"), sem("out_step"),
                                                          sem("y_step"), sem("pool_step"))
        last_step, pool2_step, pool3_step = sem("last_norm_step"), sem("pool2_step"), sem("pool3_step")
        att_added = sem("att_added")
        out2_step, out3_step, h1_kept = sem("h1_step"), sem("result_step"), sem("h1_kept")
        var_ready = [sem(f"var_ready{n}") for n in range(3)]
        root_ready = [sem(f"root_ready{n}") for n in range(3)]
        xhat_ready, xT_done, xn_ready = sem("xhat_ready"), sem("xT_done"), sem("xn_ready")
        v_done, v_ready = sem("v_done"), sem("v_ready")
        proj_done, hm_ready, qk_ready = sem("proj_done"), sem("hm_ready"), sem("qk_ready")
        s_done, mx_done, m_ready = sem("s_done"), sem("mx_done"), sem("m_ready")
        mt_done, q2_ready, st_done = sem("mt_done"), sem("q2_ready"), sem("st_done")
        p_ready, pv_done, oT_ready = sem("p_ready"), sem("pv_done"), sem("oT_ready")
        ot_done, att_ready = sem("ot_done"), sem("att_ready")
        aT_done, aT_ready, op_done, op_read = sem("aT_done"), sem("aT_ready"), sem("op_done"), sem("op_read")
        xhat2_ready, xT2_done, xn2_ready = sem("xhat2_ready"), sem("xT2_done"), sem("xn2_ready")
        h_done, h_ready, y_done, y_read, x_ready = (sem("h_done"), sem("h_ready"), sem("y_done"), sem("y_read"),
                                                    sem("x_ready"))

        ident, identr, maskqk = cst["ident"], cst["identr"], cst["maskqk"]
        half3, eps = cst["newton"][:, 0, :], cst["newton"][:, 1, :]

        def at_unit(t_, u):
            return t_[:, bass.ds((u % B) * T, T), :]

        def at_tile(t_, u, t):
            return t_[:, bass.ds((u % B) * T + t, 1), :].rearrange("p a d -> p (a d)")

        ln_loads = [(ln1, wd["ln1"])] if vit else []
        attn_loads = [(wq, wd["wq"]), (wk, wd["wk"]), (wv, wd["wv"]), (bqk, wd["bqk"]), (bqk_lo, wd["bqk_lo"]),
                      (bv, wd["bv"])]
        if proj:
            attn_loads += [(wo, wd["wo"]), (bo, wd["bo"])]
        out_loads = [(w2, wd["w2"]), (b2, wd["b2"])] if mlp else []
        mlp_loads = [(w1, wd["w1"]), (b1, wd["b1"])] if mlp else []
        mlp_loads += [(ln2, wd["ln2"])] if vit else []
        mlp_loads += [(gb, wd["gb"])] if tok else []
        NM2 = 16 * len(out_loads)
        NL, NA, NM = 16 * len(ln_loads), 16 * len(attn_loads), 16 * len(mlp_loads)

        def loads_of(u, n):
            return (u // B + 1) * n if layers > 1 else n

        block = ctx.enter_context(nc.Block())

        def load(sp, loads, l, s):
            for dst, src in loads:
                part = src[bass.ds(l, 1)].rearrange("a p n -> (a p) n")
                flat = dst[:, :] if len(dst.shape) == 2 else (
                    dst[:, :, :].rearrange("p a b -> p (a b)") if len(dst.shape) == 3
                    else dst[:, :, :, :].rearrange("p a b c -> p (a b c)"))
                sp.dma_start(flat[:, 0:src.shape[2]], part).then_inc(s, 16)

        @block.sync
        def _(sp):
            load(sp, ln_loads, 0, ln_loaded)
            load(sp, attn_loads, 0, w_loaded)
            load(sp, mlp_loads, 0, wm_loaded)
            load(sp, out_loads, 0, w2_loaded)
            if layers > 1:
                with sp.Fori(1, layers) as l:
                    sp.wait_ge(xn_ready, l * B * 2)
                    load(sp, ln_loads, l, ln_loaded)
                    sp.wait_ge(proj_done, l * B * PAIRS)
                    load(sp, attn_loads[:3], l, w_loaded)
                    sp.wait_ge(qk_ready, l * B * PAIRS)
                    sp.wait_ge(v_ready, l * B)
                    load(sp, attn_loads[3:], l, w_loaded)
                    sp.wait_ge(h_ready, l * B * FC)
                    load(sp, mlp_loads, l, wm_loaded)
                    sp.wait_ge(y_read, l * B)
                    load(sp, out_loads, l, w2_loaded)
                sp.wait_ge(ln_loaded, NL * layers)
            sp.wait_ge(w_loaded, NA * layers)
            if mlp:
                sp.wait_ge(wm_loaded, NM * layers)
                sp.wait_ge(w2_loaded, NM2 * layers)

        @block.gpsimd
        def _(pool):
            def add(u, src, ready, added):
                pool.wait_ge(ready, u + 1)
                nc.gpsimd.tensor_tensor(at_unit(x, u), at_unit(x, u), src[:, :, :], ALU.add).then_inc(added, 1)

            def norm(n, step, u, post):
                link = chain(pool, step, u, root_steps(post))
                root(nc, pool, link, rt[n], half3, eps, var_ready[n], root_ready[n], u + 1, post)
                link.finished()

            def body(i):
                loop = not isinstance(i, int)
                if not tok and (loop or i + 1 < N):
                    norm(0, pool_step, i + 1, False)
                if tok and (loop or i >= 2):
                    norm(2, pool3_step, i - 2, True)
                if vit and (loop or 1 <= i <= N):
                    add(i - 1, att, att_ready, att_added)
                if mlp and (loop or 1 <= i <= N):
                    norm(1, pool2_step, i - 1, tok)
                if vit and (loop or i >= 2):
                    add(i - 2, yb, y_read, x_ready)

            if vit:
                nc.gpsimd.memset(rt[1][:, 5, :], 0.0).then_inc(x_ready, B)
            if not tok:
                norm(0, pool_step, 0, False)
            turns(pool, N, body)

        @block.tensor
        def _(pe):
            mm, tr = nc.tensor.matmul, nc.tensor.transpose

            def transposes(src, bank):
                for t in range(T):
                    for c, k in KC:
                        last = tr(ps[0:k, bank, c * S + t * P:c * S + (t + 1) * P],
                                  src[:, t, c * P:c * P + k], ident[:, :])
                return last

            def project(u, p):
                if p == 0:
                    pe.wait_ge(w_loaded, loads_of(u, NA))
                    pe.wait_ge(xn_ready, 2 * u + 2)
                wait_from(pe, qk_ready, u * PAIRS + p)
                for i, w in enumerate((wq, wk)):
                    out = ps[:, 2, i * S:(i + 1) * S]
                    if vit:
                        r, c = SLOT * ((p // 2) % 2), p // 4
                        last = mm(out, w[r:r + SLOT, 0, p, :], xn[r:r + SLOT, c, :], start=True, stop=True)
                    else:
                        for c, k in KC:
                            last = mm(out, w[0:k, c, p, :], xn[0:k, c, :], start=(c == 0), stop=(c == 1))
                last.then_inc(proj_done, 1)

            def scores(u, p):
                pe.wait_ge(qk_ready, u * PAIRS + p + 1)
                wait_from(pe, q2_ready, u * PAIRS + p)
                for a in range(2):
                    wait_from(pe, mx_done, u * H + 2 * (p - 1) + a + 1)
                    r = SLOT * a
                    for t in range(T):
                        last = mm(ps[:, a, t * S:(t + 1) * S], qk[r:r + SLOT, p % 3, 0, t * P:(t + 1) * P],
                                  qk[r:r + SLOT, p % 3, 1, :], start=True, stop=True)
                    last.then_inc(s_done, 1)

            def max_rows(u, p):
                pe.wait_ge(m_ready, u * PAIRS + p + 1)
                for t in range(T):
                    last = mm(ps[:, 0, t * P:(t + 1) * P], mb[:, p % 2, t, :], identr[:, :], start=True, stop=True)
                last.then_inc(mt_done, 1)

            def scores_t(u, p):
                pe.wait_ge(q2_ready, u * PAIRS + p + 1)
                for a in range(2):
                    hd, r = 2 * p + a, SLOT * a
                    wait_from(pe, p_ready, u * H + hd - 1)
                    for t in range(T):
                        last = mm(ps[:, 3 + a, t * S:(t + 1) * S],
                                  qk[r:r + SLOT, p % 3, 1, t * P:(t + 1) * P], q2[r:r + SLOT, p % 2, :],
                                  start=True, stop=True)
                    last.then_inc(st_done, 1)

            def weighted(u, g, tiles=range(T)):
                if 0 in tiles:
                    if g == 0:
                        pe.wait_ge(v_ready, u + 1)
                    pe.wait_ge(p_ready, u * H + 4 * g + 4)
                    wait_from(pe, oT_ready, u * GROUPS + g)
                for t in tiles:
                    for j in range(4):
                        hd = 4 * g + j
                        last = mm(ps[32 * j:32 * j + 32, 6, 0:S], va[:, t, hd, :], pt[:, hd, t, :],
                                  start=(t == 0), stop=(t == T - 1), skip_group_check=True)
                if T - 1 in tiles:
                    last.then_inc(pv_done, 1)

            def input_t(u):
                pe.wait_ge(xhat_ready, u + 1)
                wait_from(pe, v_ready, u)
                transposes(xh, 6).then_inc(xT_done, 1)

            def values(u):
                wait_from(pe, att_ready, u)
                for t in range(T):
                    for c, k in KC:
                        out = ps[:, 6, t * D:(t + 1) * D]
                        lhs = xn[0:k, c, t * P:(t + 1) * P]
                        if vit:
                            last = mm(out[:, c * P:c * P + k], lhs, wv[0:k, c, c * P:c * P + k],
                                      start=True, stop=True)
                        else:
                            last = mm(out, lhs, wv[0:k, c, :], start=(c == 0), stop=(c == 1))
                last.then_inc(v_done, 1)

            def output_t(u):
                pe.wait_ge(oT_ready, (u + 1) * GROUPS)
                if l1:
                    wait_from(pe, op_read, u)
                for t in range(T):
                    for g in range(GROUPS):
                        last = tr(ps[:, 6 + t, g * P:(g + 1) * P], ot[:, g, t * P:(t + 1) * P], ident[:, :])
                last.then_inc(ot_done, 1)

            def normed_t(u):
                pe.wait_ge(att_ready, u + 1)
                transposes(att, 7).then_inc(aT_done, 1)

            def project_out(u):
                pe.wait_ge(aT_ready, 2 * u + 2)
                for t in range(T):
                    for c, k in KC:
                        last = mm(ps[:, 7, t * D:(t + 1) * D], at[0:k, c, t * P:(t + 1) * P], wo[0:k, c, :],
                                  start=(c == 0), stop=(c == 1))
                last.then_inc(op_done, 1)

            def mlp_input_t(u):
                pe.wait_ge(xhat2_ready, u + 1)
                pe.wait_ge(oT_ready, (u + 2) * GROUPS - 1 if not isinstance(u, int) or u + 2 <= N
                           else N * GROUPS)
                transposes(xh2, 6).then_inc(xT2_done, 1)

            def mlp_up(u, chunks):
                if 0 in chunks:
                    pe.wait_ge(wm_loaded, loads_of(u, NM))
                    pe.wait_ge(xn2_ready, 2 * u + 2)
                    wait_from(pe, y_read, u)
                for m in chunks:
                    if m >= 2:
                        pe.wait_ge(h_ready, u * FC + m - 1)
                    for c, k in KC:
                        last = mm(ps[:, 5 + 2 * (m % 2), 0:S], w1[0:k, c, m * P:(m + 1) * P], xn2[0:k, c, :],
                                  start=(c == 0), stop=(c == 1))
                    last.then_inc(h_done, 1)

            def mlp_down(u, t, chunks=range(FC)):
                if t == 0 and 0 in chunks:
                    pe.wait_ge(h_ready, (u + 1) * FC)
                    pe.wait_ge(w2_loaded, loads_of(u, NM2))
                for m in chunks:
                    last = mm(ps[:, 5, t * D:(t + 1) * D], hid[:, m, t * P:(t + 1) * P], w2[:, m, :],
                              start=(m == 0), stop=(m == FC - 1))
                if FC - 1 in chunks:
                    last.then_inc(y_done, 1)

            def body(i):
                loop = not isinstance(i, int)
                now, nxt = loop or i < N, loop or i + 1 < N
                prev, old = loop or 1 <= i <= N, loop or i >= 2
                mlp_old = old and mlp
                for s in range(PAIRS):
                    if now:
                        scores(i, s)
                    if s == 1 and mlp_old:
                        if tok:
                            mlp_input_t(i - 2)
                        mlp_up(i - 2, range(0 if tok else 2, FC))
                    if s == 2 and prev:
                        output_t(i - 1)
                    if s == 3 and now:
                        values(i)
                    if s == 3 and mlp_old:
                        if tok:
                            mlp_down(i - 2, 1)
                        else:
                            mlp_down(i - 2, 0, range(FC // 2, FC))
                    if s == 4 and nxt:
                        input_t(i + 1)
                    if s == 4 and mlp_old and vit:
                        mlp_down(i - 2, 1, range(FC // 2, FC))
                    if s > 0 and now:
                        scores_t(i, s - 1)
                    if s == 0 and prev:
                        scores_t(i - 1, PAIRS - 1)
                    if s == 0 and mlp_old and not tok:
                        mlp_input_t(i - 2)
                    if s < PAIRS - 2 and now:
                        project(i, s + 2)
                    if s == 4 and nxt:
                        project(i + 1, 0)
                    if s == PAIRS - 1 and nxt:
                        project(i + 1, 1)
                    if s == 5 and prev and proj:
                        project_out(i - 1)
                    if s == 5 and now:
                        weighted(i, 1, (0,))
                    if now:
                        max_rows(i, s)
                    if s == 0 and mlp_old and not tok:
                        mlp_up(i - 2, range(0, 2))
                    if s == 1 and prev:
                        weighted(i - 1, 2)
                    if s == 2 and mlp_old:
                        mlp_down(i - 2, 0, range(FC if tok else FC // 2))
                    if s == 3 and mlp_old and vit:
                        mlp_down(i - 2, 1, range(0, FC // 2))
                    if s == 4 and now:
                        weighted(i, 0)
                    if s == 4 and prev and proj:
                        normed_t(i - 1)
                    if s == 5 and now:
                        weighted(i, 1, (1,))

            pe.wait_ge(cleared, 1)
            input_t(0)
            project(0, 0)
            project(0, 1)
            turns(pe, N, body)

        @block.scalar
        def _(act):
            go = nc.scalar.activation

            def input_scaled(u):
                if vit:
                    act.wait_ge(ln_loaded, loads_of(u, NL))
                act.wait_ge(xT_done, u + 1)
                wait_from(act, proj_done, u * PAIRS)
                for c, k in KC:
                    src, dst = ps[0:k, 6, c * S:(c + 1) * S], xn[0:k, c, :]
                    if vit:
                        go(dst, src, ACT.Identity, bias=ln1[0:k, c, 1:2], scale=ln1[0:k, c, 0:1]).then_inc(xn_ready, 1)
                    else:
                        go(dst, src, ACT.Copy).then_inc(xn_ready, 1)

            def parts(u, p):
                if p == 0:
                    act.wait_ge(w_loaded, loads_of(u, NA))
                act.wait_ge(proj_done, u * PAIRS + p + 1)
                for i in range(2):
                    last = go(hm[:, i, :], ps[:, 2, i * S:(i + 1) * S], ACT.Identity,
                              bias=bqk_lo[:, i, p:p + 1], scale=maskqk[:, i:i + 1])
                last.then_inc(hm_ready, 1)

            def exps(u, p):
                for a in range(2):
                    hd = 2 * p + a
                    act.wait_ge(st_done, u * H + hd + 1)
                    wait_from(act, pv_done, u * GROUPS + hd // 4 - GROUPS + 1)
                    go(pt[:, hd, :, :].rearrange("p t s -> p (t s)"), ps[:, 3 + a, :], ACT.Exp,
                       scale=SCALE).then_inc(p_ready, 1)

            def out_t(u, g):
                act.wait_ge(pv_done, u * GROUPS + g + 1)
                wait_from(act, ot_done, u)
                go(ot[:, g, :], ps[:, 6, 0:S], ACT.Copy).then_inc(oT_ready, 1)

            def normed(u):
                act.wait_ge(aT_done, u + 1)
                for c, k in KC:
                    go(at[0:k, c, :], ps[0:k, 7, c * S:(c + 1) * S], ACT.Copy).then_inc(aT_ready, 1)

            def mlp_input_scaled(u):
                act.wait_ge(wm_loaded, loads_of(u, NM))
                act.wait_ge(xT2_done, u + 1)
                for c, k in KC:
                    src, dst = ps[0:k, 6, c * S:(c + 1) * S], xn2[0:k, c, :]
                    if vit:
                        go(dst, src, ACT.Identity, bias=ln2[0:k, c, 1:2], scale=ln2[0:k, c, 0:1]).then_inc(xn2_ready, 1)
                    else:
                        go(dst, src, ACT.Copy).then_inc(xn2_ready, 1)

            def hidden(u):
                for m in range(FC):
                    act.wait_ge(h_done, u * FC + m + 1)
                    go(hid[:, m, :], ps[:, 5 + 2 * (m % 2), 0:S], ACT.Relu if tok else ACT.Gelu,
                       bias=b1[:, m:m + 1]).then_inc(h_ready, 1)

            def body(i):
                loop = not isinstance(i, int)
                now, nxt = loop or i < N, loop or i + 1 < N
                prev, old = loop or 1 <= i <= N, loop or i >= 2
                for s in range(PAIRS):
                    if s == 1 and old and tok:
                        mlp_input_scaled(i - 2)
                        hidden(i - 2)
                    if s == 4 and nxt:
                        input_scaled(i + 1)
                    if s > 0 and now:
                        exps(i, s - 1)
                    if s == 0 and prev:
                        exps(i - 1, PAIRS - 1)
                    if s == 0 and old and vit:
                        mlp_input_scaled(i - 2)
                    if s < PAIRS - 2 and now:
                        parts(i, s + 2)
                    if s == 0 and old and vit:
                        hidden(i - 2)
                    if s == 1 and prev:
                        out_t(i - 1, 2)
                    if s == 4 and nxt:
                        parts(i + 1, 0)
                    if s == 4 and now:
                        out_t(i, 0)
                    if s == 4 and prev and proj:
                        normed(i - 1)
                    if s == PAIRS - 1 and nxt:
                        parts(i + 1, 1)
                    if s == 5 and now:
                        out_t(i, 1)

            input_scaled(0)
            parts(0, 0)
            parts(0, 1)
            turns(act, N, body)

        @block.vector
        def _(dve):
            v = nc.vector

            def stats(link, n, src):
                post = n == 2 or (tok and n == 1)
                r = rt[n]
                v.memset(r[:, 5, :], 0.0)
                v.bn_stats(st[:, n, 0, :], src(0))
                link(v.bn_stats(st[:, n, 1, :], src(1)))
                v.memset(r[:, 5, :], 0.0)
                v.bn_aggr(mv[:, n, 0, :], st[:, n, 0, :])
                link(v.bn_aggr(mv[:, n, 1, :], st[:, n, 1, :]))
                if post:
                    link(v.tensor_scalar(r[:, 0, :], mv[:, n, :, 1], 1e-30, None, ALU.max))
                else:
                    link(v.tensor_scalar(r[:, 0, :], mv[:, n, :, 1], 1e-5, None, ALU.add))
                bits = r[:, 1, :].bitcast(I32)
                v.tensor_scalar(r[:, 4, :], r[:, 0, :], -0.5, None, ALU.mult)
                v.tensor_scalar(bits, r[:, 0, :].bitcast(I32), -0.5, RSQRT_SEED, ALU.mult,
                                ALU.add).then_inc(var_ready[n], 1)

            def normed(n, dst, src, u, link=None):
                dve.wait_ge(root_ready[n], u + 1)
                if link is not None:
                    link(v.reciprocal(rt[n][:, 3, :], rt[n][:, 3, :]))
                for t in range(T):
                    last = v.tensor_scalar(dst[:, t, :], src(t), mv[:, n, t, 0:1], rt[n][:, 3, t:t + 1],
                                           ALU.subtract, ALU.mult)
                return last

            def affine(link, dst, src, out, k):
                for t in range(T):
                    last = v.tensor_tensor(dst[:, t, :], src[:, t, :], gb[:, k, :], ALU.mult)
                link(last)
                for t in range(T):
                    last = v.tensor_tensor(out(t), dst[:, t, :], gb[:, k + 1, :], ALU.add)
                return last

            def input_stats(u):
                if not tok:
                    link = chain(dve, ln1_step, u, 3)
                    if vit:
                        dve.wait_ge(x_ready, u + 1)
                    stats(link, 0, lambda t: at_tile(res, u, t))
                    link.finished()

            def input_normed(u):
                wait_from(dve, xT_done, u)
                if tok:
                    v.tensor_scalar(xh[:, :, :], at_unit(res, u), 1.0, None, ALU.mult).then_inc(xhat_ready, 1)
                else:
                    normed(0, xh, lambda t: at_tile(res, u, t), u).then_inc(xhat_ready, 1)

            def values(u):
                if layers > 1:
                    dve.wait_ge(w_loaded, loads_of(u, NA))
                dve.wait_ge(v_done, u + 1)
                wait_from(dve, pv_done, u * GROUPS)
                for t in range(T):
                    last = v.tensor_tensor(va[:, t, :, 0:DH],
                                           ps[:, 6, t * D:(t + 1) * D].rearrange("p (h d) -> p h d", h=H),
                                           bv[:, :].rearrange("p (h d) -> p h d", h=H), ALU.add)
                last.then_inc(v_ready, 1)

            def stack(u, p):
                if p == 0:
                    dve.wait_ge(w_loaded, loads_of(u, NA))
                dve.wait_ge(hm_ready, u * PAIRS + p + 1)
                wait_from(dve, st_done, u * H + 2 * (p - 2))
                for i in range(2):
                    last = v.scalar_tensor_tensor(out=qk[:, p % 3, i, :], in0=ps[:, 2, i * S:(i + 1) * S],
                                                  scalar=bqk[:, i, p:p + 1], in1=hm[:, i, :],
                                                  op0=ALU.add, op1=ALU.subtract)
                last.then_inc(qk_ready, 1)

            def maxima(u, p):
                for a in range(2):
                    dve.wait_ge(s_done, u * H + 2 * p + a + 1)
                    v.tensor_reduce(mx[:, p % 2, a, :], ps[:, a, :].rearrange("p (t s) -> p t s", t=T),
                                    AX.X, ALU.max).then_inc(mx_done, 1)
                dve.wait_ge(mx_done, u * H + 2 * p + 2)
                wait_from(dve, mt_done, u * PAIRS + p - 1)
                m = mx[:, p % 2, :, :].rearrange("p a t -> p t a")
                hi = mb[:, p % 2, :, :].rearrange("p t (a c) -> p t a c", a=2)[:, :, :, MROW]
                lo = mb[:, p % 2, :, :].rearrange("p t (a c) -> p t a c", a=2)[:, :, :, MROW + 1]
                v.tensor_scalar(hi, m, -1.0, None, ALU.mult).then_inc(mb_step, 1)
                dve.wait_ge(mb_step, u * PAIRS + p + 1)
                v.scalar_tensor_tensor(out=lo, in0=m, scalar=-1.0, in1=hi, op0=ALU.mult,
                                       op1=ALU.subtract).then_inc(m_ready, 1)

            def with_max(u, p):
                dve.wait_ge(mt_done, u * PAIRS + p + 1)
                wait_from(dve, st_done, u * H + 2 * (p - 1))
                v.tensor_tensor(q2[:, p % 2, :], ps[:, 0, 0:S], qk[:, p % 3, 0, :], ALU.add).then_inc(q2_ready, 1)

            def output(u):
                link = chain(dve, out_step, u, 1)
                dve.wait_ge(ot_done, u + 1)
                if proj:
                    wait_from(dve, aT_done, u)
                heads = lambda t: ps[:, 6 + t, 0:GROUPS * P].rearrange("p (h c) -> p h c", h=H)
                for t in range(T):
                    last = v.reciprocal(rcp[:, t, :], heads(t)[:, :, DH])
                link(last)
                for t in range(T):
                    last = v.tensor_tensor(att[:, t, :].rearrange("p (h d) -> p h d", h=H), heads(t)[:, :, 0:DH],
                                           rcp[:, t, :].unsqueeze(2).to_broadcast([P, H, DH]), ALU.mult)
                last.then_inc(att_ready, 1)
                link.finished()

            def output_stats(u):
                link = chain(dve, y_step, u, 3)
                dve.wait_ge(att_added, u + 1)
                stats(link, 1, lambda t: at_tile(x, u, t))
                link.finished()

            def output_normed(u):
                wait_from(dve, xT2_done, u)
                normed(1, xh2, lambda t: at_tile(x, u, t), u).then_inc(xhat2_ready, 1)

            def projected(u):
                link = chain(dve, y_step, u, 1 if l1 else 5)
                dve.wait_ge(op_done, u + 1)
                for t in range(T):
                    last = v.tensor_tensor(r1[:, t, :], ps[:, 7, t * D:(t + 1) * D], bo[:, :], ALU.add)
                link(last)
                if l1:
                    v.tensor_tensor(at_unit(res, u), at_unit(res, u), r1[:, :, :], ALU.add).then_inc(op_read, 1)
                else:
                    link(v.tensor_tensor(r1[:, :, :], at_unit(res, u), r1[:, :, :], ALU.add))
                    stats(link, 1, lambda t: r1[:, t, :])
                link.finished()

            def projected_normed(u):
                link = chain(dve, out2_step, u, 3)
                dve.wait_ge(wm_loaded, NM)
                link(normed(1, xg, lambda t: r1[:, t, :], u, link))
                wait_from(dve, xT2_done, u)
                affine(link, xg, xg, lambda t: xh2[:, t, :], 0).then_inc(xhat2_ready, 1)
                dve.wait_ge(xhat2_ready, u + 1)
                v.tensor_scalar(at_unit(x, u), xh2[:, :, :], 1.0, None, ALU.mult).then_inc(h1_kept, 1)
                link.finished()

            def mlp_out(u):
                if vit:
                    dve.wait_ge(x_ready, u + B)
                dve.wait_ge(y_done, T * (u + 1))
                dve.wait_ge(w2_loaded, loads_of(u, NM2))
                for t in range(T):
                    last = v.tensor_tensor(yb[:, t, :], ps[:, 5, t * D:(t + 1) * D], b2[:, :], ALU.add)
                last.then_inc(y_read, 1)
                if tok:
                    dve.wait_ge(y_read, u + 1)
                    link = chain(dve, last_step, u, 4)
                    dve.wait_ge(h1_kept, u + 1)
                    link(v.tensor_tensor(r2[:, :, :], at_unit(x, u), yb[:, :, :], ALU.add))
                    stats(link, 2, lambda t: r2[:, t, :])
                    link.finished()

            def mlp_normed(u):
                link = chain(dve, out3_step, u, 4)
                link(normed(2, r2, lambda t: r2[:, t, :], u, link))
                link(affine(link, r2, r2, lambda t: at_tile(h, u, t), 2))
                link.finished()

            def body(i):
                loop = not isinstance(i, int)
                now, nxt = loop or i < N, loop or i + 1 < N
                prev, old = loop or 1 <= i <= N, loop or i >= 2
                for s in range(PAIRS):
                    if now:
                        maxima(i, s)
                    if s == 2 and prev:
                        output(i - 1)
                    if s == 3 and now:
                        values(i)
                    if now:
                        with_max(i, s)
                    if s == 4 and nxt:
                        stack(i + 1, 0)
                    if s == 0 and old and tok:
                        projected_normed(i - 2)
                    if s == 0 and nxt:
                        input_stats(i + 1)
                    if s == 1 and nxt:
                        input_normed(i + 1)
                    if s == 4 and old and tok:
                        mlp_out(i - 2)
                    if s == 4 and prev and vit:
                        output_normed(i - 1)
                    if s == 5 and prev and proj:
                        projected(i - 1)
                    if s < PAIRS - 2 and now:
                        stack(i, s + 2)
                    if s == 3 and prev and vit:
                        output_stats(i - 1)
                    if s == PAIRS - 1 and nxt:
                        stack(i + 1, 1)
                    if s == 5 and old and tok:
                        mlp_normed(i - 2)
                    if s == 5 and old and vit:
                        mlp_out(i - 2)

            v.memset(mb[:, :, :, :].rearrange("p a t c -> p (a t c)").bitcast(F32), 0.0)
            v.memset(va[:, :, :, :].rearrange("p t h c -> p (t h c)"), 0.0).then_inc(zeroed, 1)
            dve.wait_ge(zeroed, 1)
            v.memset(va[:, :, :, DH:DH + 1].rearrange("p t h c -> p (t h) c"), 1.0).then_inc(cleared, 1)
            input_stats(0)
            input_normed(0)
            stack(0, 0)
            stack(0, 1)
            turns(dve, N, body)


def embedding_stage(nc, x, a, cst):
    with ExitStack() as ctx:
        sem = ctx.enter_context(semaphores(nc, "emb"))
        tok_i = ctx.enter_context(nc.sbuf_tensor("emb_tok_i", [P, B * T], I32))
        tok_f = ctx.enter_context(nc.sbuf_tensor("emb_tok_f", [P, B * T], F32))
        neg = ctx.enter_context(nc.sbuf_tensor("emb_neg", [P, B * T], F32))
        idx = ctx.enter_context(nc.sbuf_tensor("emb_idx", [P, B * T], mybir.dt.uint32))
        pos = ctx.enter_context(nc.sbuf_tensor("emb_pos", [P, T, D], F32))
        loaded = sem("loaded")
        const_loaded = sem("const_loaded")
        steps = sem("steps")
        gathered = sem("gathered")
        block = ctx.enter_context(nc.Block())

        @block.sync
        def _(sp):
            sp.dma_start(tok_i[:, :], a["tokens"]).then_inc(loaded, 16)
            sp.dma_start(pos[:, :, :].rearrange("p t d -> p (t d)"), a["pos"]).then_inc(const_loaded, 16)
            sp.dma_start(cst["ident"][:, :], a["ident"]).then_inc(const_loaded, 16)
            sp.dma_start(cst["maskqk"][:, :], a["maskqk"]).then_inc(const_loaded, 16)
            sp.dma_start(cst["blockmask"][:, :], a["blockmask"]).then_inc(const_loaded, 16)
            sp.wait_ge(const_loaded, 64)

        @block.vector
        def _(dve):
            v = nc.vector
            dve.wait_ge(loaded, 16)
            v.tensor_copy(tok_f[:, :], tok_i[:, :]).then_inc(steps, 1)
            dve.wait_ge(steps, 1)
            v.tensor_scalar(neg[:, :], tok_f[:, :], 0.0, float(VOCAB), ALU.is_lt, ALU.mult).then_inc(steps, 1)
            dve.wait_ge(steps, 2)
            v.tensor_tensor(tok_f[:, :], tok_f[:, :], neg[:, :], ALU.add).then_inc(steps, 1)
            dve.wait_ge(steps, 3)
            v.tensor_scalar(idx[:, :], tok_f[:, :], 0.0, float(VOCAB - 1), ALU.max, ALU.min).then_inc(steps, 1)
            dve.wait_ge(const_loaded, 64)
            v.tensor_copy(cst["identr"][:, :], cst["ident"][:, :])
            dve.wait_ge(gathered, 16 * T * B)
            for b in range(B):
                v.tensor_tensor(x[:, b * T:(b + 1) * T, :], x[:, b * T:(b + 1) * T, :], pos[:, :, :], ALU.add)

        @block.gpsimd
        def _(pool):
            nc.gpsimd.memset(cst["newton"][:, 0, :], 1.5)
            nc.gpsimd.memset(cst["newton"][:, 1, :], 1e-5)
            pool.wait_ge(steps, 4)
            for n in range(B * T):
                pool.indirect_dma_start(out=x[:, n, :], out_offset=None, in_=a["emb"],
                                        in_offset=bass.IndirectOffsetOnAxis(ap=idx[:, n:n + 1], axis=0)
                                        ).then_inc(gathered, 16)
            pool.wait_ge(gathered, 16 * B * T)


def glue_stage(nc, name, h, x, add):
    TILES = B * T
    with ExitStack() as ctx:
        def sb(n, shape):
            return ctx.enter_context(nc.sbuf_tensor(f"{name}_{n}", shape, F32))

        sem = ctx.enter_context(semaphores(nc, name))
        st, mv, rt = sb("st", [P, TILES, 6]), sb("mv", [P, TILES, 2]), sb("rt", [P, 6, TILES])
        half3 = sb("half3", [P, TILES])
        steps, pool_steps = sem("steps"), sem("pool_steps")
        var_ready, root_ready = sem("var_ready"), sem("root_ready")
        block = ctx.enter_context(nc.Block())

        @block.gpsimd
        def _(pool):
            link = chain(pool, pool_steps, 0, 1 + root_steps(False))
            link(nc.gpsimd.memset(half3[:, :], 1.5))
            root(nc, pool, link, rt, half3[:, :], None, var_ready, root_ready, 1, False)
            link.finished()

        @block.vector
        def _(dve):
            v = nc.vector
            link = chain(dve, steps, 0, 4 if add else 3)
            if add:
                link(v.tensor_tensor(h[:, :, :], h[:, :, :], x[:, :, :], ALU.add))
            for n in range(TILES):
                last = v.bn_stats(st[:, n, :], h[:, n, :])
            link(last)
            for n in range(TILES):
                last = v.bn_aggr(mv[:, n, :], st[:, n, :])
            link(last)
            link(v.tensor_scalar(rt[:, 0, :], mv[:, :, 1], 1e-5, None, ALU.add))
            v.tensor_scalar(rt[:, 4, :], rt[:, 0, :], -0.5, None, ALU.mult)
            v.tensor_scalar(rt[:, 1, :].bitcast(I32), rt[:, 0, :].bitcast(I32), -0.5, RSQRT_SEED, ALU.mult,
                            ALU.add).then_inc(var_ready, 1)
            dve.wait_ge(root_ready, 1)
            for n in range(TILES):
                v.tensor_scalar(x[:, n, :], h[:, n, :], mv[:, n, 0:1], rt[:, 3, n:n + 1], ALU.subtract, ALU.mult)
            link.finished()


def channel_attention_stage(nc, x, wd, cst, scratch):
    with ExitStack() as ctx:
        def sb(n, shape, dt=F32):
            return ctx.enter_context(nc.sbuf_tensor(f"ca_{n}", shape, dt))

        sem = ctx.enter_context(semaphores(nc, "ca"))

        ps = ctx.enter_context(nc.psum_tensor("ca_ps", [P, 8, 512], F32))
        w = sb("w", [P, 2, 3 * D])
        bqk = sb("bqk", [P, 2 * D])
        bv = sb("bv", [P, 2])
        xh, xn = sb("xh", [P, T, D]), sb("xn", [P, 2, S])
        qk = sb("qk", [P, T, 2 * D])
        vt = sb("vt", [P, 2, S])
        gm, ex, wt = sb("gm", [P, 2, P]), sb("ex", [P, 2, P]), sb("wt", [P, 2, P])
        mx, sm = sb("mx", [P, 2]), sb("sm", [P, 2])
        osb = sb("osb", [P, 2, S])
        loaded, dch = sem("weights_loaded"), sem("vector_chain")
        xhat_ready, xT_done, xn_ready = sem("xhat_ready"), sem("xT_done"), sem("xn_ready")
        qk_done, v_done, qk_ready, vt_ready = sem("qk_done"), sem("v_done"), sem("qk_ready"), sem("vt_ready")
        gram_done, logit_ready, e_ready, w_ready = sem("gram_done"), sem("logit_ready"), sem("e_ready"), sem("w_ready")
        wT_done, wT_ready, o_done, o_ready = sem("wT_done"), sem("wT_ready"), sem("o_done"), sem("o_ready")
        stored = sem("stored")
        mark = sb("mark", [P, 1])
        block = ctx.enter_context(nc.Block())
        ident, bmask = cst["ident"], cst["blockmask"]

        @block.sync
        def _(sp):
            sp.dma_start(w[:, :, :].rearrange("p c n -> p (c n)"), wd["w1"]).then_inc(loaded, 16)
            sp.dma_start(bqk[:, :], wd["bqk"]).then_inc(loaded, 16)
            sp.dma_start(bv[:, :], wd["bv"]).then_inc(loaded, 16)
            with sp.Fori(0, B) as b:
                sp.wait_ge(o_ready, 2 * b + 2)
                for c, k in KC:
                    dst = scratch[bass.ds(b, 1), c * P:c * P + k, :].rearrange("a c n -> (a c) n")
                    sp.dma_start(dst, osb[0:k, c, :]).then_inc(stored, 16)
            sp.wait_ge(stored, 32 * B + 32)
            sp.wait_ge(loaded, 48)

        @block.tensor
        def _(pe):
            mm, tr = nc.tensor.matmul, nc.tensor.transpose

            def input_t(b):
                pe.wait_ge(xhat_ready, b + 1)
                for t in range(T):
                    for c, k in KC:
                        last = tr(ps[0:k, 7, c * S + t * P:c * S + (t + 1) * P], xh[:, t, c * P:c * P + k], ident[:, :])
                last.then_inc(xT_done, 1)

            def project(b):
                pe.wait_ge(xn_ready, 2 * b + 2)
                for t in range(T):
                    for c, k in KC:
                        last = mm(ps[:, t, 0:2 * D], xn[0:k, c, t * P:(t + 1) * P], w[0:k, c, 0:2 * D],
                                  start=(c == 0), stop=(c == 1))
                last.then_inc(qk_done, 1)
                for o, n in KC:
                    for c, k in KC:
                        last = mm(ps[0:n, 2 + o, 0:S], w[0:k, c, 2 * D + o * P:2 * D + o * P + n], xn[0:k, c, :],
                                  start=(c == 0), stop=(c == 1))
                last.then_inc(v_done, 1)

            def body(b, last_one):
                pe.wait_ge(qk_ready, b + 1)
                for c, k in KC:
                    for t in range(T):
                        last = mm(ps[0:k, 4 + c, 0:k], qk[:, t, c * P:c * P + k], qk[:, t, D + c * P:D + c * P + k],
                                  start=(t == 0), stop=(t == 1))
                last.then_inc(gram_done, 1)
                if not last_one:
                    input_t(b + 1)
                pe.wait_ge(vt_ready, 2 * b + 2)
                if not last_one:
                    project(b + 1)
                pe.wait_ge(w_ready, b + 1)
                for c, k in KC:
                    last = tr(ps[0:k, 6, c * P:c * P + k], ex[0:k, c, 0:k], ident[0:k, 0:k])
                last.then_inc(wT_done, 1)
                pe.wait_ge(wT_ready, 2 * b + 2)
                for c, k in KC:
                    last = mm(ps[0:k, 6, c * S:(c + 1) * S], wt[0:k, c, 0:k], vt[0:k, c, :], start=True, stop=True)
                last.then_inc(o_done, 1)

            pe.wait_ge(loaded, 48)
            input_t(0)
            project(0)
            with pe.Fori(0, B - 1) as b:
                body(b, False)
            body(B - 1, True)

        @block.gpsimd
        def _(pool):
            nc.gpsimd.memset(mark[:, :], 0.0).then_inc(stored, 32)

        @block.scalar
        def _(act):
            go = nc.scalar.activation

            def input_copied(b):
                act.wait_ge(xT_done, b + 1)
                for c, k in KC:
                    go(xn[0:k, c, :], ps[0:k, 7, c * S:(c + 1) * S], ACT.Copy).then_inc(xn_ready, 1)

            def v_copied(b):
                act.wait_ge(v_done, b + 1)
                for c, k in KC:
                    go(vt[0:k, c, :], ps[0:k, 2 + c, 0:S], ACT.Identity, bias=bv[0:k, c:c + 1]).then_inc(vt_ready, 1)

            def body(b, last_one):
                if not last_one:
                    input_copied(b + 1)
                act.wait_ge(logit_ready, b + 1)
                for c, k in KC:
                    go(ex[0:k, c, 0:k], gm[0:k, c, 0:k], ACT.Exp, bias=mx[0:k, c:c + 1],
                       accum_out=sm[0:k, c:c + 1]).then_inc(e_ready, 1)
                act.wait_ge(wT_done, b + 1)
                for c, k in KC:
                    go(wt[0:k, c, 0:k], ps[0:k, 6, c * P:c * P + k], ACT.Copy).then_inc(wT_ready, 1)
                act.wait_ge(o_done, b + 1)
                act.wait_ge(stored, 32 * (b + 1))
                for c, k in KC:
                    go(osb[0:k, c, :], ps[0:k, 6, c * S:(c + 1) * S], ACT.Copy).then_inc(o_ready, 1)
                if not last_one:
                    v_copied(b + 1)

            act.wait_ge(loaded, 48)
            input_copied(0)
            v_copied(0)
            with act.Fori(0, B - 1) as b:
                body(b, False)
            body(B - 1, True)

        @block.vector
        def _(dve):
            v = nc.vector

            def input_kept(b):
                v.tensor_copy(xh[:, :, :], x[:, bass.ds(b * T, T), :]).then_inc(xhat_ready, 1)

            def qk_kept(b):
                dve.wait_ge(qk_done, b + 1)
                for t in range(T):
                    last = v.tensor_tensor(qk[:, t, :], ps[:, t, 0:2 * D], bqk[:, :], ALU.add)
                last.then_inc(qk_ready, 1)

            def body(b, last_one):
                link = chain(dve, dch, b, 3)
                if not last_one:
                    dve.wait_ge(xT_done, b + 1)
                    input_kept(b + 1)
                dve.wait_ge(gram_done, b + 1)
                for c, k in KC:
                    last = v.scalar_tensor_tensor(out=gm[0:k, c, 0:k], in0=ps[0:k, 4 + c, 0:k], scalar=1.0 / 16,
                                                  in1=bmask[0:k, 0:k], op0=ALU.mult, op1=ALU.add)
                link(last)
                for c, k in KC:
                    last = v.tensor_reduce(mx[0:k, c:c + 1], gm[0:k, c, 0:k], AX.X, ALU.max)
                link(last)
                for c, k in KC:
                    last = v.tensor_scalar(mx[0:k, c:c + 1], mx[0:k, c:c + 1], -1.0, None, ALU.mult)
                last.then_inc(logit_ready, 1)
                dve.wait_ge(e_ready, 2 * b + 2)
                for c, k in KC:
                    last = v.reciprocal(sm[0:k, c:c + 1], sm[0:k, c:c + 1])
                link(last)
                for c, k in KC:
                    last = v.tensor_scalar(ex[0:k, c, 0:k], ex[0:k, c, 0:k], sm[0:k, c:c + 1], None, ALU.mult)
                last.then_inc(w_ready, 1)
                if not last_one:
                    qk_kept(b + 1)
                link.finished()

            dve.wait_ge(loaded, 48)
            input_kept(0)
            qk_kept(0)
            with dve.Fori(0, B - 1) as b:
                body(b, False)
            body(B - 1, True)


def channel_projection_stage(nc, x, wd, cst, scratch):
    with ExitStack() as ctx:
        def sb(n, shape, dt=F32):
            return ctx.enter_context(nc.sbuf_tensor(f"cp_{n}", shape, dt))

        sem = ctx.enter_context(semaphores(nc, "cp"))

        ps = ctx.enter_context(nc.psum_tensor("cp_ps", [P, 8, 512], F32))
        a2 = sb("a2", [P, B * T, D])
        w, bo = sb("w", [P, 2, D]), sb("bo", [P, D])
        xh, xn, r = sb("xh", [P, T, D]), sb("xn", [P, 2, S]), sb("r", [P, T, D])
        loaded, dch = sem("loaded"), sem("vector_chain")
        xhat_ready, xT_done, xn_ready = sem("xhat_ready"), sem("xT_done"), sem("xn_ready")
        op_done, x_ready = sem("op_done"), sem("x_ready")
        block = ctx.enter_context(nc.Block())
        ident = cst["ident"]

        @block.sync
        def _(sp):
            sp.dma_start(w[:, :, :].rearrange("p c n -> p (c n)"), wd["w2"]).then_inc(loaded, 16)
            sp.dma_start(bo[:, :], wd["b2"]).then_inc(loaded, 16)
            flat = scratch.rearrange("b c n -> b (c n)").rearrange("b (t p d) -> p (b t) d", t=T, p=P)
            sp.dma_start(a2[:, :, :], flat).then_inc(loaded, 16)
            sp.wait_ge(loaded, 48)

        @block.tensor
        def _(pe):
            mm, tr = nc.tensor.matmul, nc.tensor.transpose

            def input_t(b):
                pe.wait_ge(xhat_ready, b + 1)
                for t in range(T):
                    for c, k in KC:
                        last = tr(ps[0:k, 7, c * S + t * P:c * S + (t + 1) * P], xh[:, t, c * P:c * P + k], ident[:, :])
                last.then_inc(xT_done, 1)

            def body(b, last_one):
                pe.wait_ge(xn_ready, 2 * b + 2)
                if not last_one:
                    input_t(b + 1)
                pe.wait_ge(x_ready, b + 1)
                for t in range(T):
                    for c, k in KC:
                        last = mm(ps[:, 1, t * D:(t + 1) * D], xn[0:k, c, t * P:(t + 1) * P], w[0:k, c, :],
                                  start=(c == 0), stop=(c == 1))
                last.then_inc(op_done, 1)

            pe.wait_ge(loaded, 48)
            input_t(0)
            with pe.Fori(0, B - 1) as b:
                body(b, False)
            body(B - 1, True)

        @block.scalar
        def _(act):
            def input_copied(b):
                act.wait_ge(xT_done, b + 1)
                for c, k in KC:
                    nc.scalar.activation(xn[0:k, c, :], ps[0:k, 7, c * S:(c + 1) * S], ACT.Copy).then_inc(xn_ready, 1)

            input_copied(0)
            with act.Fori(1, B) as b:
                act.wait_ge(op_done, b)
                input_copied(b)

        @block.vector
        def _(dve):
            v = nc.vector

            def input_kept(b):
                v.tensor_copy(xh[:, :, :], a2[:, bass.ds(b * T, T), :]).then_inc(xhat_ready, 1)

            def body(b, last_one):
                link = chain(dve, dch, b, 1)
                if not last_one:
                    dve.wait_ge(xT_done, b + 1)
                    input_kept(b + 1)
                dve.wait_ge(op_done, b + 1)
                for t in range(T):
                    last = v.tensor_tensor(r[:, t, :], ps[:, 1, t * D:(t + 1) * D], bo[:, :], ALU.add)
                link(last)
                xt = x[:, bass.ds(b * T, T), :]
                v.tensor_tensor(xt, xt, r[:, :, :], ALU.add).then_inc(x_ready, 1)
                dve.wait_ge(x_ready, b + 2)
                link.finished()

            dve.wait_ge(loaded, 48)
            v.tensor_copy(xh[:, :, :], a2[:, 0:T, :]).then_inc(xhat_ready, 1)
            v.memset(r[:, 0, 0:1], 0.0).then_inc(x_ready, 1)
            dve.wait_ge(x_ready, 1)
            with dve.Fori(0, B - 1) as b:
                body(b, False)
            body(B - 1, True)


def global_norm_stage(nc, name, x, h, wd, cst):
    N = B * S * D
    with ExitStack() as ctx:
        def sb(n, shape, dt=F32):
            return ctx.enter_context(nc.sbuf_tensor(f"{name}_{n}", shape, dt))

        sem = ctx.enter_context(semaphores(nc, name))

        ps = ctx.enter_context(nc.psum_tensor(f"{name}_ps", [P, 2, 512], F32))
        wb = sb("wb", [P, 2, D])
        ones = sb("ones", [P, P])
        part, stat = sb("part", [P, 2]), sb("stat", [P, 2])
        tsum = sb("tsum", [P, B * T])
        sq = sb("sq", [P, B * T * D])
        rt = sb("rt", [P, 6, T])
        loaded, dch, pch = sem("loaded"), sem("vector_chain"), sem("pool_chain")
        ones_ready, sum_ready, sum_all, centred = sem("ones_ready"), sem("sum_ready"), sem("sum_all"), sem("centred")
        sq_ready, sq_all, var_ready, root_ready = sem("sq_ready"), sem("sq_all"), sem("var_ready"), sem("root_ready")
        block = ctx.enter_context(nc.Block())
        flat = x[:, :, :].rearrange("p a d -> p (a d)")

        @block.sync
        def _(sp):
            sp.dma_start(wb[:, :, :].rearrange("p a d -> p (a d)"), wd).then_inc(loaded, 16)
            sp.wait_ge(loaded, 16)

        @block.tensor
        def _(pe):
            pe.wait_ge(ones_ready, 1)
            pe.wait_ge(sum_ready, 1)
            nc.tensor.matmul(ps[:, 0, 0:1], ones[:, :], part[:, 0:1], start=True, stop=True).then_inc(sum_all, 1)
            pe.wait_ge(sq_ready, 1)
            nc.tensor.matmul(ps[:, 1, 0:1], ones[:, :], part[:, 1:2], start=True, stop=True).then_inc(sq_all, 1)

        @block.scalar
        def _(act):
            act.wait_ge(centred, 1)
            nc.scalar.activation(sq[:, :], flat, ACT.Square, accum_out=part[:, 1:2]).then_inc(sq_ready, 1)

        @block.gpsimd
        def _(pool):
            nc.gpsimd.memset(ones[:, :], 1.0).then_inc(ones_ready, 1)
            half3, eps = cst["newton"][:, 0, :], cst["newton"][:, 1, :]
            link = chain(pool, pch, 0, root_steps(False))
            root(nc, pool, link, rt, half3, eps, var_ready, root_ready, 1, False)
            link.finished()

        @block.vector
        def _(dve):
            v = nc.vector
            link = chain(dve, dch, 0, 6 + (1 if h is not None else 0))
            link(v.tensor_reduce(tsum[:, :], x[:, :, :], AX.X, ALU.add))
            v.tensor_reduce(part[:, 0:1], tsum[:, :], AX.X, ALU.add).then_inc(sum_ready, 1)
            dve.wait_ge(sum_all, 1)
            link(v.tensor_scalar(stat[:, 0:1], ps[:, 0, 0:1], 1.0 / N, None, ALU.mult))
            v.tensor_scalar(flat, flat, stat[:, 0:1], None, ALU.subtract).then_inc(centred, 1)
            dve.wait_ge(centred, 1)
            dve.wait_ge(sq_all, 1)
            for t in range(T):
                last = v.tensor_scalar(rt[:, 0, t:t + 1], ps[:, 1, 0:1], 1.0 / (N - 1), 1e-12, ALU.mult, ALU.add)
            link(last)
            bits = rt[:, 1, :].bitcast(I32)
            v.tensor_scalar(rt[:, 4, :], rt[:, 0, :], -0.5, None, ALU.mult)
            v.tensor_scalar(bits, rt[:, 0, :].bitcast(I32), -0.5, RSQRT_SEED, ALU.mult, ALU.add).then_inc(var_ready, 1)
            dve.wait_ge(root_ready, 1)
            link(v.tensor_scalar(flat, flat, rt[:, 3, 0:1], None, ALU.mult))
            dve.wait_ge(loaded, 16)
            every = lambda n: wb[:, n:n + 1, :].to_broadcast([P, B * T, D])
            link(v.tensor_tensor(x[:, :, :], x[:, :, :], every(0), ALU.mult))
            link(v.tensor_tensor(x[:, :, :], x[:, :, :], every(1), ALU.add))
            if h is not None:
                link(v.tensor_tensor(h[:, :, :], h[:, :, :], x[:, :, :], ALU.add))
            link.finished()


def gate_stage(nc, x, wd, cst, vals, picks):
    E = MOE_E
    with ExitStack() as ctx:
        def sb(n, shape, dt=F32):
            return ctx.enter_context(nc.sbuf_tensor(f"gate_{n}", shape, dt))

        sem = ctx.enter_context(semaphores(nc, "gate"))

        ps = ctx.enter_context(nc.psum_tensor("gate_ps", [P, 8, 512], F32))
        rw, rb, iota = sb("rw", [P, 2, E]), sb("rb", [P, E]), sb("iota", [P, E])
        ones = sb("ones", [P, P])
        xh, xn = sb("xh", [P, T, D]), sb("xn", [P, 2, S])
        sc, z = sb("sc", [P, T, E]), sb("z", [P, B, E])
        m, g, eq, cand = sb("m", [P, B]), sb("g", [P, B, E]), sb("eq", [P, B, E]), sb("cand", [P, B, E])
        pf = sb("pf", [P, TOP_K, B])
        loaded, dch = sem("loaded"), sem("vector_chain")
        ones_ready, xhat_ready, xT_done, xn_ready = sem("ones_ready"), sem("xhat_ready"), sem("xT_done"), sem("xn_ready")
        sc_done, sc_ready, mean_done, z_ready = sem("sc_done"), sem("sc_ready"), sem("mean_done"), sem("z_ready")
        logits_ready, exp_ready = sem("logits_ready"), sem("exp_ready")
        block = ctx.enter_context(nc.Block())
        ident = cst["ident"]

        @block.sync
        def _(sp):
            sp.dma_start(rw[:, :, :].rearrange("p c e -> p (c e)"), wd["rw"]).then_inc(loaded, 16)
            sp.dma_start(rb[:, :], wd["rb"]).then_inc(loaded, 16)
            sp.dma_start(iota[:, :], wd["iota"]).then_inc(loaded, 16)
            sp.wait_ge(loaded, 48)

        @block.gpsimd
        def _(pool):
            nc.gpsimd.memset(ones[:, :], 1.0).then_inc(ones_ready, 1)

        @block.tensor
        def _(pe):
            mm, tr = nc.tensor.matmul, nc.tensor.transpose

            def input_t(b):
                pe.wait_ge(xhat_ready, b + 1)
                for t in range(T):
                    for c, k in KC:
                        last = tr(ps[0:k, 7, c * S + t * P:c * S + (t + 1) * P], xh[:, t, c * P:c * P + k], ident[:, :])
                last.then_inc(xT_done, 1)

            def score(b):
                for t in range(T):
                    for c, k in KC:
                        last = mm(ps[:, 0, t * E:(t + 1) * E], xn[0:k, c, t * P:(t + 1) * P], rw[0:k, c, :],
                                  start=(c == 0), stop=(c == 1))
                last.then_inc(sc_done, 1)

            def total(b):
                pe.wait_ge(sc_ready, b + 1)
                for t in range(T):
                    last = mm(ps[:, 1, 0:E], ones[:, :], sc[:, t, :], start=(t == 0), stop=(t == 1))
                last.then_inc(mean_done, 1)

            pe.wait_ge(loaded, 48)
            pe.wait_ge(ones_ready, 1)
            input_t(0)
            with pe.Fori(0, B - 1) as b:
                pe.wait_ge(xn_ready, 2 * b + 2)
                score(b)
                input_t(b + 1)
                total(b)
            pe.wait_ge(xn_ready, 2 * B)
            score(B - 1)
            total(B - 1)

        @block.scalar
        def _(act):
            def input_copied(b):
                act.wait_ge(xT_done, b + 1)
                for c, k in KC:
                    nc.scalar.activation(xn[0:k, c, :], ps[0:k, 7, c * S:(c + 1) * S], ACT.Copy).then_inc(xn_ready, 1)

            with act.Fori(0, B) as b:
                input_copied(b)
            act.wait_ge(logits_ready, 1)
            nc.scalar.activation(g[:, :, :].rearrange("p b e -> p (b e)"), z[:, :, :].rearrange("p b e -> p (b e)"),
                                 ACT.Exp).then_inc(exp_ready, 1)

        @block.vector
        def _(dve):
            v = nc.vector
            dve.wait_ge(loaded, 48)

            def body(b, last_one):
                if not last_one:
                    dve.wait_ge(xT_done, b + 1)
                    v.tensor_copy(xh[:, :, :], x[:, bass.ds((b + 1) * T, T), :]).then_inc(xhat_ready, 1)
                dve.wait_ge(sc_done, b + 1)
                v.tensor_copy(sc[:, :, :].rearrange("p t e -> p (t e)"), ps[:, 0, 0:T * E]).then_inc(sc_ready, 1)
                dve.wait_ge(mean_done, b + 1)
                v.scalar_tensor_tensor(out=z[:, bass.ds(b, 1), :].rearrange("p a e -> p (a e)"), in0=ps[:, 1, 0:E],
                                       scalar=1.0 / S, in1=rb[:, :], op0=ALU.mult, op1=ALU.add).then_inc(z_ready, 1)
                dve.wait_ge(z_ready, b + 1)

            v.tensor_copy(xh[:, :, :], x[:, 0:T, :]).then_inc(xhat_ready, 1)
            with dve.Fori(0, B - 1) as b:
                body(b, False)
            body(B - 1, True)
            link = chain(dve, dch, 0, 14)
            over = lambda a: a.unsqueeze(2).to_broadcast([P, B, E])
            io = iota[:, :].unsqueeze(1).to_broadcast([P, B, E])
            link(v.tensor_reduce(m[:, :], z[:, :, :], AX.X, ALU.max))
            v.tensor_tensor(z[:, :, :], z[:, :, :], over(m[:, :]), ALU.subtract).then_inc(logits_ready, 1)
            dve.wait_ge(exp_ready, 1)
            link(v.tensor_reduce(m[:, :], g[:, :, :], AX.X, ALU.add))
            link(v.reciprocal(m[:, :], m[:, :]))
            link(v.tensor_tensor(g[:, :, :], g[:, :, :], over(m[:, :]), ALU.mult))
            for k in range(TOP_K):
                link(v.tensor_reduce(vals[:, k, :], g[:, :, :], AX.X, ALU.max))
                link(v.tensor_tensor(eq[:, :, :], g[:, :, :], over(vals[:, k, :]), ALU.is_ge))
                link(v.scalar_tensor_tensor(out=cand[:, :, :], in0=eq[:, :, :], scalar=-float(E), in1=io,
                                            op0=ALU.mult, op1=ALU.add))
                link(v.tensor_reduce(pf[:, k, :], cand[:, :, :], AX.X, ALU.min))
                if k == 0:
                    link(v.tensor_tensor(eq[:, :, :], cand[:, :, :], over(pf[:, k, :]), ALU.is_equal))
                    link(v.scalar_tensor_tensor(out=g[:, :, :], in0=eq[:, :, :], scalar=-2.0, in1=g[:, :, :],
                                                op0=ALU.mult, op1=ALU.add))
            v.tensor_scalar(picks[:, :, :], pf[:, :, :].rearrange("p k b -> p b k"), float(E), None, ALU.add)
            link.finished()


def expert_stage(nc, name, x, dst, n, func, wd, cst, moe):
    with ExitStack() as ctx:
        def sb(nm, shape, dt=F32):
            return ctx.enter_context(nc.sbuf_tensor(f"{name}_{nm}", shape, dt))

        sem = ctx.enter_context(semaphores(nc, name))

        ps = ctx.enter_context(nc.psum_tensor(f"{name}_ps", [P, 8, 512], F32))
        sets = 2 if moe else 1
        w1, w2 = sb("w1", [P, sets * n, 2 * F]), sb("w2", [P, sets * n, FC * D])
        b1, b2 = sb("b1", [P, sets * n, FC]), sb("b2", [P, sets * n, D])
        xh, xn = sb("xh", [P, T, D]), sb("xn", [P, 2, S])
        hid = sb("hid", [P, 2, FC, S])
        yb = sb("yb", [P, T, D])
        wg, bg, iota = sb("wg", [P, 2, n]), sb("bg", [P, n]), sb("iota", [P, MOE_E])
        lg, eq, m, hot = sb("lg", [P, T, n]), sb("eq", [P, T, n]), sb("m", [P, T]), sb("hot", [P, T, n])
        w1_hi, w1_lo = sb("w1_hi", [P, sets * n, 2 * F], F32R), sb("w1_lo", [P, sets * n, 2 * F], F32R)
        x_hi, x_lo = sb("x_hi", [P, 2, S], F32R), sb("x_lo", [P, 2, S], F32R)
        w_rounded, w_split, x_split = sem("w_rounded"), sem("w_split"), sem("x_split")
        marks = sb("marks", [P, 3])
        loaded = [sem(f"loaded{j}") for j in range(sets * n)]
        gate_loaded, dch = sem("gate_loaded"), sem("vector_chain")
        xhat_ready, xT_done, xn_ready = sem("xhat_ready"), sem("xT_done"), sem("xn_ready")
        lg_done, h_done, y_done = sem("lg_done"), sem("h_done"), sem("y_done")
        h_read, y_used, acc_ready = sem("h_read"), sem("hidden_used"), sem("acc_ready")
        FREE = 2
        block = ctx.enter_context(nc.Block())
        ident = cst["ident"]
        LOADS = 64

        def wait_weights(eng, b, s, j):
            if moe:
                eng.wait_ge(loaded[s * n + j], (b - s + sets) * (LOADS // sets))
            else:
                eng.wait_ge(loaded[j], LOADS)

        def sequences(eng, body):
            with eng.Fori(0, B // sets - 1) as i:
                for s in range(sets):
                    body(i * sets + s, s, False)
            for s in range(sets):
                body(B - sets + s, s, s == sets - 1)

        @block.sync
        def _(sp):
            def fetch(j, e):
                for d, s in ((w1, wd["w1"]), (w2, wd["w2"]), (b1, wd["b1"]), (b2, wd["b2"])):
                    sp.dma_start(d[:, j, :], s[bass.ds(e, 1)].rearrange("a p n -> (a p) n")).then_inc(loaded[j], 16)

            if moe:
                def pick(b, s, j):
                    fetch(s * n + j, sp.value_load(moe[1][0:1, bass.ds(b, 1), j:j + 1].rearrange("p a k -> p (a k)"),
                                                   min_val=0, max_val=MOE_E - 1))

                for s in range(sets):
                    for j in range(n):
                        pick(s, s, j)
                with sp.Fori(1, B // sets) as i:
                    for s in range(sets):
                        for j in range(n):
                            sp.wait_ge(acc_ready, FREE + ((i - 1) * sets + s) * n + j + 1)
                            pick(i * sets + s, s, j)
            else:
                for d, s in ((wg[:, :, :].rearrange("p c e -> p (c e)"), wd["wg"]), (bg[:, :], wd["bg"]),
                             (iota[:, :], wd["iota"])):
                    sp.dma_start(d, s).then_inc(gate_loaded, 16)
                for j in range(n):
                    fetch(j, j)
                sp.wait_ge(gate_loaded, 48)
            for j in range(sets * n):
                sp.wait_ge(loaded[j], LOADS * (B // sets if moe else 1))

        @block.gpsimd
        def _(pool):
            for k, freed in enumerate((h_read, y_used, acc_ready)):
                nc.gpsimd.memset(marks[:, k:k + 1], 0.0).then_inc(freed, FREE)

        @block.tensor
        def _(pe):
            mm, tr = nc.tensor.matmul, nc.tensor.transpose

            def input_t(b):
                pe.wait_ge(xhat_ready, b + 1)
                for t in range(T):
                    for c, k in KC:
                        last = tr(ps[0:k, 7, c * S + t * P:c * S + (t + 1) * P], xh[:, t, c * P:c * P + k], ident[:, :])
                last.then_inc(xT_done, 1)

            def logits(b):
                pe.wait_ge(xn_ready, 4 * b + 4)
                for t in range(T):
                    for c, k in KC:
                        last = mm(ps[:, 6, t * n:(t + 1) * n], xn[0:k, c, t * P:(t + 1) * P], wg[0:k, c, :],
                                  start=(c == 0), stop=(c == 1))
                last.then_inc(lg_done, 1)

            def up(b, s, j):
                pe.wait_ge(w_split, b * n + j + 1 if moe else j + 1)
                if j == 0:
                    pe.wait_ge(xn_ready, 4 * b + 4)
                    pe.wait_ge(x_split, b + 1)
                hi, lo = (w_[:, (s * n if moe else 0) + j, :].rearrange("p (c f) -> p c f", c=2)
                          for w_ in (w1_hi, w1_lo))
                for q in range(FC):
                    pe.wait_ge(h_read, (b * n + j) * FC + q + 1)
                    for c, k in KC:
                        for n_pass, (w, xp) in enumerate(((hi, x_hi), (hi, x_lo), (lo, x_hi))):
                            last = mm(ps[:, q % 2, 0:S], w[0:k, c, q * P:(q + 1) * P], xp[0:k, c, :],
                                      start=(c == 0 and n_pass == 0), stop=(c == 1 and n_pass == 2))
                    last.then_inc(h_done, 1)

            def down(b, s, j):
                wait_weights(pe, b, s, j)
                pe.wait_ge(acc_ready, b * n + j + 1)
                w = w2[:, (s * n if moe else 0) + j, :].rearrange("p (q d) -> p q d", q=FC)
                for t in range(T):
                    for q in range(FC):
                        if t == 0:
                            pe.wait_ge(h_read, FREE + (b * n + j) * FC + q + 1)
                        last = mm(ps[:, 2 + 2 * (j % 2) + t, 0:D], hid[:, j % 2, q, t * P:(t + 1) * P], w[:, q, :],
                                  start=(q == 0), stop=(q == FC - 1))
                last.then_inc(y_used, 1)

            def body(b, s, last):
                for j in range(n):
                    if j + 1 < n:
                        up(b, s, j + 1)
                        if j + 1 == n - 1 and not last:
                            input_t(b + 1)
                    elif not last:
                        if not moe:
                            logits(b + 1)
                        up(b + 1, (s + 1) % sets, 0)
                    down(b, s, j)

            if not moe:
                pe.wait_ge(gate_loaded, 48)
            input_t(0)
            if not moe:
                logits(0)
            up(0, 0, 0)
            sequences(pe, body)

        @block.scalar
        def _(act):
            go = nc.scalar.activation

            def input_copied(b):
                act.wait_ge(xT_done, b + 1)
                for c, k in KC:
                    go(xn[0:k, c, :], ps[0:k, 7, c * S:(c + 1) * S], ACT.Copy).then_inc(xn_ready, 1)
                    go(x_hi[0:k, c, :], ps[0:k, 7, c * S:(c + 1) * S], ACT.Copy).then_inc(xn_ready, 1)

            def hidden(b, s, j):
                wait_weights(act, b, s, j)
                act.wait_ge(y_used, b * n + j + 1)
                for q in range(FC):
                    act.wait_ge(h_done, (b * n + j) * FC + q + 1)
                    bias = b1[:, (s * n if moe else 0) + j, q:q + 1]
                    go(hid[:, j % 2, q, :], ps[:, q % 2, 0:S], func, bias=bias).then_inc(h_read, 1)

            def body(b, s, last):
                for j in range(n):
                    hidden(b, s, j)
                if not last:
                    input_copied(b + 1)

            input_copied(0)
            sequences(act, body)

        @block.vector
        def _(dve):
            v = nc.vector

            def input_kept(b):
                v.tensor_copy(xh[:, :, :], x[:, bass.ds(b * T, T), :]).then_inc(xhat_ready, 1)

            def input_split(b):
                dve.wait_ge(xn_ready, 4 * b + 4)
                for c, k in KC:
                    last = v.tensor_tensor(x_lo[0:k, c, :], xn[0:k, c, :], x_hi[0:k, c, :], ALU.subtract)
                last.then_inc(x_split, 1)

            def weights_split(b, s, j):
                wait_weights(dve, b, s, j)
                at = (s * n if moe else 0) + j
                v.tensor_copy(w1_hi[:, at, :], w1[:, at, :]).then_inc(w_rounded, 1)
                dve.wait_ge(w_rounded, b * n + j + 1 if moe else j + 1)
                v.tensor_tensor(w1_lo[:, at, :], w1[:, at, :], w1_hi[:, at, :], ALU.subtract).then_inc(w_split, 1)

            def gates(b, link):
                dve.wait_ge(lg_done, b + 1)
                over = lambda a: a.unsqueeze(2).to_broadcast([P, T, n])
                bgt = bg[:, :].unsqueeze(1).to_broadcast([P, T, n])
                io = iota[:, 0:n].unsqueeze(1).to_broadcast([P, T, n])
                link(v.tensor_tensor(lg[:, :, :], ps[:, 6, 0:T * n].rearrange("p (t e) -> p t e", t=T), bgt, ALU.add))
                link(v.tensor_reduce(m[:, :], lg[:, :, :], AX.X, ALU.max))
                link(v.tensor_tensor(eq[:, :, :], lg[:, :, :], over(m[:, :]), ALU.is_ge))
                link(v.scalar_tensor_tensor(out=lg[:, :, :], in0=eq[:, :, :], scalar=-8.0, in1=io, op0=ALU.mult,
                                            op1=ALU.add))
                link(v.tensor_reduce(m[:, :], lg[:, :, :], AX.X, ALU.min))
                v.tensor_tensor(hot[:, :, :], lg[:, :, :], over(m[:, :]), ALU.is_equal)

            def add(b, s, j, link):
                dve.wait_ge(y_used, FREE + b * n + j + 1)
                wait_weights(dve, b, s, j)
                for t in range(T):
                    last = v.tensor_tensor(yb[:, t, :], ps[:, 2 + 2 * (j % 2) + t, 0:D],
                                           b2[:, (s * n if moe else 0) + j, :], ALU.add)
                link(last)
                for t in range(T):
                    dt = dst[:, bass.ds(b * T + t, 1), :].rearrange("p a d -> p (a d)")
                    co = (moe[0][:, j, bass.ds(b, 1)] if moe else hot[:, t, j:j + 1])
                    last = v.scalar_tensor_tensor(out=dt, in0=yb[:, t, :], scalar=co, in1=dt, op0=ALU.mult,
                                                  op1=ALU.add)
                last.then_inc(acc_ready, 1)
                dve.wait_ge(acc_ready, FREE + b * n + j + 1)

            def body(b, s, last):
                link = chain(dve, dch, b, n + (0 if moe else 5))
                if not last:
                    dve.wait_ge(xT_done, b + 1)
                    input_kept(b + 1)
                if not moe:
                    gates(b, link)
                for j in range(n):
                    if moe and not last:
                        weights_split(b + 1, (s + 1) % sets, j)
                    if j == n - 2 and not last:
                        input_split(b + 1)
                    add(b, s, j, link)
                link.finished()

            if not moe:
                dve.wait_ge(gate_loaded, 48)
            input_kept(0)
            input_split(0)
            for j in range(n):
                weights_split(0, 0, j)
            sequences(dve, body)


def store_stage(nc, h, out):
    with nc.semaphore("out_stored") as stored, nc.Block() as block:
        @block.sync
        def _(sp):
            dst = out.rearrange("b s d -> (b s) d").rearrange("(n p) d -> p n d", p=P)
            sp.dma_start(dst, h[:, :, :]).then_inc(stored, 16)
            sp.wait_ge(stored, 16)


def lm_tower(nc, a, out):
    part = lambda prefix: {k[len(prefix):]: v for k, v in a.items() if k.startswith(prefix)}
    with ExitStack() as ctx:
        def sb(n, shape, dt=F32):
            return ctx.enter_context(nc.sbuf_tensor(n, shape, dt))

        h = sb("h_stream", [P, B * T, D])
        x = sb("x_stream", [P, B * T, D])
        vals, picks = sb("vals", [P, TOP_K, B]), sb("picks", [P, B, TOP_K], I32)
        cst = {"ident": sb("ident", [P, P]), "identr": sb("identr", [P, P], F32R), "maskqk": sb("maskqk", [P, 2]),
               "blockmask": sb("blockmask", [P, P]), "newton": sb("newton", [P, 2, T])}
        scratch = nc.dram_tensor("channel_attention", [B, D, S], F32, kind="Internal").ap()
        embedding_stage(nc, x, a, cst)
        attention_stage(nc, "tok", "tok", h, x, part("tok_"), cst)
        glue_stage(nc, "to_vit", h, x, False)
        attention_stage(nc, "vit", "vit", h, x, part("vit_"), cst)
        glue_stage(nc, "to_ffn", h, x, True)
        f = part("ffn_")
        channel_attention_stage(nc, x, f, cst, scratch)
        channel_projection_stage(nc, x, f, cst, scratch)
        global_norm_stage(nc, "gn1", x, None, f["ln1"], cst)
        gate_stage(nc, x, f, cst, vals, picks)
        expert_stage(nc, "moe", x, x, TOP_K, ACT.Gelu_apprx_tanh, part("moe_"), cst, (vals, picks))
        global_norm_stage(nc, "gn2", x, h, f["ln2"], cst)
        attention_stage(nc, "l1", "l1", h, x, part("l1_"), cst)
        glue_stage(nc, "to_experts", h, x, False)
        expert_stage(nc, "ex", x, h, L1_E, ACT.Gelu, part("ex_"), cst, None)
        store_stage(nc, h, out)


def positions():
    f = np.float32
    pos = np.arange(S, dtype=f)[:, None]
    i = np.arange(D, dtype=f)[None, :]
    ang = (pos / np.power(f(10000.0), (f(2.0) * i / f(D)).astype(f)).astype(f)).astype(f)
    tab = np.where(np.arange(D)[None, :] % 2 == 0, np.cos(ang), np.sin(ang)).astype(f)
    return np.ascontiguousarray(tab.reshape(T, P, D).transpose(1, 0, 2).reshape(P, T * D))


def rows(w):
    lead, n = w.shape[:-2], w.shape[-1]
    out = np.zeros(lead + (P, 2, n), np.float32)
    out[..., :, 0, :] = w[..., 0:P, :]
    out[..., 0:D2, 1, :] = w[..., P:D, :]
    return out.reshape(lead + (P, 2 * n))


def hidden_rows(w):
    lead, n = w.shape[:-2], w.shape[-1]
    w = w.reshape(lead + (FC, P, n))
    return np.ascontiguousarray(np.moveaxis(w, -3, -2)).reshape(lead + (P, FC * n))


def spread(v):
    return np.ascontiguousarray(np.broadcast_to(v[..., None, :], v.shape[:-1] + (P, v.shape[-1])))


def stacked(w):
    out = np.zeros((D, PAIRS, 2, SLOT), np.float32)
    cols = w.reshape(D, PAIRS, 2, DH)
    for s in range(3):
        out[:, :, :, s * DH:(s + 1) * DH] = cols
    return rows(out.reshape(D, PAIRS * P))


def stacked_heads(w):
    out = np.zeros((w.shape[0], P, PAIRS, 2, SLOT), np.float32)
    for p in range(PAIRS):
        for a in range(2):
            hd = 2 * p + a
            r = SLOT * ((p // 2) % 2) + DH * (hd % 4)
            for s in range(3):
                out[:, r:r + DH, p, a, s * DH:(s + 1) * DH] = w[:, hd].transpose(0, 2, 1)
    return out.reshape(w.shape[0], P, PAIRS * P)


LO_ROWS = ((2,), (1,))


def stacked_bias(bq, bk):
    L = bq.shape[0]
    full = np.zeros((L, 2, SLOT, 2, PAIRS), np.float32)
    low = np.zeros_like(full)
    for i, bias in enumerate((bq, bk)):
        bb = bias.reshape(L, PAIRS, 2, DH).transpose(0, 2, 3, 1)
        for s in range(3):
            full[:, :, s * DH:(s + 1) * DH, i, :] = bb
            if s in LO_ROWS[i]:
                low[:, :, s * DH:(s + 1) * DH, i, :] = bb
    full[:, :, MROW:MROW + 2, 1, :] = 1.0
    return full.reshape(L, P, 2 * PAIRS), low.reshape(L, P, 2 * PAIRS)


def feature_pairs(g, b):
    gb = np.stack([g, b], -1)
    return rows(gb)


def block_diagonal(w):
    out = np.zeros((w.shape[0], D, D), np.float32)
    for hd in range(H):
        out[:, hd * DH:(hd + 1) * DH, hd * DH:(hd + 1) * DH] = w[:, hd].transpose(0, 2, 1)
    return out


def pack(i):
    f = {k: np.asarray(v) for k, v in i.items()}
    one = lambda v: v[None]
    n = {}
    n["tokens"] = np.ascontiguousarray(f["x"].reshape(B * T, P).T)
    n["pos"] = positions()
    n["ident"] = np.eye(P, dtype=np.float32)
    mask = np.zeros((2, SLOT, 2), np.float32)
    for j in range(2):
        for s in LO_ROWS[j]:
            mask[:, s * DH:(s + 1) * DH, j] = 1.0
    n["maskqk"] = mask.reshape(P, 2)
    r = np.arange(P) // DH
    n["blockmask"] = np.where(r[:, None] == r[None, :], 0.0, -1e30).astype(np.float32)
    n["emb"] = f["L0_tok_emb"]
    t = "L0_tok_"
    n["tok_wq"], n["tok_wk"], n["tok_wv"] = (one(stacked(f[t + "wq"])), one(stacked(f[t + "wk"])),
                                             one(rows(f[t + "wv"])))
    n["tok_bqk"], n["tok_bqk_lo"] = stacked_bias(one(f[t + "bq"]), one(f[t + "bk"]))
    n["tok_bv"], n["tok_wo"], n["tok_bo"] = one(spread(f[t + "bv"])), one(rows(f[t + "wo"])), one(spread(f[t + "bo"]))
    n["tok_w1"], n["tok_w2"] = one(rows(f[t + "w1"])), one(hidden_rows(f[t + "w2"]))
    n["tok_b1"], n["tok_b2"] = one(f[t + "b1"].reshape(FC, P).T), one(spread(f[t + "b2"]))
    n["tok_gb"] = one(spread(np.stack([f[t + "gamma1"], f[t + "beta1"], f[t + "gamma2"], f[t + "beta2"]])
                             .transpose(0, 1)).transpose(1, 0, 2).reshape(P, 4 * D))
    t = "L0_attn_"
    n["vit_wq"], n["vit_wk"] = stacked_heads(f[t + "qw"]), stacked_heads(f[t + "kw"])
    n["vit_wv"] = rows(block_diagonal(f[t + "vw"]))
    L = VIT_LAYERS
    n["vit_bqk"], n["vit_bqk_lo"] = stacked_bias(f[t + "qb"].reshape(L, D), f[t + "kb"].reshape(L, D))
    n["vit_bv"] = spread(f[t + "vb"].reshape(L, D))
    n["vit_ln1"] = feature_pairs(f[t + "ln1_g"], f[t + "ln1_b"])
    n["vit_ln2"] = feature_pairs(f[t + "ln2_g"], f[t + "ln2_b"])
    n["vit_w1"], n["vit_w2"] = rows(f[t + "w1"].transpose(0, 2, 1)), hidden_rows(f[t + "w2"].transpose(0, 2, 1))
    n["vit_b1"], n["vit_b2"] = f[t + "b1"].reshape(L, FC, P).transpose(0, 2, 1), spread(f[t + "b2"])
    t = "L1_attn_"
    w, z = f[t + "W_qkv"], np.zeros((1, D), np.float32)
    n["l1_wq"], n["l1_wk"], n["l1_wv"] = (one(stacked(w[:, 0:D])), one(stacked(w[:, D:2 * D])),
                                          one(rows(w[:, 2 * D:3 * D])))
    n["l1_bqk"], n["l1_bqk_lo"] = stacked_bias(z, z)
    n["l1_bv"] = spread(z)
    n["l1_wo"], n["l1_bo"] = one(rows(f[t + "W_proj"])), one(spread(f[t + "b_proj"]))
    t = "L0_ffn_"
    n["ffn_w1"] = rows(f[t + "W1_w"])
    n["ffn_bqk"] = spread(f[t + "W1_b"][0:2 * D])
    bv = np.zeros((P, 2), np.float32)
    bv[:, 0], bv[0:D2, 1] = f[t + "W1_b"][2 * D:2 * D + P], f[t + "W1_b"][2 * D + P:]
    n["ffn_bv"] = bv
    n["ffn_w2"], n["ffn_b2"] = rows(f[t + "W2_w"]), spread(f[t + "W2_b"])
    for ln in ("ln1", "ln2"):
        n["ffn_" + ln] = np.concatenate([spread(f[t + ln + "_w"]), spread(f[t + ln + "_b"])], 1)
    n["ffn_rw"], n["ffn_rb"] = rows(f[t + "r_w"]), spread(f[t + "r_b"])
    iota = spread(np.arange(MOE_E, dtype=np.float32))
    n["ffn_iota"] = n["ex_iota"] = iota
    n["moe_w1"], n["moe_w2"] = rows(f[t + "fc_w"]), hidden_rows(f[t + "proj_w"])
    n["moe_b1"], n["moe_b2"] = f[t + "fc_b"].reshape(MOE_E, FC, P).transpose(0, 2, 1), spread(f[t + "proj_b"])
    t = "L1_ffn_"
    n["ex_w1"], n["ex_w2"] = rows(f[t + "W1"]), hidden_rows(f[t + "W2"])
    n["ex_b1"], n["ex_b2"] = f[t + "b1"].reshape(L1_E, FC, P).transpose(0, 2, 1), spread(f[t + "b2"])
    n["ex_wg"], n["ex_bg"] = rows(f[t + "Wg"]), spread(f[t + "bg"])
    return {k: np.ascontiguousarray(v) for k, v in n.items()}


def kernel(**inputs):
    import concourse.bacc as bacc
    from concourse.bass_utils import run_bass_kernel_spmd

    nc = bacc.Bacc("TRN2", target_bir_lowering=False, num_devices=1)
    arrays, aps = {}, {}
    for name, value in pack(inputs).items():
        arrays[f"in_{name}_dram"] = value
        aps[name] = nc.dram_tensor(f"in_{name}_dram", value.shape, mybir.dt.from_np(value.dtype),
                                   kind="ExternalInput").ap()
    out = nc.dram_tensor("out_0_dram", (B, S, D), F32, kind="ExternalOutput").ap()
    lm_tower(nc, aps, out)
    return run_bass_kernel_spmd(nc, [arrays], core_ids=[0]).results[0]["out_0_dram"]
```
